# Optimizing a Trainium2 kernel written in Bass

```python
import numpy as np
import jax
import jax.numpy as jnp

def _softmax(x, axis=-1):
    return jax.nn.softmax(x, axis=axis)

def _gelu(x):
    return jax.nn.gelu(x, approximate=True)

def _silu(x):
    return jax.nn.silu(x)

def _sigmoid(x):
    return jax.nn.sigmoid(x)

def _layernorm(x, axis=-1, eps=1e-05):
    m = jnp.mean(x, axis=axis, keepdims=True)
    v = jnp.var(x, axis=axis, keepdims=True)
    return (x - m) / jnp.sqrt(v + eps)

def _scatter_add(tgt, idx, src, axis=0):
    return tgt.at[idx].add(src)

def _segment_sum(src, seg, n):
    return jax.ops.segment_sum(src, seg, n)
kernel_name = 'mk_cond_seq_d4_seqx_r4_8acaa7'

def setup_inputs(seed: int=0):
    np.random.seed(seed)
    _w = jnp.asarray

    def _rec_inputs():
        import jax
        import jax.numpy as jnp
        _rk = jax.random.key(seed)
        x = -0.000125 + 0.9999 * jax.random.normal(jax.random.fold_in(_rk, 1), (16, 256, 256), jnp.float32)
        _lenS = 256 - jax.random.randint(jax.random.fold_in(_rk, 7), (16,), 0, max(1, 256 // 4) + 1, jnp.int32)
        _lenS2 = 256 - jax.random.randint(jax.random.fold_in(_rk, 8), (16,), 0, max(1, 256 // 4) + 1, jnp.int32)
        itok_B_0_15 = jax.random.randint(jax.random.fold_in(_rk, 11), (16,), 0, 16, jnp.int32)
        itok_B_34_63 = jax.random.randint(jax.random.fold_in(_rk, 13), (16,), 34, 64, jnp.int32)
        fside_Bx16xSxS_0 = -1.47943e-05 + 1.00017 * jax.random.normal(jax.random.fold_in(_rk, 14), (16, 16, 256, 256), jnp.float32)
        itok_B_0_2 = jax.random.randint(jax.random.fold_in(_rk, 15), (16,), 0, 3, jnp.int32)
        condB_dt = jax.random.uniform(jax.random.fold_in(_rk, 16), (16,), jnp.float32, 0.0, 0.981965)
        _validS = jnp.arange(256)[None, :] < _lenS[:, None]
        _validS2 = jnp.arange(256)[None, :] < _lenS2[:, None]
        _causal = jnp.tril(jnp.ones((256, 256), dtype=bool))
        mask_Bx1xSxS_bk0 = jnp.logical_not(jnp.broadcast_to(_validS[:, None, None, :], (16, 1, 256, 256)))
        return (x, itok_B_0_15, itok_B_34_63, fside_Bx16xSxS_0, itok_B_0_2, condB_dt, mask_Bx1xSxS_bk0)
    x, itok_B_0_15, itok_B_34_63, fside_Bx16xSxS_0, itok_B_0_2, condB_dt, mask_Bx1xSxS_bk0 = _rec_inputs()

    def _L0_cond_setup():
        import jax, jax.numpy as jnp
        import numpy as np
        B, S, D = (32, 256, 256)
        A = 64
        E = 16
        LN_EPS = 1e-05
        key = jax.random.key(seed)
        ks = jax.random.split(key, 10)
        s = lambda fan_in: 1.0 / np.sqrt(fan_in)
        return {'hidden_states': jax.random.normal(ks[0], (B, S, D), dtype=jnp.float32), 'domain_id': jax.random.randint(ks[1], (B,), 0, E, dtype=jnp.int64), 'down_W': jax.random.uniform(ks[2], (A, D), jnp.float32, -s(D), s(D)), 'down_b': jax.random.uniform(ks[3], (A,), jnp.float32, -s(D), s(D)), 'up_W': jax.random.uniform(ks[4], (D, A), jnp.float32, -s(A), s(A)), 'up_b': jax.random.uniform(ks[5], (D,), jnp.float32, -s(A), s(A)), 'expert_W': jax.random.uniform(ks[6], (E, A, A), jnp.float32, -s(A), s(A)), 'expert_b': jax.random.uniform(ks[7], (E, A), jnp.float32, -s(A), s(A)), 'domain_emb': jax.random.normal(ks[8], (E, A), dtype=jnp.float32), 'ln_gamma': jnp.ones((D,), jnp.float32), 'ln_beta': jnp.zeros((D,), jnp.float32)}
    _L0_cond_all = _L0_cond_setup()
    _L0_cond_in = {k: v for k, v in _L0_cond_all.items() if k in ('down_W', 'down_b', 'up_W', 'up_b', 'expert_W', 'expert_b', 'domain_emb', 'ln_gamma', 'ln_beta')}
    del _L0_cond_all

    def _L1_cond_setup():
        import jax, jax.numpy as jnp
        import numpy as np
        import math
        D_MODEL = 256
        N_HEAD = 16
        HEAD_DIM = D_MODEL // N_HEAD
        D_FF = 1024
        NUM_STEPS = 100.0
        RESCALE = 4000.0
        EPS = 1e-05

        def _sin_emb(t):
            half = D_MODEL // 2
            x = t.astype(jnp.float32) / NUM_STEPS * RESCALE
            freqs = jnp.exp(jnp.arange(half, dtype=jnp.float32) * (-math.log(10000.0) / (half - 1)))
            e = x[:, None] * freqs[None, :]
            return jnp.concatenate([jnp.sin(e), jnp.cos(e)], axis=-1)

        def _ln(x):
            m = jnp.mean(x, axis=-1, keepdims=True)
            v = jnp.var(x, axis=-1, keepdims=True)
            return (x - m) / jnp.sqrt(v + EPS)

        def _gelu2(x):
            return x * jax.nn.sigmoid(1.702 * x)
        key = jax.random.key(seed)
        ks = jax.random.split(key, 24)
        B, S, D, F = (4, 128, D_MODEL, D_FF)
        std = 0.02
        inp = {'src': jax.random.normal(ks[0], (B, S, D), dtype=jnp.float32), 'src_mask': jax.random.randint(ks[1], (B, 1, S, S), 0, 2).astype(bool), 'timestep': jax.random.randint(ks[2], (B,), 0, 100, dtype=jnp.int32), 'attention_bias': jax.random.normal(ks[3], (B, N_HEAD, S, S), dtype=jnp.float32), 'W_ada': jax.random.normal(ks[4], (D, 2 * D), dtype=jnp.float32) * std, 'b_ada': jnp.zeros((2 * D,), dtype=jnp.float32), 'Wq': jax.random.normal(ks[5], (D, D), dtype=jnp.float32) * std, 'bq': jnp.zeros((D,), dtype=jnp.float32), 'Wk': jax.random.normal(ks[6], (D, D), dtype=jnp.float32) * std, 'bk': jnp.zeros((D,), dtype=jnp.float32), 'Wv': jax.random.normal(ks[7], (D, D), dtype=jnp.float32) * std, 'bv': jnp.zeros((D,), dtype=jnp.float32), 'Wo': jax.random.normal(ks[8], (D, D), dtype=jnp.float32) * std, 'bo': jnp.zeros((D,), dtype=jnp.float32), 'W1': jax.random.normal(ks[9], (D, F), dtype=jnp.float32) * std, 'b1': jnp.zeros((F,), dtype=jnp.float32), 'W2': jax.random.normal(ks[10], (F, D), dtype=jnp.float32) * std, 'b2': jnp.zeros((D,), dtype=jnp.float32), 'g2': jnp.ones((D,), dtype=jnp.float32), 'beta2': jnp.zeros((D,), dtype=jnp.float32)}
        return inp
    _L1_cond_all = _L1_cond_setup()
    _L1_cond_in = {k: v for k, v in _L1_cond_all.items() if k in ('W_ada', 'b_ada', 'Wq', 'bq', 'Wk', 'bk', 'Wv', 'bv', 'Wo', 'bo', 'W1', 'b1', 'W2', 'b2', 'g2', 'beta2')}
    del _L1_cond_all

    def _L2_cond_setup():
        import jax, jax.numpy as jnp
        import numpy as np
        H = 256
        EPS = 1e-05

        def _gelu(x):
            return jax.nn.gelu(x, approximate=False)
        key = jax.random.key(seed)
        ks = jax.random.split(key, 16)
        s = 1.0 / np.sqrt(H)
        inp = {'x': jax.random.normal(ks[0], (64, 256, H), dtype=jnp.float32), 'condition': jax.random.randint(ks[1], (64,), 0, 3), 'w1_nr': jax.random.normal(ks[2], (H, H), dtype=jnp.float32) * s, 'b1_nr': jnp.zeros((H,), dtype=jnp.float32), 'w2_nr': jax.random.normal(ks[3], (H, H), dtype=jnp.float32) * s, 'b2_nr': jnp.zeros((H,), dtype=jnp.float32), 'w1_tsr': jax.random.normal(ks[4], (H, H), dtype=jnp.float32) * s, 'b1_tsr': jnp.zeros((H,), dtype=jnp.float32), 'w2_tsr': jax.random.normal(ks[5], (H, H), dtype=jnp.float32) * s, 'b2_tsr': jnp.zeros((H,), dtype=jnp.float32), 'w1_sr': jax.random.normal(ks[6], (H, 2 * H), dtype=jnp.float32) * s, 'b1_sr': jnp.zeros((2 * H,), dtype=jnp.float32), 'w2_sr': jax.random.normal(ks[7], (2 * H, H), dtype=jnp.float32) * (1.0 / np.sqrt(2 * H)), 'b2_sr': jnp.zeros((H,), dtype=jnp.float32), 'w3_sr': jax.random.normal(ks[8], (H, H), dtype=jnp.float32) * s, 'b3_sr': jnp.zeros((H,), dtype=jnp.float32), 'gamma': jnp.ones((H,), dtype=jnp.float32), 'beta': jnp.zeros((H,), dtype=jnp.float32)}
        return inp
    _L2_cond_all = _L2_cond_setup()
    _L2_cond_in = {k: v for k, v in _L2_cond_all.items() if k in ('w1_nr', 'b1_nr', 'w2_nr', 'b2_nr', 'w1_tsr', 'b1_tsr', 'w2_tsr', 'b2_tsr', 'w1_sr', 'b1_sr', 'w2_sr', 'b2_sr', 'w3_sr', 'b3_sr', 'gamma', 'beta')}
    del _L2_cond_all

    def _L3_cond_setup():
        import jax, jax.numpy as jnp
        import numpy as np
        B, NX, NY = (16, 256, 256)

        def _grad(f, axis):
            fm = jnp.moveaxis(f, axis, -1)
            g = (jnp.roll(fm, -1, -1) - jnp.roll(fm, 1, -1)) * 0.5
            g0 = (-3.0 * fm[..., 0] + 4.0 * fm[..., 1] - fm[..., 2]) * 0.5
            gN = (3.0 * fm[..., -1] - 4.0 * fm[..., -2] + fm[..., -3]) * 0.5
            g = g.at[..., 0].set(g0).at[..., -1].set(gN)
            return jnp.moveaxis(g, -1, axis)

        def _grad2(f, axis):
            fm = jnp.moveaxis(f, axis, -1)
            g = jnp.roll(fm, -1, -1) - 2.0 * fm + jnp.roll(fm, 1, -1)
            g0 = 2.0 * fm[..., 0] - 5.0 * fm[..., 1] + 4.0 * fm[..., 2] - fm[..., 3]
            gN = 2.0 * fm[..., -1] - 5.0 * fm[..., -2] + 4.0 * fm[..., -3] - fm[..., -4]
            g = g.at[..., 0].set(g0).at[..., -1].set(gN)
            return jnp.moveaxis(g, -1, axis)
        key = jax.random.key(seed)
        k1, k2, k3, k4 = jax.random.split(key, 4)
        f = jax.random.uniform(k1, (B, NX, NY), dtype=jnp.float32)
        A_grid = jax.random.normal(k2, (2, NX, NY), dtype=jnp.float32)
        B_grid = jax.random.uniform(k3, (3, NX, NY), dtype=jnp.float32)
        dt = jax.random.uniform(k4, (B,), dtype=jnp.float32)
        return {'f': f, 'A_grid': A_grid, 'B_grid': B_grid, 'dt': dt}
    _L3_cond_all = _L3_cond_setup()
    _L3_cond_in = {k: v for k, v in _L3_cond_all.items() if k in ('A_grid', 'B_grid')}
    del _L3_cond_all
    return {'x': x, 'itok_B_0_15': itok_B_0_15, 'itok_B_34_63': itok_B_34_63, 'fside_Bx16xSxS_0': fside_Bx16xSxS_0, 'itok_B_0_2': itok_B_0_2, 'condB_dt': condB_dt, 'mask_Bx1xSxS_bk0': mask_Bx1xSxS_bk0, 'L0_cond_down_W': _L0_cond_in['down_W'], 'L0_cond_down_b': _L0_cond_in['down_b'], 'L0_cond_up_W': _L0_cond_in['up_W'], 'L0_cond_up_b': _L0_cond_in['up_b'], 'L0_cond_expert_W': _L0_cond_in['expert_W'], 'L0_cond_expert_b': _L0_cond_in['expert_b'], 'L0_cond_domain_emb': _L0_cond_in['domain_emb'], 'L0_cond_ln_gamma': _L0_cond_in['ln_gamma'], 'L0_cond_ln_beta': _L0_cond_in['ln_beta'], 'L1_cond_W_ada': _L1_cond_in['W_ada'], 'L1_cond_b_ada': _L1_cond_in['b_ada'], 'L1_cond_Wq': _L1_cond_in['Wq'], 'L1_cond_bq': _L1_cond_in['bq'], 'L1_cond_Wk': _L1_cond_in['Wk'], 'L1_cond_bk': _L1_cond_in['bk'], 'L1_cond_Wv': _L1_cond_in['Wv'], 'L1_cond_bv': _L1_cond_in['bv'], 'L1_cond_Wo': _L1_cond_in['Wo'], 'L1_cond_bo': _L1_cond_in['bo'], 'L1_cond_W1': _L1_cond_in['W1'], 'L1_cond_b1': _L1_cond_in['b1'], 'L1_cond_W2': _L1_cond_in['W2'], 'L1_cond_b2': _L1_cond_in['b2'], 'L1_cond_g2': _L1_cond_in['g2'], 'L1_cond_beta2': _L1_cond_in['beta2'], 'L2_cond_w1_nr': _L2_cond_in['w1_nr'], 'L2_cond_b1_nr': _L2_cond_in['b1_nr'], 'L2_cond_w2_nr': _L2_cond_in['w2_nr'], 'L2_cond_b2_nr': _L2_cond_in['b2_nr'], 'L2_cond_w1_tsr': _L2_cond_in['w1_tsr'], 'L2_cond_b1_tsr': _L2_cond_in['b1_tsr'], 'L2_cond_w2_tsr': _L2_cond_in['w2_tsr'], 'L2_cond_b2_tsr': _L2_cond_in['b2_tsr'], 'L2_cond_w1_sr': _L2_cond_in['w1_sr'], 'L2_cond_b1_sr': _L2_cond_in['b1_sr'], 'L2_cond_w2_sr': _L2_cond_in['w2_sr'], 'L2_cond_b2_sr': _L2_cond_in['b2_sr'], 'L2_cond_w3_sr': _L2_cond_in['w3_sr'], 'L2_cond_b3_sr': _L2_cond_in['b3_sr'], 'L2_cond_gamma': _L2_cond_in['gamma'], 'L2_cond_beta': _L2_cond_in['beta'], 'L3_cond_A_grid': _L3_cond_in['A_grid'], 'L3_cond_B_grid': _L3_cond_in['B_grid']}

def reference(x, itok_B_0_15, itok_B_34_63, fside_Bx16xSxS_0, itok_B_0_2, condB_dt, mask_Bx1xSxS_bk0, L0_cond_down_W, L0_cond_down_b, L0_cond_up_W, L0_cond_up_b, L0_cond_expert_W, L0_cond_expert_b, L0_cond_domain_emb, L0_cond_ln_gamma, L0_cond_ln_beta, L1_cond_W_ada, L1_cond_b_ada, L1_cond_Wq, L1_cond_bq, L1_cond_Wk, L1_cond_bk, L1_cond_Wv, L1_cond_bv, L1_cond_Wo, L1_cond_bo, L1_cond_W1, L1_cond_b1, L1_cond_W2, L1_cond_b2, L1_cond_g2, L1_cond_beta2, L2_cond_w1_nr, L2_cond_b1_nr, L2_cond_w2_nr, L2_cond_b2_nr, L2_cond_w1_tsr, L2_cond_b1_tsr, L2_cond_w2_tsr, L2_cond_b2_tsr, L2_cond_w1_sr, L2_cond_b1_sr, L2_cond_w2_sr, L2_cond_b2_sr, L2_cond_w3_sr, L2_cond_b3_sr, L2_cond_gamma, L2_cond_beta, L3_cond_A_grid, L3_cond_B_grid):
    import jax
    import jax.numpy as jnp

    def _L0_cond_ref(hidden_states, domain_id, down_W, down_b, up_W, up_b, expert_W, expert_b, domain_emb, ln_gamma, ln_beta):
        import jax, jax.numpy as jnp
        import numpy as np
        B, S, D = (32, 256, 256)
        A = 64
        E = 16
        LN_EPS = 1e-05
        residual = hidden_states
        hidden = jnp.einsum('bsd,ad->bsa', hidden_states, down_W) + down_b
        hidden = jax.nn.gelu(hidden, approximate=False)
        valid = (domain_id >= 0) & (domain_id < E)
        idx = jnp.clip(domain_id, 0, E - 1)
        Wsel = expert_W[idx]
        bsel = expert_b[idx]
        expert_out = jnp.einsum('bsa,boa->bso', hidden, Wsel) + bsel[:, None, :]
        domain_output = jnp.where(valid[:, None, None], expert_out, hidden)
        hidden = domain_output + domain_emb[idx][:, None, :]
        hidden = jnp.einsum('bsa,da->bsd', hidden, up_W) + up_b
        x = hidden + residual
        mu = jnp.mean(x, axis=-1, keepdims=True)
        var = jnp.mean(jnp.square(x - mu), axis=-1, keepdims=True)
        return (x - mu) * jax.lax.rsqrt(var + LN_EPS) * ln_gamma + ln_beta

    def _L1_cond_ref(src, src_mask, timestep, attention_bias, W_ada, b_ada, Wq, bq, Wk, bk, Wv, bv, Wo, bo, W1, b1, W2, b2, g2, beta2):
        import jax, jax.numpy as jnp
        import numpy as np
        import math
        D_MODEL = 256
        N_HEAD = 16
        HEAD_DIM = D_MODEL // N_HEAD
        D_FF = 1024
        NUM_STEPS = 100.0
        RESCALE = 4000.0
        EPS = 1e-05

        def _sin_emb(t):
            half = D_MODEL // 2
            x = t.astype(jnp.float32) / NUM_STEPS * RESCALE
            freqs = jnp.exp(jnp.arange(half, dtype=jnp.float32) * (-math.log(10000.0) / (half - 1)))
            e = x[:, None] * freqs[None, :]
            return jnp.concatenate([jnp.sin(e), jnp.cos(e)], axis=-1)

        def _ln(x):
            m = jnp.mean(x, axis=-1, keepdims=True)
            v = jnp.var(x, axis=-1, keepdims=True)
            return (x - m) / jnp.sqrt(v + EPS)

        def _gelu2(x):
            return x * jax.nn.sigmoid(1.702 * x)
        B, S, D = src.shape
        emb = jax.nn.silu(_sin_emb(timestep)) @ W_ada + b_ada
        scale, shift = jnp.split(emb[:, None, :], 2, axis=-1)
        x = _ln(src) * (1.0 + scale) + shift
        q = (x @ Wq + bq).reshape(B, S, N_HEAD, HEAD_DIM).transpose(0, 2, 1, 3)
        k = (x @ Wk + bk).reshape(B, S, N_HEAD, HEAD_DIM).transpose(0, 2, 1, 3)
        v = (x @ Wv + bv).reshape(B, S, N_HEAD, HEAD_DIM).transpose(0, 2, 1, 3)
        scores = jnp.einsum('bhqd,bhkd->bhqk', q / math.sqrt(HEAD_DIM), k)
        scores = scores + attention_bias
        scores = jnp.where(src_mask, -jnp.inf, scores.astype(jnp.float32))
        probs = jax.nn.softmax(scores, axis=-1).astype(v.dtype)
        ctx = jnp.einsum('bhqk,bhkd->bhqd', probs, v)
        ctx = ctx.transpose(0, 2, 1, 3).reshape(B, S, D)
        x = x + (ctx @ Wo + bo)
        h = _ln(x) * g2 + beta2
        ff = _gelu2(h @ W1 + b1) @ W2 + b2
        return x + ff

    def _L2_cond_ref(x, condition, w1_nr, b1_nr, w2_nr, b2_nr, w1_tsr, b1_tsr, w2_tsr, b2_tsr, w1_sr, b1_sr, w2_sr, b2_sr, w3_sr, b3_sr, gamma, beta):
        import jax, jax.numpy as jnp
        import numpy as np
        H = 256
        EPS = 1e-05

        def _gelu(x):
            return jax.nn.gelu(x, approximate=False)
        out_nr = _gelu(jnp.einsum('bth,hk->btk', x, w1_nr) + b1_nr)
        out_nr = jnp.einsum('bth,hk->btk', out_nr, w2_nr) + b2_nr
        out_tsr = _gelu(jnp.einsum('bth,hk->btk', x, w1_tsr) + b1_tsr)
        out_tsr = jnp.einsum('bth,hk->btk', out_tsr, w2_tsr) + b2_tsr
        h = _gelu(jnp.einsum('bth,hk->btk', x, w1_sr) + b1_sr)
        h = _gelu(jnp.einsum('bth,hk->btk', h, w2_sr) + b2_sr)
        out_sr = jnp.einsum('bth,hk->btk', h, w3_sr) + b3_sr
        c = condition[:, None, None]
        out = jnp.where(c == 0, out_nr, jnp.where(c == 1, out_tsr, jnp.where(c == 2, out_sr, jnp.zeros_like(x))))
        y = x + out
        mu = jnp.mean(y, axis=-1, keepdims=True)
        var = jnp.mean((y - mu) ** 2, axis=-1, keepdims=True)
        return (y - mu) * jax.lax.rsqrt(var + EPS) * gamma + beta

    def _L3_cond_ref(f, A_grid, B_grid, dt):
        import jax, jax.numpy as jnp
        import numpy as np
        B, NX, NY = (16, 256, 256)

        def _grad(f, axis):
            fm = jnp.moveaxis(f, axis, -1)
            g = (jnp.roll(fm, -1, -1) - jnp.roll(fm, 1, -1)) * 0.5
            g0 = (-3.0 * fm[..., 0] + 4.0 * fm[..., 1] - fm[..., 2]) * 0.5
            gN = (3.0 * fm[..., -1] - 4.0 * fm[..., -2] + fm[..., -3]) * 0.5
            g = g.at[..., 0].set(g0).at[..., -1].set(gN)
            return jnp.moveaxis(g, -1, axis)

        def _grad2(f, axis):
            fm = jnp.moveaxis(f, axis, -1)
            g = jnp.roll(fm, -1, -1) - 2.0 * fm + jnp.roll(fm, 1, -1)
            g0 = 2.0 * fm[..., 0] - 5.0 * fm[..., 1] + 4.0 * fm[..., 2] - fm[..., 3]
            gN = 2.0 * fm[..., -1] - 5.0 * fm[..., -2] + 4.0 * fm[..., -3] - fm[..., -4]
            g = g.at[..., 0].set(g0).at[..., -1].set(gN)
            return jnp.moveaxis(g, -1, axis)
        Af = A_grid[None] * f[:, None]
        Bf = B_grid[None] * f[:, None]
        gradv_Af = _grad(Af[:, 0], 1) + _grad(Af[:, 1], 2)
        gradvv_Bf = _grad2(Bf[:, 0], 1) + _grad2(Bf[:, 1], 2) + _grad(_grad(Bf[:, 2], 2), 1) + _grad(_grad(Bf[:, 2], 1), 2)
        df = -gradv_Af + gradvv_Bf * 0.5
        f_new = f + df * dt[:, None, None]
        return jnp.maximum(f_new, 0.0)
    x = _L0_cond_ref(x, itok_B_0_15, L0_cond_down_W, L0_cond_down_b, L0_cond_up_W, L0_cond_up_b, L0_cond_expert_W, L0_cond_expert_b, L0_cond_domain_emb, L0_cond_ln_gamma, L0_cond_ln_beta)
    x = _L1_cond_ref(x, mask_Bx1xSxS_bk0, itok_B_34_63, fside_Bx16xSxS_0, L1_cond_W_ada, L1_cond_b_ada, L1_cond_Wq, L1_cond_bq, L1_cond_Wk, L1_cond_bk, L1_cond_Wv, L1_cond_bv, L1_cond_Wo, L1_cond_bo, L1_cond_W1, L1_cond_b1, L1_cond_W2, L1_cond_b2, L1_cond_g2, L1_cond_beta2)
    x = _L2_cond_ref(x, itok_B_0_2, L2_cond_w1_nr, L2_cond_b1_nr, L2_cond_w2_nr, L2_cond_b2_nr, L2_cond_w1_tsr, L2_cond_b1_tsr, L2_cond_w2_tsr, L2_cond_b2_tsr, L2_cond_w1_sr, L2_cond_b1_sr, L2_cond_w2_sr, L2_cond_b2_sr, L2_cond_w3_sr, L2_cond_b3_sr, L2_cond_gamma, L2_cond_beta)
    x = _L3_cond_ref(x, L3_cond_A_grid, L3_cond_B_grid, condB_dt)
    return x

_drawn_inputs = setup_inputs


def setup_inputs(seed=0):
    import zlib

    import numpy as np

    out = dict(_drawn_inputs(seed))
    spreads = {'L0_cond_ln_gamma': (1.0, 0.2),
     'L0_cond_ln_beta': (0.0, 0.1),
     'L1_cond_b_ada': (0.0, 0.1),
     'L1_cond_bq': (0.0, 0.8),
     'L1_cond_bk': (0.0, 0.8),
     'L1_cond_bv': (0.0, 0.1),
     'L1_cond_bo': (0.0, 0.1),
     'L1_cond_b1': (0.0, 0.1),
     'L1_cond_b2': (0.0, 0.1),
     'L1_cond_g2': (1.0, 0.6),
     'L1_cond_beta2': (0.0, 0.656),
     'L2_cond_b1_nr': (0.0, 0.1),
     'L2_cond_b2_nr': (0.0, 0.1),
     'L2_cond_b1_tsr': (0.0, 0.1),
     'L2_cond_b2_tsr': (0.0, 0.1),
     'L2_cond_b1_sr': (0.0, 0.1),
     'L2_cond_b2_sr': (0.0, 0.1),
     'L2_cond_b3_sr': (0.0, 0.1),
     'L2_cond_gamma': (1.0, 0.2),
     'L2_cond_beta': (0.0, 0.1)}
    factors = {'fside_Bx16xSxS_0': 8.0, 'L0_cond_down_b': 8.0, 'L1_cond_Wq': 8.0, 'L1_cond_Wk': 8.0}
    for name, (base, spread) in spreads.items():
        noise = np.random.default_rng([zlib.crc32(name.encode()), seed]).standard_normal(out[name].shape)
        drawn = base * np.exp(spread * noise) if base else spread * noise
        out[name] = jnp.asarray(drawn.astype(out[name].dtype))
    for name, factor in factors.items():
        out[name] = (out[name] * factor).astype(out[name].dtype)
    return out
```

```python
from contextlib import ExitStack

import numpy as np

import concourse.bass as bass
from concourse import mybir

ALU = mybir.AluOpType
ACT = mybir.ActivationFunctionType
AX_X = mybir.AxisListType.X
F32 = mybir.dt.float32
F32R = mybir.dt.float32r
BF16 = mybir.dt.bfloat16
I32 = mybir.dt.int32
U8 = mybir.dt.uint8

P = 128
NB = 16
S = 256
D = 256
TT = S // P
KT = D // P
H = 16
DH = D // H
HM = H // KT
A = 64
NE = 16
FF = 1024
FM = FF // P
NC2 = 3
NSIDE = 8
A2 = 512
VW = 32
NBLK = 4
SLOTS = 18
EPS = 1e-5
MASKED = -float(2.0 ** 127)
ROUND = float(1.5 * 2 ** 23)
TWO_PI = (6.28125, 0.0019350051879882812, 3.0198672e-07)

EVENTS = """
xT_turned xT_ready down_done g0_ready wexp_ready expert_done g1_ready up_done xa_ready
xa_stats xa_aggr xa_var xa_rstd n1_ready y_scaled y_ready
y_stats y_aggr y_var y_rstd z_ready x1_scaled x1_ready x1_turned x1T_ready
q_done qh_ready ql_ready k_done kh_ready kl_ready mask_ready
v_done v_ready x1res_ready ct_lo ct_hi nan_twice nan_ready
c1_lo c1_hi sum_lo sum_hi inv_lo inv_hi ctxn_lo ctxn_hi c2_turned ctxT_ready wo_done x2_ready
x2_stats x2_aggr x2_var x2_rstd n3_ready x2b_ready n3_turned n3T_ready
w2_done x3_ready bcf_ready x3c_ready x3_turned x3T_ready b_done gb_ready c_done x4_ready
x4_stats x4_aggr x4_var x4_rstd n5_ready f_scaled f_ready
ga_ready gb2_ready gc_ready r1_ready r2_ready p_ready u_edge u_cols u_inner u_ready
e_edge e_cols e_inner e_ready d_done w_ready w2s_ready out_ready
""".split()


class Sample:

    def __init__(self, e, t, off):
        self.e, self.t, self.off = e, t, off
        self.i = self.keep(t + off)
        self.p = self.i
        self.n = self.keep(t + (off + 1))
        self.h = {k: self.keep(t * 4 + (4 * off + k + 1)) for k in range(-1, 4)}

    def keep(self, v):
        return v if isinstance(v, int) else self.e.snap(v)


def rest_grad(n):
    m = np.zeros((n, n), np.float32)
    for i in range(1, n - 1):
        m[i, i + 1], m[i, i - 1] = 0.5, -0.5
    m[0, :3] = (-1.5, 2.0, -0.5)
    m[n - 1, n - 3:] = (0.5, -2.0, 1.5)
    return m


def rest_grad2(n):
    m = np.zeros((n, n), np.float32)
    for i in range(1, n - 1):
        m[i, i - 1], m[i, i], m[i, i + 1] = 1.0, -2.0, 1.0
    m[0, :4] = (2.0, -5.0, 4.0, -1.0)
    m[n - 1, n - 4:] = (-1.0, 4.0, -5.0, 2.0)
    return m


def build(nc, d):
    with ExitStack() as ctx:
        def sb(name, shape, dt=F32):
            return ctx.enter_context(nc.sbuf_tensor(name, shape, dt))

        def sem(name):
            return ctx.enter_context(nc.semaphore(name))

        ident = sb("ident", [P, P])
        ident_b = sb("ident_b", [P, P], BF16)
        ones_row = sb("ones_row", [1, P])
        downT = sb("downT", [P, KT, A])
        down_b = sb("down_b", [A, 1])
        upT = sb("upT", [A + 1, D])
        wq = sb("wq", [P, KT, D])
        wk = sb("wk", [P, KT, D])
        wv = sb("wv", [P, KT, D])
        wo = sb("wo", [P, KT, D])
        w1 = sb("w1", [P, KT, FF])
        w2 = sb("w2", [P, FM, D])
        wa = sb("wa", [P, KT, A2])
        cols = sb("cols", [P, 64])
        bq, bk, bv = cols[:, 0:2], cols[:, 2:4], cols[:, 4:6]
        g2c, beta2c, b1c, bac, freq = cols[:, 6:8], cols[:, 8:10], cols[:, 10:18], cols[:, 18:22], cols[:, 22:23]
        bbc = cols[:, 24:30].rearrange("p (c m) -> p c m", c=NC2)
        gamma0 = sb("gamma0", [P, D])
        beta0 = sb("beta0", [P, D])
        b2r = sb("b2r", [P, D])
        bo = sb("bo", [P, D])
        gamma3 = sb("gamma3", [P, D])
        beta3 = sb("beta3", [P, D])
        d1T = sb("d1T", [P, KT, S])
        d2T = sb("d2T", [P, KT, S])
        grid_a = sb("grid_a", [P, TT, D])
        grid_b = sb("grid_b", [P, TT, D])
        grid_c = sb("grid_c", [P, TT, D])
        grid_r1 = sb("grid_r1", [P, TT, D])
        grid_r2 = sb("grid_r2", [P, TT, D])
        grid_p = sb("grid_p", [P, TT, D])
        edge_e = sb("edge_e", [P, TT, 2, 4])
        edge_u = sb("edge_u", [P, TT, 2, 4])
        ids = sb("ids", [P, 3, NB], I32)
        idf = sb("idf", [P, 3, NB])
        flags = sb("flags", [P, 8, NB])
        dom_ok, dom_no, kind_ok, dt = flags[:, 0, :], flags[:, 1, :], flags[:, 2, :], flags[:, 3, :]
        ids_ok = sb("ids_ok", [P, 3, NB], I32)
        half_neg = sb("half_neg", [P, TT])
        bsel = sb("bsel", [P, NB, KT])

        xN = sb("xN", [P, TT, D])
        xT = sb("xT", [P, KT, S])
        g0 = sb("g0", [A, S])
        g1 = sb("g1", [A + 1, S])
        wexp_raw = sb("wexp_raw", [A, A + 2])
        wexp = sb("wexp", [A, A + 2])
        xa = sb("xa", [P, TT, D])
        yN = xa
        x1 = sb("x1", [P, TT, D])
        x1T = sb("x1T", [P, KT, S])
        ada = sb("ada", [P, 2, D])
        qh = sb("qh", [P, KT, S], F32R)
        ql = sb("ql", [P, KT, S], F32R)
        kh = sb("kh", [P, KT, S], F32R)
        kl = sb("kl", [P, KT, S], F32R)
        qs = sb("qs", [P, H, S], F32R)
        ks = sb("ks", [P, H, S], F32R)
        mask_raw = sb("mask_raw", [P, TT, S // 4], I32)
        mask_neg = sb("mask_neg", [P, TT, S], BF16)
        side = sb("side", [P, NSIDE, TT, S])
        NS, NP2 = 3, 3
        sc = sb("sc", [P, NS, TT, S])
        pt = sb("pt", [P, NP2, TT, S])
        negmax = sb("negmax", [P, TT, H])
        nan2 = sb("nan2", [P, TT, H])
        nanz = sb("nanz", [P, TT, H])
        vp = sb("vp", [P, TT, H, VW])
        cts = sb("cts", [P, H // 4, S])
        rsum = sb("rsum", [P, TT, H])
        rinv = sb("rinv", [P, TT, H])
        x1res = sb("x1res", [P, TT, D])
        n3 = sb("n3", [P, TT, D])
        n3T = sb("n3T", [P, KT, S])
        ctxN, ctxT, x3T = n3, n3T, n3T
        x2 = sb("x2", [P, TT, D])
        x2b = x2
        ffT = sb("ffT", [P, FM, S])
        x3 = sb("x3", [P, TT, D])
        x3c = sb("x3c", [P, TT, D])
        gaT = sb("gaT", [P, A2 // P, S])
        gbT = sb("gbT", [P, KT, S])
        wb = sb("wb", [P, A2 // P, D])
        wc = sb("wc", [P, KT, D])
        bcr = sb("bcr", [P, D])
        bcf = sb("bcf", [P, D])
        x4 = sb("x4", [P, TT, D])
        fN = sb("fN", [P, TT, D])
        t_a = sb("t_a", [P, TT, D])
        t_b = sb("t_b", [P, TT, D])
        t_c = sb("t_c", [P, TT, D])
        t_r1 = sb("t_r1", [P, TT, D])
        t_r2 = sb("t_r2", [P, TT, D])
        t_u = sb("t_u", [P, TT, D])
        t_e = sb("t_e", [P, TT, D])
        t_p = t_e
        edge_t = sb("edge_t", [P, 2, TT, 2, 4])
        outN = sb("outN", [P, TT, D])
        stats = sb("stats", [P, 4, TT, 6])
        mv = sb("mv", [P, 4, TT, 2])
        var = sb("var", [P, 4, TT])
        rstd = sb("rstd", [P, 4, TT])

        def bank(name):
            return ctx.enter_context(nc.psum_tensor(name, [P, 512], F32))

        sbank = [bank("score_bank0"), bank("score_bank1")]
        tbank = [bank("turn_bank0"), bank("turn_bank1")]
        cbank = bank("context_bank")
        fbank = bank("front_bank")
        bbank = [bank("back_bank0"), bank("back_bank1")]

        def two(b):
            return b[:, :].rearrange("p (a x) -> p a x", a=2)

        ev = {n: sem(n) for n in EVENTS}
        scored = [sem(f"scored{h}") for h in range(4)]
        biased = [sem(f"biased{h}") for h in range(4)]
        expd = [sem(f"expd{h}") for h in range(4)]
        turned = [sem(f"turned{h}") for h in range(4)]
        copied = [sem(f"copied{h}") for h in range(4)]
        mixed = [sem(f"mixed{h}") for h in range(4)]
        w1_done = [sem(f"w1_done{j}") for j in range(4)]
        ff_ready = [sem(f"ff_ready{j}") for j in range(4)]
        wa_done = [sem(f"wa_done{j}") for j in range(2)]
        ga2_ready = [sem(f"ga2_ready{j}") for j in range(2)]
        ld_x, ld_mask, ld_exp, ld_ada, ld_kind = sem("ld_x"), sem("ld_mask"), sem("ld_exp"), sem("ld_ada"), sem("ld_kind")
        ld_side = [sem(f"ld_side{c}") for c in range(4)]
        ld_stack = [sem(f"ld_stack{m}") for m in range(KT)]
        stored = sem("stored")
        wexp_half = sem("wexp_half")
        passed = {k: sem(f"passed_{n}") for k, n in ((nc.vector.engine, "dve"), (nc.tensor.engine, "pe"), (nc.gpsimd.engine, "pool"))}
        ld_set, ld_ids, st_ada = sem("ld_set"), sem("ld_ids"), sem("st_ada")
        pool_set, dve_set, act_set, pe_set, idx_ready, ready = (
            sem("pool_set"), sem("dve_set"), sem("act_set"), sem("pe_set"), sem("idx_ready"), sem("ready"))
        sem_dve = sem("sem_dve")

        block = ctx.enter_context(nc.Block())

        def wait(e, s, n):
            if not (isinstance(n, int) and n <= 0):
                e.wait_ge(s, n)

        def phase(e, t, off):
            if isinstance(t, int) and not 0 <= t + off < NB:
                return None
            return Sample(e, t, off)

        def hold(e):
            e.sem_inc(passed[e.engine], 1)

        def times(x, k, prev=False):
            return x.keep((x.t + x.off + (0 if prev else 1)) * k)

        def head(e, s, x, h):
            wait(e, s[h % 4], x.h[h // 4])

        def turns(e, body):
            for t in (-1, 0, 1, 2):
                body(t)
            with e.Fori(3, NB - 1) as t:
                body(t)
            for t in (NB - 1, NB, NB + 1):
                body(t)

        def phases(e, t):
            return phase(e, t, 1), phase(e, t, 0), phase(e, t, -1), phase(e, t, -2)

        LOADS = 29

        @block.sync
        def _(e):
            for k in range(3):
                e.dma_start(ids[:, k, :], d[("dom", "step", "kind")[k]].partition_broadcast(P)).then_inc(ld_ids, 16)
            e.dma_start(dt, d["dt"].partition_broadcast(P)).then_inc(ld_ids, 16)
            n = 0
            for dst, src in (
                (freq, d["freq"].rearrange("(p a) -> p a", a=1)),
                (down_b[:, :], d["down_b"].rearrange("(p a) -> p a", a=1)),
                (downT[:, :, :], d["downT"].rearrange("(k p) a -> p k a", p=P)),
                (upT[0:A, :], d["upT"]),
                (upT[A:A + 1, :], d["up_b"].rearrange("(a n) -> a n", a=1)),
                (wq[:, :, :], d["wq"].rearrange("(k p) n -> p k n", p=P)),
                (wk[:, :, :], d["wk"].rearrange("(k p) n -> p k n", p=P)),
                (wv[:, :, :], d["wv"].rearrange("(k p) n -> p k n", p=P)),
                (wo[:, :, :], d["wo"].rearrange("(k p) n -> p k n", p=P)),
                (w1[:, :, :], d["w1"].rearrange("(k p) n -> p k n", p=P)),
                (w2[:, :, :], d["w2"].rearrange("(k p) n -> p k n", p=P)),
                (wa[:, :, :], d["wa"].rearrange("(k p) n -> p k n", p=P)),
                (cols[:, 0:22], d["colpack"][:, 0:22]),
                (cols[:, 24:30], d["colpack"][:, 22:28]),
                (gamma0[:, :], d["gamma0"].partition_broadcast(P)),
                (beta0[:, :], d["beta0"].partition_broadcast(P)),
                (b2r[:, :], d["b2"].partition_broadcast(P)),
                (bo[:, :], d["bo"].partition_broadcast(P)),
                (gamma3[:, :], d["gamma3"].partition_broadcast(P)),
                (beta3[:, :], d["beta3"].partition_broadcast(P)),
                (d1T[:, :, :], d["d1T"].rearrange("(k p) n -> p k n", p=P)),
                (d2T[:, :, :], d["d2T"].rearrange("(k p) n -> p k n", p=P)),
                (x2[:, :, :], d["grid_A"][0].rearrange("(t p) n -> p t n", p=P)),
                (x3[:, :, :], d["grid_A"][1].rearrange("(t p) n -> p t n", p=P)),
                (t_a[:, :, :], d["grid_B"][0].rearrange("(t p) n -> p t n", p=P)),
                (t_b[:, :, :], d["grid_B"][1].rearrange("(t p) n -> p t n", p=P)),
                (t_c[:, :, :], d["grid_B"][2].rearrange("(t p) n -> p t n", p=P)),
                (ffT[:, 0:4, :], d["w_ada"].rearrange("(k p) n -> p k n", p=P)),
                (xa[0:1, :, :], d["b_ada"].rearrange("(a k n) -> a k n", a=1, k=2)),
            ):
                e.dma_start(dst, src).then_inc(ld_set, 16)
                n += 1
            assert n == LOADS
            e.wait_ge(dve_set, 2)
            e.dma_start(d["ada_rows"], x3T[0:NB, :, :]).then_inc(st_ada, 16)
            e.wait_ge(idx_ready, 1)
            e.wait_ge(st_ada, 16)
            e.wait_ge(ready, 4)

            def load_side(x, c):
                e.dma_start(side[:, 4 * c % NSIDE:4 * c % NSIDE + 4, :, :],
                            d["side"][bass.ds(x.i, 1), 4 * c:4 * c + 4].rearrange("b h (t p) k -> p (b h) t k", p=P)
                            ).then_inc(ld_side[c], 16)

            def stack(x, prev, m):
                if prev is not None:
                    head(e, scored, prev, HM * m + HM - 1)
                for b in range(NBLK):
                    for dst, hi, lo, low in ((qs, qh, ql, b >= 2), (ks, kh, kl, b % 2 == 1)):
                        src = lo if low else hi
                        e.dma_start(dst[DH * b:DH * b + DH, HM * m:HM * m + HM, :].bitcast(F32), src[:, m, :].bitcast(F32)).then_inc(ld_stack[m], 16)

            def body(t):
                F, X, B, T = phases(e, t)
                for s in range(SLOTS):
                    if s == 0 and F:
                        wait(e, ev["xa_ready"], F.p)
                        e.dma_start(xN[:, :, :], d["x"][bass.ds(F.i, 1)].rearrange("b (t p) n -> p (b t) n", p=P)).then_inc(ld_x, 16)
                        wait(e, ev["mask_ready"], F.p)
                        e.dma_start(mask_raw[:, :, :], d["mask"][bass.ds(F.i, 1)].rearrange("b (t p) n -> p (b t) n", p=P)).then_inc(ld_mask, 16)
                        wait(e, ev["wexp_ready"], F.p)
                        dom = e.value_load(ids_ok[0:1, 0, bass.ds(F.i, 1)], min_val=0, max_val=NE - 1)
                        e.dma_start(wexp_raw[:, :], d["expert"][bass.ds(dom, 1)].rearrange("e a n -> (e a) n")).then_inc(ld_exp, 16)
                        wait(e, ev["x1_ready"], F.p)
                        e.dma_start(ada[:, :, :].rearrange("p a n -> p (a n)"), d["ada_rows"][bass.ds(F.i, 1)].rearrange("b n -> (b n)").partition_broadcast(P)).then_inc(ld_ada, 16)
                        if isinstance(t, int) and t == -1:
                            for c in range(2):
                                load_side(F, c)
                    if s == 1 and B:
                        kind = e.value_load(ids_ok[0:1, 2, bass.ds(B.i, 1)], min_val=0, max_val=NC2 - 1)
                        wait(e, ev["b_done"], B.p)
                        e.dma_start(wb[:, :, :], d["wb"][bass.ds(kind, 2)].rearrange("c (k p) n -> p (c k) n", p=P)).then_inc(ld_kind, 16)
                        wait(e, ev["c_done"], B.p)
                        e.dma_start(wc[:, :, :], d["wc"][bass.ds(kind, 1)].rearrange("c (k p) n -> p (c k) n", p=P)).then_inc(ld_kind, 16)
                        wait(e, ev["bcf_ready"], B.p)
                        e.dma_start(bcr[:, :], d["bc"][bass.ds(kind, 1)].rearrange("c n -> (c n)").partition_broadcast(P)).then_inc(ld_kind, 16)
                    if s in (4, 8, 12, 16) and X and (F or s < 12):
                        c = s // 4 - 1
                        head(e, biased, X, 4 * c + 3)
                        load_side(X if c < 2 else F, (c + 2) % 4)
                    if s == 11 and T:
                        e.wait_ge(ev["out_ready"], T.n)
                        e.dma_start(d["out"][bass.ds(T.i, 1)].rearrange("b (t p) n -> p (b t) n", p=P), outN[:, :, :]).then_inc(stored, 16)
                    if s == 14 and F:
                        e.wait_ge(ev["ql_ready"], F.n)
                        e.wait_ge(ev["kl_ready"], F.n)
                        stack(F, X, 0)
                    if s == 17 and F:
                        stack(F, X, 1)

            turns(e, body)
            e.wait_ge(stored, 16 * NB)

        @block.gpsimd
        def _(e):
            e.memset(ident[:, :], 0.0).then_inc(pool_set, 1)
            e.memset(half_neg[:, :], -0.5)
            e.memset(ones_row[:, :], 1.0)
            e.memset(g1[:, :], 1.0)
            e.memset(vp[:, :, :, :], 0.0).then_inc(pool_set, 1)
            e.wait_ge(pool_set, 2)
            e.memset(vp[:, :, :, DH:DH + 1], 1.0)
            e.affine_select(out=ident[:, :], in_=ident[:, :], compare_op=ALU.not_equal, fill=1.0,
                            base=0, pattern=[[-1, P]], channel_multiplier=1).then_inc(pool_set, 1)
            e.wait_ge(pool_set, 3)
            e.tensor_copy(ident_b[:, :], ident[:, :]).then_inc(ready, 1)
            e.wait_ge(ready, 4)

            def power(x, k, var_ev, rstd_ev):
                e.wait_ge(var_ev, x.n)
                e.tensor_tensor(rstd[:, k, :], var[:, k, :], half_neg[:, :], ALU.pow).then_inc(rstd_ev, 1)

            def rows(r):
                return r.unsqueeze(1).broadcast_to([P, TT, D])

            def body(t):
                F, X, B, T = phases(e, t)
                for s in range(SLOTS):
                    if s == 0 and T:
                        power(T, 3, ev["x4_var"], ev["x4_rstd"])
                    if s == 1 and T:
                        e.wait_ge(ev["n5_ready"], T.n)
                        e.tensor_tensor(fN[:, :, :], x4[:, :, :], rows(gamma3[:, :]), ALU.mult).then_inc(ev["f_scaled"], 1)
                        e.wait_ge(ev["f_scaled"], T.n)
                        e.tensor_tensor(fN[:, :, :], fN[:, :, :], rows(beta3[:, :]), ALU.add).then_inc(ev["f_ready"], 1)
                    if s == 2 and T:
                        e.wait_ge(ev["f_ready"], T.n)
                        e.tensor_tensor(t_r1[:, :, :], fN[:, :, :], grid_r1[:, :, :], ALU.mult).then_inc(ev["r1_ready"], 1)
                        e.tensor_tensor(t_r2[:, :, :], fN[:, :, :], grid_r2[:, :, :], ALU.mult).then_inc(ev["r2_ready"], 1)
                    if s == 4 and B:
                        power(B, 2, ev["x2_var"], ev["x2_rstd"])
                    if s == 4 and T:
                        e.tensor_tensor(t_a[:, :, :], fN[:, :, :], grid_a[:, :, :], ALU.mult).then_inc(ev["ga_ready"], 1)
                    if s == 5 and F:
                        power(F, 0, ev["xa_var"], ev["xa_rstd"])
                    if s == 5 and T:
                        e.tensor_tensor(t_b[:, :, :], fN[:, :, :], grid_b[:, :, :], ALU.mult).then_inc(ev["gb2_ready"], 1)
                    if s == 5 and X:
                        wait(e, ev["x2_ready"], X.p)
                        e.wait_ge(ev["x1_ready"], X.n)
                        e.tensor_tensor(x1res[:, :, :], x1[:, :, :], rows(bo[:, :]), ALU.add).then_inc(ev["x1res_ready"], 1)
                    if s == 6 and F:
                        e.wait_ge(ev["n1_ready"], F.n)
                        e.tensor_tensor(yN[:, :, :], xa[:, :, :], rows(gamma0[:, :]), ALU.mult).then_inc(ev["y_scaled"], 1)
                        e.wait_ge(ev["y_scaled"], F.n)
                        e.tensor_tensor(yN[:, :, :], yN[:, :, :], rows(beta0[:, :]), ALU.add).then_inc(ev["y_ready"], 1)
                    if s == 6 and T:
                        e.tensor_tensor(t_c[:, :, :], fN[:, :, :], grid_c[:, :, :], ALU.mult).then_inc(ev["gc_ready"], 1)
                    if s == 7 and B:
                        e.wait_ge(ev["n3_ready"], B.n)
                        e.tensor_tensor(x2b[:, :, :], x2[:, :, :], rows(b2r[:, :]), ALU.add).then_inc(ev["x2b_ready"], 1)
                    if s == 8 and F:
                        power(F, 1, ev["y_var"], ev["y_rstd"])
                    if s == 9 and F:
                        e.wait_ge(ev["z_ready"], F.n)
                        e.wait_ge(ld_ada, times(F, 16))
                        wait(e, ev["x1_turned"], F.p)
                        wait(e, ev["x1res_ready"], F.p)
                        e.tensor_tensor(x1[:, :, :], yN[:, :, :], rows(ada[:, 0, :]), ALU.mult).then_inc(ev["x1_scaled"], 1)
                        e.wait_ge(ev["x1_scaled"], F.n)
                        e.tensor_tensor(x1[:, :, :], x1[:, :, :], rows(ada[:, 1, :]), ALU.add).then_inc(ev["x1_ready"], 1)
                    if s == 13 and B:
                        e.wait_ge(ev["bcf_ready"], B.n)
                        e.wait_ge(ev["x3_ready"], B.n)
                        wait(e, ev["x4_ready"], B.p)
                        e.tensor_tensor(x3c[:, :, :], x3[:, :, :], rows(bcf[:, :]), ALU.add).then_inc(ev["x3c_ready"], 1)
                    if s == 17 and F:
                        e.wait_ge(ld_mask, times(F, 16))
                        head(e, scored, F, -1)
                        hold(e)
                        e.tensor_scalar(mask_neg[:, :, :], mask_raw[:, :, :].bitcast(U8), MASKED, None, ALU.mult).then_inc(ev["mask_ready"], 1)

            turns(e, body)

        @block.scalar
        def _(e):
            e.wait_ge(dve_set, 1)
            e.activation(x1T[:, :, 0:NB], x1T[:, :, 0:NB], ACT.Sin).then_inc(act_set, 1)
            e.wait_ge(act_set, 1)
            e.activation(x1T[:, :, 0:NB], x1T[:, :, 0:NB], ACT.Silu).then_inc(act_set, 1)
            e.wait_ge(ready, 4)

            def copy_turned(x, h):
                head(e, turned, x, h)
                head(e, mixed, x, h - NP2)
                e.activation(pt[:, h % NP2, :, :], two(tbank[h % 2]), ACT.Copy).then_inc(copied[h % 4], 1)

            def body(t):
                F, X, B, T = phases(e, t)
                if B:
                    kind = e.value_load(ids_ok[0:1, 2, bass.ds(B.i, 1)], min_val=0, max_val=NC2 - 1)
                for s in range(SLOTS):
                    if s < H and X:
                        head(e, biased, X, s)
                        for q in range(TT):
                            i = e.activation(sc[:, s % NS, q, :], sc[:, s % NS, q, :], ACT.Exp,
                                             bias=negmax[:, q, s:s + 1], scale=-1.0)
                        i.then_inc(expd[s % 4], 1)
                    if 1 <= s <= H and X and (s - 1) % 2 == 0:
                        copy_turned(X, s - 1)
                    if s == 0 and X:
                        e.wait_ge(ev["v_done"], X.n)
                        head(e, mixed, X, -1)
                        e.activation(vp[:, :, :, 0:DH], fbank[:, :].rearrange("p (t h c) -> p t h c", t=TT, h=H), ACT.Copy).then_inc(ev["v_ready"], 1)
                    if s == 1 and F:
                        e.wait_ge(ev["xT_turned"], F.n)
                        wait(e, ev["down_done"], F.p)
                        e.activation(xT[:, :, :], two(fbank), ACT.Copy).then_inc(ev["xT_ready"], 1)
                    if s == 2 and F:
                        e.wait_ge(ev["down_done"], F.n)
                        wait(e, ev["expert_done"], F.p)
                        e.activation(g0[:, :], fbank[0:A, 0:S], ACT.Gelu, bias=down_b[:, 0:1]).then_inc(ev["g0_ready"], 1)
                    if s == 2 and B:
                        e.wait_ge(ev["c2_turned"], B.n)
                        wait(e, ev["wo_done"], B.p)
                        e.activation(ctxT[:, :, :], two(bbank[0]), ACT.Copy).then_inc(ev["ctxT_ready"], 1)
                    if s == 3 and F:
                        e.wait_ge(ev["expert_done"], F.n)
                        e.wait_ge(ev["wexp_ready"], F.n)
                        wait(e, ev["up_done"], F.p)
                        e.activation(g1[0:A, :], fbank[0:A, 0:S], ACT.Identity, bias=wexp[:, A:A + 1]).then_inc(ev["g1_ready"], 1)
                    if s == 6 and B:
                        e.wait_ge(ev["n3_turned"], B.n)
                        wait(e, w1_done[3], B.p)
                        e.activation(n3T[:, :, :], two(bbank[0]), ACT.Copy).then_inc(ev["n3T_ready"], 1)
                    if s in (7, 8, 9, 10) and B:
                        j = s - 7
                        e.wait_ge(w1_done[j], B.n)
                        wait(e, ev["w2_done"], B.p)
                        for m in range(2):
                            i = e.activation(ffT[:, 2 * j + m, :], two(bbank[(j + 1) % 2])[:, m, :], ACT.Gelu_apprx_sigmoid,
                                             bias=b1c[:, 2 * j + m:2 * j + m + 1])
                        i.then_inc(ff_ready[j], 1)
                    if s == 10 and F:
                        e.wait_ge(ev["x1_turned"], F.n)
                        wait(e, ev["v_done"], F.p)
                        e.activation(x1T[:, :, :], two(fbank), ACT.Copy).then_inc(ev["x1T_ready"], 1)
                    if s in (11, 12) and F:
                        done, hi, b, out = ((ev["q_done"], qh, bq, ev["qh_ready"]), (ev["k_done"], kh, bk, ev["kh_ready"]))[s - 11]
                        e.wait_ge(done, F.n)
                        for m in range(KT):
                            wait(e, ld_stack[m], times(F, 128, prev=True))
                        for m in range(KT):
                            i = e.activation(hi[:, m, :], two(fbank)[:, m, :], ACT.Identity, bias=b[:, m:m + 1])
                        i.then_inc(out, 1)
                    if s == 10 and T:
                        e.wait_ge(ev["w2s_ready"], T.n)
                        wait(e, stored, times(T, 16, prev=True))
                        e.activation(outN[:, :, :], t_e[:, :, :], ACT.Relu).then_inc(ev["out_ready"], 1)
                    if s == 9 and X:
                        head(e, mixed, X, HM - 1)
                        wait(e, ev["c1_hi"], X.p)
                        e.activation(cts[:, 0:2, :], two(cbank), ACT.Copy).then_inc(ev["ct_lo"], 1)
                    if s == 13 and B:
                        e.wait_ge(ev["x3_turned"], B.n)
                        wait(e, ev["b_done"], B.p)
                        e.activation(x3T[:, :, :], two(bbank[0]), ACT.Copy).then_inc(ev["x3T_ready"], 1)
                    if s == 14 and B:
                        with e.If(kind == 2):
                            for j in range(2):
                                e.wait_ge(wa_done[j], B.n)
                                for m in range(2):
                                    i = e.activation(gaT[:, 2 * j + m, :], two(bbank[(j + 1) % 2])[:, m, :], ACT.Gelu,
                                                     bias=bac[:, 2 * j + m:2 * j + m + 1])
                                i.then_inc(ga2_ready[j], 1)
                        with e.Else():
                            for j in range(2):
                                e.sem_inc(ga2_ready[j], 1)
                    if s == 15 and B:
                        e.wait_ge(ev["b_done"], B.n)
                        wait(e, ev["c_done"], B.p)
                        for m in range(KT):
                            i = e.activation(gbT[:, m, :], two(bbank[1])[:, m, :], ACT.Gelu, bias=bsel[:, bass.ds(B.i, 1), m])
                        i.then_inc(ev["gb_ready"], 1)
                    if s == 17 and X:
                        head(e, mixed, X, H - 1)
                        e.activation(cts[:, 2:4, :], two(cbank), ACT.Copy).then_inc(ev["ct_hi"], 1)

            turns(e, body)

        @block.vector
        def _(e):
            chain = [0]
            own = sem_dve

            def link(i):
                chain[0] += 1
                i.then_inc(own, 1)
                e.wait_ge(own, chain[0])

            e.memset(qs[64:128, :, :].bitcast(F32), 0.0)
            link(e.memset(ks[64:128, :, :].bitcast(F32), 0.0))
            e.wait_ge(ld_ids, 64)
            link(e.tensor_copy(idf[:, :, :], ids[:, :, :]))
            e.tensor_scalar(flags[:, 4, :], idf[:, 0, :], 0.0, None, ALU.is_ge)
            e.tensor_scalar(flags[:, 5, :], idf[:, 0, :], float(NE), None, ALU.is_lt)
            e.tensor_scalar(flags[:, 6, :], idf[:, 2, :], 0.0, None, ALU.is_ge)
            link(e.tensor_scalar(flags[:, 7, :], idf[:, 2, :], float(NC2), None, ALU.is_lt))
            e.tensor_tensor(dom_ok, flags[:, 4, :], flags[:, 5, :], ALU.mult)
            link(e.tensor_tensor(kind_ok, flags[:, 6, :], flags[:, 7, :], ALU.mult))
            e.tensor_scalar(dom_no, dom_ok, -1.0, 1.0, ALU.mult, ALU.add)
            e.tensor_scalar(ids_ok[:, 0, :], idf[:, 0, :], 0.0, float(NE - 1), ALU.max, ALU.min)
            e.tensor_copy(ids_ok[:, 1, :], idf[:, 1, :])
            link(e.tensor_scalar(ids_ok[:, 2, :], idf[:, 2, :], 0.0, float(NC2 - 1), ALU.max, ALU.min))
            e.sem_inc(idx_ready, 1)
            e.wait_ge(ld_set, 16 * LOADS)
            ang, turn, red = x1T[:, 0, 32:48], x1T[:, 0, 48:64], x1T[:, 0, 64:80]
            link(e.tensor_scalar(turn, idf[:, 1, :], 40.0, None, ALU.mult))
            link(e.tensor_scalar(ang, turn, freq, None, ALU.mult))
            for k in range(2):
                link(e.tensor_scalar(turn, ang, 1.0 / (2 * np.pi), 0.25 * k, ALU.mult, ALU.add))
                link(e.tensor_scalar(turn, turn, ROUND, None, ALU.add))
                link(e.tensor_scalar(turn, turn, -ROUND, None, ALU.add))
                link(e.scalar_tensor_tensor(out=red, in0=turn, scalar=-TWO_PI[0], in1=ang, op0=ALU.mult, op1=ALU.add))
                link(e.scalar_tensor_tensor(out=red, in0=turn, scalar=-TWO_PI[1], in1=red, op0=ALU.mult, op1=ALU.add))
                link(e.scalar_tensor_tensor(out=red, in0=turn, scalar=-TWO_PI[2], in1=red, op0=ALU.mult, op1=ALU.add))
                link(e.tensor_scalar(red, red, float(np.pi / 2) * k, None, ALU.add))
                i = e.tensor_scalar(x1T[:, k, 0:NB], red, -3.1415925, 3.1415925, ALU.max, ALU.min)
                link(i)
            e.sem_inc(dve_set, 1)
            e.wait_ge(pe_set, 1)
            i = e.tensor_scalar(x3T[0:NB, 0, :], fbank[0:NB, 0:D], 1.0, None, ALU.add)
            link(i)
            link(e.tensor_copy(x3T[0:NB, 1, :], fbank[0:NB, D:2 * D]))
            e.sem_inc(dve_set, 1)
            e.tensor_scalar(wq[:, :, :], wq[:, :, :], DH ** -0.5, None, ALU.mult)
            link(e.tensor_scalar(bq, bq, DH ** -0.5, None, ALU.mult))
            ones = n3[:, 0, 0:P]
            link(e.memset(n3[:, 0, 0:P], 1.0))
            for k in range(KT):
                i = e.tensor_scalar(gbT[:, k, 0:P], ones, bv[:, k:k + 1], None, ALU.mult)
            link(i)
            e.sem_inc(dve_set, 1)
            e.wait_ge(pe_set, 2)
            link(e.tensor_tensor(bo[:, :], bbank[0][:, 0:D], bo[:, :], ALU.add))
            link(e.tensor_tensor(b1c, bbank[1][:, 0:FM], b1c, ALU.add))
            for k in range(KT):
                i = e.tensor_scalar(w1[:, k, :], w1[:, k, :], g2c[:, k:k + 1], None, ALU.mult)
            link(i)
            link(e.memset(bsel[:, :, :], 0.0))
            for c in range(NC2):
                link(e.tensor_scalar(flags[:, 4, :], idf[:, 2, :], float(c), None, ALU.is_equal))
                for m in range(KT):
                    link(e.scalar_tensor_tensor(out=bsel[:, :, m], in0=flags[:, 4, :], scalar=bbc[:, c, m:m + 1],
                                                in1=bsel[:, :, m], op0=ALU.mult, op1=ALU.add))
            A0, A1, B0, B1, B2 = x2, x3, t_a, t_b, t_c
            e.tensor_scalar(grid_r1[:, :, :], A0[:, :, :], -1.0, None, ALU.mult)
            e.tensor_scalar(grid_r2[:, :, :], B0[:, :, :], 0.5, None, ALU.mult)
            e.tensor_scalar(grid_p[:, :, :], B2[:, :, :], 0.5, None, ALU.mult)
            link(e.tensor_scalar(grid_c[:, :, :], B1[:, :, :], -1.0, None, ALU.mult))
            e.tensor_tensor(grid_a[:, :, :], B1[:, :, :], A1[:, :, :], ALU.subtract)
            link(e.tensor_tensor(grid_b[:, :, :], B1[:, :, :], A1[:, :, :], ALU.add))
            e.tensor_scalar(grid_a[:, :, :], grid_a[:, :, :], 0.5, None, ALU.mult)
            link(e.tensor_scalar(grid_b[:, :, :], grid_b[:, :, :], -0.5, None, ALU.mult))
            link(e.memset(edge_u[:, :, :, :], 0.0))
            for side_, cs in ((0, (0, 1, 2, 3)), (1, (3, 2, 1, 0))):
                sign = 1.0 if side_ == 0 else -1.0
                for k, (ca, cb, cu) in enumerate(((1.5, 1.0, -1.5), (-2.0, -2.5, 2.0), (0.5, 2.0, -0.5), (0.0, -0.5, 0.0))):
                    j = cs[k] if side_ == 0 else D - 4 + cs[k]
                    e.tensor_scalar(edge_u[:, :, side_, cs[k]], B2[:, :, j], sign * cu, None, ALU.mult)
                    link(e.tensor_scalar(edge_e[:, :, side_, cs[k]], B1[:, :, j], cb, None, ALU.mult))
                    link(e.scalar_tensor_tensor(out=edge_e[:, :, side_, cs[k]], in0=A1[:, :, j], scalar=sign * ca,
                                                in1=edge_e[:, :, side_, cs[k]], op0=ALU.mult, op1=ALU.add))
            e.sem_inc(ready, 1)
            e.wait_ge(ready, 4)

            def norm_stats(x, k, src, s_ev, a_ev, v_ev):
                for q in range(TT):
                    i = e.bn_stats(stats[:, k, q, :], src[:, q, :])
                i.then_inc(s_ev, 1)
                e.wait_ge(s_ev, x.n)
                hold(e)
                for q in range(TT):
                    i = e.bn_aggr(mv[:, k, q, :], stats[:, k, q, :])
                i.then_inc(a_ev, 1)
                e.wait_ge(a_ev, x.n)
                e.tensor_scalar(var[:, k, :], mv[:, k, :, 1], EPS, None, ALU.add).then_inc(v_ev, 1)

            def norm_apply(x, k, dst, src, r_ev, o_ev):
                e.wait_ge(r_ev, x.n)
                for q in range(TT):
                    i = e.tensor_scalar(dst[:, q, :], src[:, q, :], mv[:, k, q, 0:1], rstd[:, k, q:q + 1], ALU.subtract, ALU.mult)
                i.then_inc(o_ev, 1)

            def context(x, q, c1, s_ev, i_ev, o_ev):
                e.wait_ge(c1, x.n)
                v = bbank[q][:, :].rearrange("p (h c) -> p h c", h=H)
                if q == 0:
                    e.wait_ge(ev["nan_ready"], x.n)
                e.tensor_tensor(rsum[:, q, :], v[:, :, DH], nanz[:, q, :], ALU.add).then_inc(s_ev, 1)
                e.wait_ge(s_ev, x.n)
                e.reciprocal(rinv[:, q, :], rsum[:, q, :]).then_inc(i_ev, 1)
                e.wait_ge(i_ev, x.n)
                e.tensor_tensor(ctxN[:, q, :].rearrange("p (h c) -> p h c", h=H), v[:, :, 0:DH],
                                rinv[:, q, :].unsqueeze(2).broadcast_to([P, H, DH]), ALU.mult).then_inc(o_ev, 1)

            def edges(x, grid, k, dst, t_ev, c_ev):
                near = bass.AP(fN, 0, [[TT * D, P], [D, TT], [D - 4, 2], [1, 4]])
                e.tensor_tensor(edge_t[:, k, :, :, :], near, grid[:, :, :, :], ALU.mult).then_inc(t_ev, 1)
                e.wait_ge(t_ev, x.n)
                e.tensor_reduce(bass.AP(dst, 0, [[TT * D, P], [D, TT], [D - 1, 2]]), edge_t[:, k, :, :, :], AX_X, ALU.add).then_inc(c_ev, 1)

            def body(t):
                F, X, B, T = phases(e, t)
                for s in range(SLOTS):
                    if s < H and X:
                        head(e, scored, X, s)
                        e.wait_ge(ld_side[s // 4], times(X, 16))
                        head(e, turned, X, s - NS)
                        if s == 0:
                            head(e, expd, X, -1)
                            wait(e, ev["nan_ready"], X.p)
                        hold(e)
                        for q in range(TT):
                            i = e.tensor_tensor_reduce(sc[:, s % NS, q, :], two(sbank[s % 2])[:, q, :], side[:, s % NSIDE, q, :],
                                                       -1.0, 3.4e38, ALU.add, ALU.min, negmax[:, q, s:s + 1])
                        i.then_inc(biased[s % 4], 1)
                    if 1 <= s <= H and X and (s - 1) % 2 == 1:
                        h = s - 1
                        head(e, turned, X, h)
                        head(e, mixed, X, h - NP2)
                        e.tensor_copy(pt[:, h % NP2, :, :], two(tbank[h % 2])).then_inc(copied[h % 4], 1)
                    if s == 0 and T:
                        e.wait_ge(ev["x4_ready"], T.n)
                        norm_stats(T, 3, x4, ev["x4_stats"], ev["x4_aggr"], ev["x4_var"])
                    if s == 0 and B:
                        context(B, 0, ev["c1_lo"], ev["sum_lo"], ev["inv_lo"], ev["ctxn_lo"])
                    if s == 0 and F:
                        e.wait_ge(ld_exp, times(F, 16))
                        wait(e, ev["expert_done"], F.p)
                        wait(e, ev["g1_ready"], F.p)
                        e.tensor_scalar(wexp[:, 0:A], ident[0:A, 0:A], dom_no[0:A, bass.ds(F.i, 1)], None, ALU.mult)
                        e.tensor_scalar(wexp[:, A:A + 1], wexp_raw[:, A + 1:A + 2], 1.0, None, ALU.mult).then_inc(wexp_half, 1)
                        e.wait_ge(wexp_half, F.n)
                        e.scalar_tensor_tensor(out=wexp[:, 0:A + 1], in0=wexp_raw[:, 0:A + 1], scalar=dom_ok[0:A, bass.ds(F.i, 1)],
                                               in1=wexp[:, 0:A + 1], op0=ALU.mult, op1=ALU.add).then_inc(ev["wexp_ready"], 1)
                    if s == 1 and T:
                        norm_apply(T, 3, x4, x4, ev["x4_rstd"], ev["n5_ready"])
                    if s == 1 and B:
                        context(B, 1, ev["c1_hi"], ev["sum_hi"], ev["inv_hi"], ev["ctxn_hi"])
                    if s == 3 and B:
                        e.wait_ge(ev["wo_done"], B.n)
                        e.wait_ge(ev["x1res_ready"], B.n)
                        e.tensor_tensor(x2[:, :, :], two(bbank[1]), x1res[:, :, :], ALU.add).then_inc(ev["x2_ready"], 1)
                        e.wait_ge(ev["x2_ready"], B.n)
                        norm_stats(B, 2, x2, ev["x2_stats"], ev["x2_aggr"], ev["x2_var"])
                    if s == 4 and F:
                        e.wait_ge(ev["up_done"], F.n)
                        wait(e, ev["x1_scaled"], F.p)
                        e.tensor_tensor(xa[:, :, :], two(fbank), xN[:, :, :], ALU.add).then_inc(ev["xa_ready"], 1)
                        e.wait_ge(ev["xa_ready"], F.n)
                        norm_stats(F, 0, xa, ev["xa_stats"], ev["xa_aggr"], ev["xa_var"])
                    if s == 4 and T:
                        e.wait_ge(ev["f_ready"], T.n)
                        wait(e, ev["out_ready"], T.p)
                        e.tensor_tensor(t_p[:, :, :], fN[:, :, :], grid_p[:, :, :], ALU.mult).then_inc(ev["p_ready"], 1)
                        edges(T, edge_u, 0, t_u, ev["u_edge"], ev["u_cols"])
                        e.wait_ge(ev["p_ready"], T.n)
                        e.tensor_tensor(t_u[:, :, 1:D - 1], t_p[:, :, 2:D], t_p[:, :, 0:D - 2], ALU.subtract).then_inc(ev["u_inner"], 1)
                    if s == 5 and B:
                        norm_apply(B, 2, n3, x2, ev["x2_rstd"], ev["n3_ready"])
                    if s == 5 and F:
                        norm_apply(F, 0, xa, xa, ev["xa_rstd"], ev["n1_ready"])
                    if s == 6 and T:
                        e.wait_ge(ev["u_inner"], T.n)
                        e.wait_ge(ev["u_cols"], T.n)
                        e.wait_ge(ev["r1_ready"], T.n)
                        e.tensor_tensor(t_u[:, :, :], t_u[:, :, :], t_r1[:, :, :], ALU.add).then_inc(ev["u_ready"], 1)
                    if s == 7 and F:
                        e.wait_ge(ev["y_ready"], F.n)
                        norm_stats(F, 1, yN, ev["y_stats"], ev["y_aggr"], ev["y_var"])
                    if s == 7 and T:
                        e.wait_ge(ev["ga_ready"], T.n)
                        e.wait_ge(ev["gb2_ready"], T.n)
                        wait(e, ev["out_ready"], T.p)
                        edges(T, edge_e, 1, t_e, ev["e_edge"], ev["e_cols"])
                        e.tensor_tensor(t_e[:, :, 1:D - 1], t_a[:, :, 2:D], t_b[:, :, 0:D - 2], ALU.subtract).then_inc(ev["e_inner"], 1)
                        e.wait_ge(ev["gc_ready"], T.n)
                        e.wait_ge(ev["e_inner"], T.n)
                        e.tensor_tensor(t_e[:, :, 1:D - 1], t_e[:, :, 1:D - 1], t_c[:, :, 1:D - 1], ALU.add).then_inc(ev["e_ready"], 1)
                    if s == 8 and F:
                        norm_apply(F, 1, yN, yN, ev["y_rstd"], ev["z_ready"])
                    if s == 9 and T:
                        e.wait_ge(ev["d_done"], T.n)
                        e.wait_ge(ev["e_ready"], T.n)
                        e.wait_ge(ev["e_cols"], T.n)
                        e.tensor_tensor(t_e[:, :, :], two(fbank), t_e[:, :, :], ALU.add).then_inc(ev["w_ready"], 1)
                        e.wait_ge(ev["w_ready"], T.n)
                        e.scalar_tensor_tensor(out=t_e[:, :, :], in0=t_e[:, :, :], scalar=dt[:, bass.ds(T.i, 1)], in1=fN[:, :, :],
                                               op0=ALU.mult, op1=ALU.add).then_inc(ev["w2s_ready"], 1)
                    if s in (11, 12) and F:
                        ready_, hi, lo, b, out = ((ev["qh_ready"], qh, ql, bq, ev["ql_ready"]), (ev["kh_ready"], kh, kl, bk, ev["kl_ready"]))[s - 11]
                        e.wait_ge(ready_, F.n)
                        for m in range(KT):
                            i = e.scalar_tensor_tensor(out=lo[:, m, :], in0=two(fbank)[:, m, :], scalar=b[:, m:m + 1],
                                                       in1=hi[:, m, :].bitcast(F32), op0=ALU.add, op1=ALU.subtract)
                        i.then_inc(out, 1)
                    if s == 12 and B:
                        e.wait_ge(ev["w2_done"], B.n)
                        e.wait_ge(ev["x2b_ready"], B.n)
                        wait(e, ev["x3c_ready"], B.p)
                        e.tensor_tensor(x3[:, :, :], two(bbank[1]), x2b[:, :, :], ALU.add).then_inc(ev["x3_ready"], 1)
                    if s == 10 and B:
                        e.wait_ge(ld_kind, times(B, 48))
                        wait(e, ev["x3c_ready"], B.p)
                        e.tensor_scalar(bcf[:, :], bcr[:, :], kind_ok[:, bass.ds(B.i, 1)], None, ALU.mult).then_inc(ev["bcf_ready"], 1)
                    if s == 16 and B:
                        e.wait_ge(ev["c_done"], B.n)
                        e.wait_ge(ev["x3c_ready"], B.n)
                        wait(e, ev["f_scaled"], B.p)
                        e.scalar_tensor_tensor(out=x4[:, :, :], in0=two(bbank[0]), scalar=kind_ok[:, bass.ds(B.i, 1)], in1=x3c[:, :, :],
                                               op0=ALU.mult, op1=ALU.add).then_inc(ev["x4_ready"], 1)
                    if s == 17 and X:
                        head(e, biased, X, H - 1)
                        e.tensor_scalar(nan2[:, :, :], negmax[:, :, :], 2.0, None, ALU.mult).then_inc(ev["nan_twice"], 1)
                        e.wait_ge(ev["nan_twice"], X.n)
                        e.tensor_tensor(nanz[:, :, :], nan2[:, :, :], nan2[:, :, :], ALU.subtract).then_inc(ev["nan_ready"], 1)

            turns(e, body)

        @block.tensor
        def _(e):
            e.wait_ge(act_set, 2)
            e.wait_ge(ld_set, 16 * LOADS)
            e.wait_ge(pool_set, 3)
            for k in range(KT):
                e.matmul(fbank[0:NB, :], x1T[:, k, 0:NB], ffT[:, 2 * k:2 * k + 2, :], start=(k == 0), stop=False)
            e.matmul(fbank[0:NB, :], ones_row[0:1, 0:NB], xa[0:1, :, :], start=False, stop=True).then_inc(pe_set, 1)
            e.wait_ge(dve_set, 3)
            for k in range(KT):
                e.matmul(bbank[0][:, 0:D], gbT[:, k, 0:P], wo[:, k, :], start=(k == 0), stop=(k == KT - 1))
            for m in range(FM):
                for k in range(KT):
                    i = e.matmul(bbank[1][:, m:m + 1], w1[:, k, m * P:m * P + P], beta2c[:, k:k + 1], start=(k == 0), stop=(k == KT - 1))
            i.then_inc(pe_set, 1)
            e.sem_inc(ready, 2)
            e.wait_ge(ready, 4)

            def turn(dst, src, done):
                for k in range(KT):
                    for q in range(TT):
                        i = e.transpose(dst[:, k * S + q * P:k * S + q * P + P], src[:, q, k * P:k * P + P], ident[:, :])
                i.then_inc(done, 1)

            def project_T(dst, w, c0, xt, n_m, n_k, done):
                for m in range(n_m):
                    for k in range(n_k):
                        i = e.matmul(two(dst)[:, m, :], w[:, k, c0 + m * P:c0 + m * P + P], xt[:, k, :], start=(k == 0), stop=(k == n_k - 1))
                if done is not None:
                    i.then_inc(done, 1)

            def project(dst, xt, w, n_k, done, q0=0, q1=TT):
                for q in range(q0, q1):
                    for k in range(n_k):
                        i = e.matmul(two(dst)[:, q, :], xt[:, k, q * P:q * P + P], w[:, k, :], start=(k == 0), stop=(k == n_k - 1))
                if done is not None:
                    i.then_inc(done, 1)

            def body(t):
                F, X, B, T = phases(e, t)
                if B:
                    kind = e.value_load(ids_ok[0:1, 2, bass.ds(B.i, 1)], min_val=0, max_val=NC2 - 1)
                for s in range(SLOTS):
                    if s < H and X:
                        if s % HM == 0:
                            e.wait_ge(ld_stack[s // HM], times(X, 128))
                        if s == 0:
                            e.wait_ge(ev["mask_ready"], X.n)
                        head(e, biased, X, s - 2)
                        for q in range(TT):
                            e.matmul(two(sbank[s % 2])[:, q, :], qs[:, s, q * P:q * P + P], ks[:, s, :], start=True, stop=False)
                            i = e.matmul(two(sbank[s % 2])[:, q, :], ident_b[:, :], mask_neg[:, q, :], start=False, stop=True)
                        i.then_inc(scored[s % 4], 1)
                    if 1 <= s <= H and X:
                        h = s - 1
                        head(e, expd, X, h)
                        head(e, copied, X, h - 2)
                        for k in range(TT):
                            for q in range(TT):
                                i = e.transpose(tbank[h % 2][:, k * S + q * P:k * S + q * P + P], sc[:, h % NS, q, k * P:k * P + P], ident[:, :])
                        i.then_inc(turned[h % 4], 1)
                    if 2 <= s <= H + 1 and X:
                        h = s - 2
                        head(e, copied, X, h)
                        if h == 0:
                            e.wait_ge(ev["v_ready"], X.n)
                            wait(e, ev["ct_hi"], X.p)
                        if h == HM:
                            e.wait_ge(ev["ct_lo"], X.n)
                        o = VW * (h % 4)
                        for k in range(TT):
                            i = e.matmul(two(cbank)[o:o + VW, h // 4 % 2, :], vp[:, k, h, :], pt[:, h % NP2, k, :],
                                         start=(k == 0), stop=(k == TT - 1))
                        i.then_inc(mixed[h % 4], 1)
                    if s == 0 and X:
                        e.wait_ge(ev["x1T_ready"], X.n)
                        e.wait_ge(ev["kl_ready"], X.n)
                        project(fbank, x1T, wv, KT, ev["v_done"])
                    if s == 0 and B:
                        e.wait_ge(ev["ct_hi"], B.n)
                        for q in range(TT):
                            wait(e, (ev["x4_ready"], ev["gb_ready"])[q], B.p)
                            for g in range(H // 4):
                                i = e.transpose(bbank[q][:, g * P:g * P + P], cts[:, g, q * P:q * P + P], ident[:, :])
                            i.then_inc((ev["c1_lo"], ev["c1_hi"])[q], 1)
                    if s == 1 and F:
                        e.wait_ge(ld_x, times(F, 16))
                        wait(e, ev["v_ready"], F.p)
                        turn(fbank, xN, ev["xT_turned"])
                    if s == 2 and B:
                        e.wait_ge(ev["ctxn_lo"], B.n)
                        e.wait_ge(ev["ctxn_hi"], B.n)
                        turn(bbank[0], ctxN, ev["c2_turned"])
                    if s == 2 and F:
                        e.wait_ge(ev["xT_ready"], F.n)
                        for k in range(KT):
                            i = e.matmul(fbank[0:A, 0:S], downT[:, k, :], xT[:, k, :], start=(k == 0), stop=(k == KT - 1))
                        i.then_inc(ev["down_done"], 1)
                    if s == 3 and B:
                        e.wait_ge(ev["ctxT_ready"], B.n)
                        project(bbank[1], ctxT, wo, KT, ev["wo_done"])
                    if s == 3 and F:
                        e.wait_ge(ev["g0_ready"], F.n)
                        e.wait_ge(ev["wexp_ready"], F.n)
                        hold(e)
                        e.matmul(fbank[0:A, 0:S], wexp[:, 0:A], g0[:, :], start=True, stop=True).then_inc(ev["expert_done"], 1)
                    if s == 4 and F:
                        e.wait_ge(ev["g1_ready"], F.n)
                        for q in range(TT):
                            i = e.matmul(two(fbank)[:, q, :], g1[:, q * P:q * P + P], upT[:, :], start=True, stop=True)
                        i.then_inc(ev["up_done"], 1)
                    if s == 6 and B:
                        e.wait_ge(ev["n3_ready"], B.n)
                        turn(bbank[0], n3, ev["n3_turned"])
                    if s in (7, 8, 9, 10) and B:
                        j = s - 7
                        e.wait_ge((ev["x2_ready"], ev["n3T_ready"], ff_ready[0], ff_ready[1])[j], B.n)
                        if j == 0:
                            e.wait_ge(ev["n3T_ready"], B.n)
                        project_T(bbank[(j + 1) % 2], w1, 2 * j * P, n3T, 2, KT, w1_done[j])
                    if s == 9 and T:
                        e.wait_ge(ev["u_ready"], T.n)
                        e.wait_ge(ev["r2_ready"], T.n)
                        if X:
                            e.wait_ge(ev["v_ready"], X.n)
                        if F:
                            e.wait_ge(ev["xa_ready"], F.n)
                        wait(e, ev["w_ready"], T.p)
                        for q in range(TT):
                            for n, (m, u) in enumerate(((d1T, t_u), (d2T, t_r2))):
                                for k in range(KT):
                                    i = e.matmul(two(fbank)[:, q, :], m[:, k, q * P:q * P + P], u[:, k, :],
                                                 start=(n == 0 and k == 0), stop=(n == 1 and k == KT - 1))
                        i.then_inc(ev["d_done"], 1)
                    if s == 10 and F:
                        e.wait_ge(ev["x1_ready"], F.n)
                        if T:
                            e.wait_ge(ev["w_ready"], T.n)
                        turn(fbank, x1, ev["x1_turned"])
                    if s == 11 and F:
                        e.wait_ge(ev["x1T_ready"], F.n)
                        project_T(fbank, wq, 0, x1T, KT, KT, ev["q_done"])
                    if s == 11 and B:
                        for j in range(4):
                            e.wait_ge(ff_ready[j], B.n)
                        project(bbank[1], ffT, w2, FM, None, 0, 1)
                    if s == 12 and B:
                        project(bbank[1], ffT, w2, FM, ev["w2_done"], 1, 2)
                    if s == 12 and F:
                        e.wait_ge(ev["ql_ready"], F.n)
                        project_T(fbank, wk, 0, x1T, KT, KT, ev["k_done"])
                    if s == 13 and B:
                        e.wait_ge(ev["x3_ready"], B.n)
                        turn(bbank[0], x3, ev["x3_turned"])
                    if s == 14 and B:
                        e.wait_ge(ev["x3T_ready"], B.n)
                        with e.If(kind == 2):
                            for j in range(2):
                                project_T(bbank[(j + 1) % 2], wa, 2 * j * P, x3T, 2, KT, wa_done[j])
                        with e.Else():
                            for j in range(2):
                                e.sem_inc(wa_done[j], 1)
                    if s == 15 and B:
                        e.wait_ge(ld_kind, times(B, 48))
                        for j in range(2):
                            e.wait_ge(ga2_ready[j], B.n)
                        with e.If(kind == 2):
                            project_T(bbank[1], wb, 0, gaT, KT, A2 // P, ev["b_done"])
                        with e.Else():
                            project_T(bbank[1], wb, 0, x3T, KT, KT, ev["b_done"])
                    if s == 16 and B:
                        e.wait_ge(ev["gb_ready"], B.n)
                        project(bbank[0], gbT, wc, KT, ev["c_done"])

            turns(e, body)


def kernel(x, itok_B_0_15, itok_B_34_63, fside_Bx16xSxS_0, itok_B_0_2, condB_dt, mask_Bx1xSxS_bk0, **w):
    import concourse.bacc as bacc
    from concourse.bass_utils import run_bass_kernel_spmd

    def arr(a):
        return np.ascontiguousarray(np.asarray(a))

    c = {k.replace("_cond_", "_"): arr(v) for k, v in w.items()}

    def by_head(a):
        return arr(a.reshape(-1, KT, HM, DH).transpose(0, 1, 3, 2).reshape(a.shape))

    def column(v):
        return v.reshape(-1, P).T

    ins = {
        "x": arr(x), "dom": arr(itok_B_0_15), "step": arr(itok_B_34_63), "kind": arr(itok_B_0_2), "dt": arr(condB_dt),
        "side": arr(fside_Bx16xSxS_0), "mask": arr(mask_Bx1xSxS_bk0).reshape(NB, S, S).view(np.int32),
        "freq": np.exp(np.arange(D // 2, dtype=np.float32) * np.float32(-np.log(10000.0) / (D // 2 - 1))),
        "down_b": c["L0_down_b"], "downT": arr(c["L0_down_W"].T), "upT": arr(c["L0_up_W"].T), "up_b": c["L0_up_b"],
        "expert": np.concatenate([c["L0_expert_W"].transpose(0, 2, 1), c["L0_expert_b"][:, :, None],
                                  c["L0_domain_emb"][:, :, None]], axis=2),
        "gamma0": c["L0_ln_gamma"], "beta0": c["L0_ln_beta"],
        "wq": by_head(c["L1_Wq"]), "wk": by_head(c["L1_Wk"]), "wv": c["L1_Wv"], "wo": c["L1_Wo"],
        "w1": c["L1_W1"], "w2": c["L1_W2"], "w_ada": c["L1_W_ada"], "b_ada": c["L1_b_ada"],
        "b2": c["L1_b2"], "bo": c["L1_bo"],
        "colpack": arr(np.concatenate([column(v) for v in (
            by_head(c["L1_bq"]), by_head(c["L1_bk"]), c["L1_bv"], c["L1_g2"], c["L1_beta2"], c["L1_b1"], c["L2_b1_sr"],
            c["L2_b1_nr"], c["L2_b1_tsr"], c["L2_b2_sr"])], axis=1)),
        "wa": c["L2_w1_sr"],
        "wb": np.concatenate([c["L2_w1_nr"], c["L2_w1_tsr"], c["L2_w2_sr"]]).reshape(4, D, D),
        "wc": np.stack([c["L2_w2_nr"], c["L2_w2_tsr"], c["L2_w3_sr"]]),
        "bc": np.stack([c["L2_b2_nr"], c["L2_b2_tsr"], c["L2_b3_sr"]]),
        "gamma3": c["L2_gamma"], "beta3": c["L2_beta"],
        "d1T": arr(rest_grad(S).T), "d2T": arr(rest_grad2(S).T),
        "grid_A": c["L3_A_grid"], "grid_B": c["L3_B_grid"],
    }
    nc = bacc.Bacc("TRN2", target_bir_lowering=False, num_devices=1)
    d = {n: nc.dram_tensor("in_" + n, a.shape, mybir.dt.from_np(a.dtype), kind="ExternalInput").ap() for n, a in ins.items()}
    d["ada_rows"] = nc.dram_tensor("ada_rows", (NB, 2 * D), F32, kind="Internal").ap()
    d["out"] = nc.dram_tensor("out", (NB, S, D), F32, kind="ExternalOutput").ap()
    build(nc, d)
    return run_bass_kernel_spmd(nc, [{"in_" + n: a for n, a in ins.items()}], core_ids=[0]).results[0]["out"]
```

```python
from contextlib import ExitStack

import numpy as np

import concourse.bass as bass
from concourse import mybir

ALU = mybir.AluOpType
ACT = mybir.ActivationFunctionType
AX_X = mybir.AxisListType.X
F32 = mybir.dt.float32
F32R = mybir.dt.float32r
I32 = mybir.dt.int32
U8 = mybir.dt.uint8

P = 128
NB = 16
S = 256
D = 256
TT = S // P
KT = D // P
H = 16
DH = D // H
HM = H // KT
A = 64
NE = 16
FF = 1024
FM = FF // P
NC2 = 3
NSIDE = 8
A2 = 512
VW = 32
NBLK = 4
LM = 3
LT, LP = 2, 3
ACT_COPIES = (0, 1, 2, 3, 4, 5, 6, 7, 8, 9, 10, 14)
SLOTS = H
EPS = 1e-5
MASKED = -float(2.0 ** 127)
ROUND = float(1.5 * 2 ** 23)
TWO_PI = (6.28125, 0.0019350051879882812, 3.0198672e-07)

EVENTS = """
xT_turned xT_ready down_done g0_ready wexp_ready expert_done g1_ready up_done xa_ready
xa_stats xa_aggr xa_var xa_rstd y_scaled y_ready
y_stats y_aggr y_var y_rstd x1_scaled x1_ready x1_turned x1T_ready
q_done qh_ready ql_ready k_done kh_ready kl_ready mask_ready
v_done v_ready vp_ready res_moved x1res_ready ct_lo ct_hi nan_twice nan_ready
c1_lo c1_hi sum_lo sum_hi inv_lo inv_hi ctxn_lo ctxn_hi c2_turned ctxT_ready wo_done x2_ready
x2_stats x2_aggr x2_var x2_rstd n3_ready x2b_ready n3_turned n3T_ready
w1_done u1_ready th_ready ff_ready w2_done x3_ready bcf_ready x3c_ready x3_turned x3T_ready b_done gb_ready c_done x4_ready
x4_stats x4_aggr x4_var x4_rstd f_scaled f_ready
ga_ready gb2_ready gc_ready r1_ready r2_ready p_ready u_edge u_cols u_inner u_ready
e_edge e_cols e_inner e_ready d_done w_ready w2s_ready out_ready
""".split()


class Sample:

    def __init__(self, e, t, off):
        self.e, self.t, self.off = e, t, off
        self.i = self.keep(t + off)
        self.p = self.i
        self.n = self.keep(t + (off + 1))
        self.h = {k: self.keep(t * 4 + (4 * off + k + 1)) for k in range(-1, 4)}

    def keep(self, v):
        return v if isinstance(v, int) else self.e.snap(v)


def rest_grad(n):
    m = np.zeros((n, n), np.float32)
    for i in range(1, n - 1):
        m[i, i + 1], m[i, i - 1] = 0.5, -0.5
    m[0, :3] = (-1.5, 2.0, -0.5)
    m[n - 1, n - 3:] = (0.5, -2.0, 1.5)
    return m


def rest_grad2(n):
    m = np.zeros((n, n), np.float32)
    for i in range(1, n - 1):
        m[i, i - 1], m[i, i], m[i, i + 1] = 1.0, -2.0, 1.0
    m[0, :4] = (2.0, -5.0, 4.0, -1.0)
    m[n - 1, n - 4:] = (-1.0, 4.0, -5.0, 2.0)
    return m


def build(nc, d):
    with ExitStack() as ctx:
        def sb(name, shape, dt=F32):
            return ctx.enter_context(nc.sbuf_tensor(name, shape, dt))

        def sem(name):
            return ctx.enter_context(nc.semaphore(name))

        ident = sb("ident", [P, P])
        ones_row = sb("ones_row", [1, P])
        downT = sb("downT", [P, KT, A])
        down_b = sb("down_b", [A, 1])
        upT = sb("upT", [A + 1, D])
        wq = sb("wq", [P, KT, D])
        wk = sb("wk", [P, KT, D])
        wv = sb("wv", [P, KT, D])
        wo = sb("wo", [P, KT, D])
        w1 = sb("w1", [P, KT, FF])
        w2 = sb("w2", [P, FM, D])
        wa = sb("wa", [P, KT, A2])
        cols = sb("cols", [P, 64])
        bq, bk, bv = cols[:, 0:2], cols[:, 2:4], cols[:, 4:6]
        g2c, beta2c, b1c, bac, freq = cols[:, 6:8], cols[:, 8:10], cols[:, 10:18], cols[:, 18:22], cols[:, 22:23]
        bbc = cols[:, 24:30].rearrange("p (c m) -> p c m", c=NC2)
        gamma0 = sb("gamma0", [P, D])
        beta0 = sb("beta0", [P, D])
        b2r = sb("b2r", [P, D])
        bo = sb("bo", [P, D])
        gamma3 = sb("gamma3", [P, D])
        beta3 = sb("beta3", [P, D])
        d1T = sb("d1T", [P, KT, S])
        d2T = sb("d2T", [P, KT, S])
        grid_a = sb("grid_a", [P, TT, D])
        grid_b = sb("grid_b", [P, TT, D])
        grid_c = sb("grid_c", [P, TT, D])
        grid_r1 = sb("grid_r1", [P, TT, D])
        grid_r2 = sb("grid_r2", [P, TT, D])
        grid_p = sb("grid_p", [P, TT, D])
        edge_e = sb("edge_e", [P, TT, 2, 4])
        edge_u = sb("edge_u", [P, TT, 2, 4])
        ids = sb("ids", [P, 3, NB], I32)
        idf = sb("idf", [P, 3, NB])
        flags = sb("flags", [P, 8, NB])
        dom_ok, dom_no, kind_ok, dt = flags[:, 0, :], flags[:, 1, :], flags[:, 2, :], flags[:, 3, :]
        ids_ok = sb("ids_ok", [P, 3, NB], I32)
        half_neg = sb("half_neg", [P, TT])
        bsel = sb("bsel", [P, NB, KT])

        xN = sb("xN", [P, TT, D])
        g0 = sb("g0", [A, S])
        g1 = sb("g1", [A + 1, S])
        wexp_raw = sb("wexp_raw", [A, A + 2])
        wexp = sb("wexp", [A, A + 2])
        xa = sb("xa", [P, TT, D])
        yN = xa
        x1 = sb("x1", [P, TT, D])
        x1T = sb("x1T", [P, KT, S])
        xT = sb("xT", [P, KT, S])
        ada = sb("ada", [P, 2, D])
        qh = sb("qh", [P, KT, S], F32R)
        ql = sb("ql", [P, KT, S], F32R)
        kh = sb("kh", [P, KT, S], F32R)
        kl = sb("kl", [P, KT, S], F32R)
        qs = sb("qs", [P, H, S], F32R)
        ks = sb("ks", [P, H, S], F32R)
        mask_raw = sb("mask_raw", [P, TT, S // 4], I32)
        mask_neg = sb("mask_neg", [P, TT, S])
        side = sb("side", [P, NSIDE, TT, S])
        NS, NP2 = 4, 2
        sc = sb("sc", [P, NS, TT, S])
        pt = sb("pt", [P, NP2, TT, S])
        negmax = sb("negmax", [P, TT, H])
        nan2 = sb("nan2", [P, TT, H])
        nanz = sb("nanz", [P, TT, H])
        vp = sb("vp", [P, TT, H, VW])
        cts = sb("cts", [P, H // 4, S])
        rsum = sb("rsum", [P, TT, H])
        rinv = sb("rinv", [P, TT, H])
        x1res = sb("x1res", [P, TT, D])
        x1late = sb("x1late", [P, TT, D])
        vnext = sb("vnext", [P, TT, D])
        n3 = sb("n3", [P, TT, D])
        n3T = sb("n3T", [P, KT, S])
        ctxN, ctxT, x3T = n3, n3T, n3T
        x2 = sb("x2", [P, TT, D])
        x2b = x2
        ffT = sb("ffT", [P, FM, S])
        th = sb("th", [P, 2, 2, S])
        x3 = sb("x3", [P, TT, D])
        x3c = x3
        gaT = ffT[:, 0:A2 // P, :]
        gbT = sb("gbT", [P, KT, S])
        wb = sb("wb", [P, A2 // P, D])
        wc = sb("wc", [P, KT, D])
        bcr = sb("bcr", [P, D])
        bcf = sb("bcf", [P, D])
        x4 = sb("x4", [P, TT, D])
        fN = sb("fN", [P, TT, D])
        t_a = sb("t_a", [P, TT, D])
        t_b = sb("t_b", [P, TT, D])
        t_c = sb("t_c", [P, TT, D])
        t_r1 = sb("t_r1", [P, TT, D])
        t_r2 = sb("t_r2", [P, TT, D])
        t_u = sb("t_u", [P, TT, D])
        t_e = sb("t_e", [P, TT, D])
        t_p = t_e
        edge_t = sb("edge_t", [P, 2, TT, 2, 4])
        outN = t_r1
        stats = sb("stats", [P, 4, TT, 6])
        mv = sb("mv", [P, 4, TT, 2])
        var = sb("var", [P, 4, TT])
        rstd = sb("rstd", [P, 4, TT])

        def bank(name):
            return ctx.enter_context(nc.psum_tensor(name, [P, 512], F32))

        sbank = [bank("score_bank0"), bank("score_bank1")]
        tbank = [bank("turn_bank0"), bank("turn_bank1")]
        cbank = bank("context_bank")
        fbank = bank("front_bank")
        bbank = [bank("back_bank0"), bank("back_bank1")]

        def two(b):
            return b[:, :].rearrange("p (a x) -> p a x", a=2)

        ev = {n: sem(n) for n in EVENTS}
        masked = [sem(f"masked{h}") for h in range(4)]
        scored = [sem(f"scored{h}") for h in range(4)]
        biased = [sem(f"biased{h}") for h in range(4)]
        expd = [sem(f"expd{h}") for h in range(4)]
        turned = [sem(f"turned{h}") for h in range(4)]
        copied = [sem(f"copied{h}") for h in range(4)]
        mixed = [sem(f"mixed{h}") for h in range(4)]
        wa_done = [sem(f"wa_done{j}") for j in range(2)]
        ga2_ready = [sem(f"ga2_ready{j}") for j in range(2)]
        ld_x, ld_mask, ld_exp, ld_ada, ld_kind = sem("ld_x"), sem("ld_mask"), sem("ld_exp"), sem("ld_ada"), sem("ld_kind")
        ld_side = [sem(f"ld_side{c}") for c in range(4)]
        ld_stack = [sem(f"ld_stack{m}") for m in range(KT)]
        stored = sem("stored")
        wexp_half = sem("wexp_half")
        passed = {k: sem(f"passed_{n}") for k, n in ((nc.vector.engine, "dve"), (nc.tensor.engine, "pe"), (nc.gpsimd.engine, "pool"))}
        ld_set, ld_ids, st_ada = sem("ld_set"), sem("ld_ids"), sem("st_ada")
        pool_set, dve_set, act_set, pe_set, idx_ready, ready = (
            sem("pool_set"), sem("dve_set"), sem("act_set"), sem("pe_set"), sem("idx_ready"), sem("ready"))
        sem_dve = sem("sem_dve")

        block = ctx.enter_context(nc.Block())

        def wait(e, s, n):
            if not (isinstance(n, int) and n <= 0):
                e.wait_ge(s, n)

        def phase(e, t, off):
            if isinstance(t, int) and not 0 <= t + off < NB:
                return None
            return Sample(e, t, off)

        def hold(e):
            e.sem_inc(passed[e.engine], 1)

        def quarter(e, s, x, j):
            e.wait_ge(ev[s], x.h[j])

        def times(x, k, prev=False):
            return x.keep((x.t + x.off + (0 if prev else 1)) * k)

        def head(e, s, x, h):
            wait(e, s[h % 4], x.h[h // 4])

        def turns(e, body):
            for t in range(-2, 4):
                body(t)
            with e.Fori(4, NB - 2) as t:
                body(t)
            for t in range(NB - 2, NB + 3):
                body(t)

        def lagging(x, before, h):
            x, h = (x, h) if h >= 0 else (before, h + H)
            return [(x, h)] if x else []

        def phases(e, t):
            return phase(e, t, 2), phase(e, t, 1), phase(e, t, 0), phase(e, t, -1), phase(e, t, -2), phase(e, t, -3)

        LOADS = 29

        @block.sync
        def _(e):
            for k in range(3):
                e.dma_start(ids[:, k, :], d[("dom", "step", "kind")[k]].partition_broadcast(P)).then_inc(ld_ids, 16)
            e.dma_start(dt, d["dt"].partition_broadcast(P)).then_inc(ld_ids, 16)
            n = 0
            for dst, src in (
                (freq, d["freq"].rearrange("(p a) -> p a", a=1)),
                (down_b[:, :], d["down_b"].rearrange("(p a) -> p a", a=1)),
                (downT[:, :, :], d["downT"].rearrange("(k p) a -> p k a", p=P)),
                (upT[0:A, :], d["upT"]),
                (upT[A:A + 1, :], d["up_b"].rearrange("(a n) -> a n", a=1)),
                (wq[:, :, :], d["wq"].rearrange("(k p) n -> p k n", p=P)),
                (wk[:, :, :], d["wk"].rearrange("(k p) n -> p k n", p=P)),
                (wv[:, :, :], d["wv"].rearrange("(k p) n -> p k n", p=P)),
                (wo[:, :, :], d["wo"].rearrange("(k p) n -> p k n", p=P)),
                (w1[:, :, :], d["w1"].rearrange("(k p) n -> p k n", p=P)),
                (w2[:, :, :], d["w2"].rearrange("(k p) n -> p k n", p=P)),
                (wa[:, :, :], d["wa"].rearrange("(k p) n -> p k n", p=P)),
                (cols[:, 0:22], d["colpack"][:, 0:22]),
                (cols[:, 24:30], d["colpack"][:, 22:28]),
                (gamma0[:, :], d["gamma0"].partition_broadcast(P)),
                (beta0[:, :], d["beta0"].partition_broadcast(P)),
                (b2r[:, :], d["b2"].partition_broadcast(P)),
                (bo[:, :], d["bo"].partition_broadcast(P)),
                (gamma3[:, :], d["gamma3"].partition_broadcast(P)),
                (beta3[:, :], d["beta3"].partition_broadcast(P)),
                (d1T[:, :, :], d["d1T"].rearrange("(k p) n -> p k n", p=P)),
                (d2T[:, :, :], d["d2T"].rearrange("(k p) n -> p k n", p=P)),
                (x2[:, :, :], d["grid_A"][0].rearrange("(t p) n -> p t n", p=P)),
                (x3[:, :, :], d["grid_A"][1].rearrange("(t p) n -> p t n", p=P)),
                (t_a[:, :, :], d["grid_B"][0].rearrange("(t p) n -> p t n", p=P)),
                (t_b[:, :, :], d["grid_B"][1].rearrange("(t p) n -> p t n", p=P)),
                (t_c[:, :, :], d["grid_B"][2].rearrange("(t p) n -> p t n", p=P)),
                (ffT[:, 0:4, :], d["w_ada"].rearrange("(k p) n -> p k n", p=P)),
                (xa[0:1, :, :], d["b_ada"].rearrange("(a k n) -> a k n", a=1, k=2)),
            ):
                e.dma_start(dst, src).then_inc(ld_set, 16)
                n += 1
            assert n == LOADS
            e.wait_ge(dve_set, 2)
            e.dma_start(d["ada_rows"], x3T[0:NB, :, :]).then_inc(st_ada, 16)
            e.wait_ge(idx_ready, 1)
            e.wait_ge(st_ada, 16)
            e.wait_ge(ready, 4)

            def load_side(x, c):
                e.dma_start(side[:, 4 * c % NSIDE:4 * c % NSIDE + 4, :, :],
                            d["side"][bass.ds(x.i, 1), 4 * c:4 * c + 4].rearrange("b h (t p) k -> p (b h) t k", p=P)
                            ).then_inc(ld_side[c], 16)

            def stack(x, prev, m):
                if prev is not None:
                    head(e, scored, prev, HM * m + HM - 1)
                for b in range(NBLK):
                    for dst, hi, lo, low in ((qs, qh, ql, b >= 2), (ks, kh, kl, b % 2 == 1)):
                        src = lo if low else hi
                        e.dma_start(dst[DH * b:DH * b + DH, HM * m:HM * m + HM, :].bitcast(F32), src[:, m, :].bitcast(F32)).then_inc(ld_stack[m], 16)

            def body(t):
                G, F, X, B, T, U = phases(e, t)
                for s in range(SLOTS):
                    if s == 0 and G:
                        wait(e, ev["xa_ready"], G.p)
                        e.dma_start(xN[:, :, :], d["x"][bass.ds(G.i, 1)].rearrange("b (t p) n -> p (b t) n", p=P)).then_inc(ld_x, 16)
                        wait(e, ev["wexp_ready"], G.p)
                        dom = e.value_load(ids_ok[0:1, 0, bass.ds(G.i, 1)], min_val=0, max_val=NE - 1)
                        e.dma_start(wexp_raw[:, :], d["expert"][bass.ds(dom, 1)].rearrange("e a n -> (e a) n")).then_inc(ld_exp, 16)
                    if s == 2 and G:
                        wait(e, ev["x1_ready"], G.p)
                        e.dma_start(ada[:, :, :].rearrange("p a n -> p (a n)"), d["ada_rows"][bass.ds(G.i, 1)].rearrange("b n -> (b n)").partition_broadcast(P)).then_inc(ld_ada, 16)
                    if s == 0 and F:
                        wait(e, ev["mask_ready"], F.p)
                        e.dma_start(mask_raw[:, :, :], d["mask"][bass.ds(F.i, 1)].rearrange("b (t p) n -> p (b t) n", p=P)).then_inc(ld_mask, 16)
                        if isinstance(t, int) and t == -1:
                            for c in range(2):
                                load_side(F, c)
                    if s == 5 and B:
                        kind = e.value_load(ids_ok[0:1, 2, bass.ds(B.i, 1)], min_val=0, max_val=NC2 - 1)
                        wait(e, ev["b_done"], B.p)
                        e.dma_start(wb[:, :, :], d["wb"][bass.ds(kind, 2)].rearrange("c (k p) n -> p (c k) n", p=P)).then_inc(ld_kind, 16)
                    if s == 6 and B:
                        wait(e, ev["c_done"], B.p)
                        e.dma_start(wc[:, :, :], d["wc"][bass.ds(kind, 1)].rearrange("c (k p) n -> p (c k) n", p=P)).then_inc(ld_kind, 16)
                        wait(e, ev["bcf_ready"], B.p)
                        e.dma_start(bcr[:, :], d["bc"][bass.ds(kind, 1)].rearrange("c n -> (c n)").partition_broadcast(P)).then_inc(ld_kind, 16)
                    if s % 4 == 0 and X and (s < 12 or F):
                        c = s // 4
                        head(e, biased, X, 4 * c - 1)
                        if not (isinstance(t, int) and t == 0 and s == 0):
                            load_side(X if c < 3 else F, (c + 1) % 4)
                    if s == 5 and U:
                        e.wait_ge(ev["out_ready"], U.n)
                        e.dma_start(d["out"][bass.ds(U.i, 1)].rearrange("b (t p) n -> p (b t) n", p=P), outN[:, :, :]).then_inc(stored, 16)
                    if s == 8 and F:
                        e.wait_ge(ev["ql_ready"], F.n)
                        e.wait_ge(ev["kl_ready"], F.n)
                        stack(F, X, 0)
                    if s == 0 and X:
                        stack(X, B, 1)

            turns(e, body)
            e.wait_ge(stored, 16 * NB)

        @block.gpsimd
        def _(e):
            e.memset(ident[:, :], 0.0).then_inc(pool_set, 1)
            e.memset(half_neg[:, :], -0.5)
            e.memset(ones_row[:, :], 1.0)
            e.memset(g1[:, :], 1.0)
            e.memset(vp[:, :, :, :], 0.0).then_inc(pool_set, 1)
            e.wait_ge(pool_set, 2)
            e.memset(vp[:, :, :, DH:DH + 1], 1.0)
            e.affine_select(out=ident[:, :], in_=ident[:, :], compare_op=ALU.not_equal, fill=1.0,
                            base=0, pattern=[[-1, P]], channel_multiplier=1).then_inc(pool_set, 1)
            e.wait_ge(pool_set, 3)
            e.sem_inc(ready, 1)
            e.wait_ge(ready, 4)

            def power(x, k, var_ev, rstd_ev):
                e.wait_ge(var_ev, x.n)
                e.tensor_tensor(rstd[:, k, :], var[:, k, :], half_neg[:, :], ALU.pow).then_inc(rstd_ev, 1)

            def rows(r):
                return r.unsqueeze(1).broadcast_to([P, TT, D])

            def mask_bias(x, h):
                if h % 4 == 0:
                    e.wait_ge(ld_side[h // 4], times(x, 16))
                v = side[:, h % NSIDE, :, :]
                e.tensor_tensor(v, v, mask_neg[:, :, :], ALU.add).then_inc(masked[h % 4], 1)

            def body(t):
                G, F, X, B, T, U = phases(e, t)
                for s in range(SLOTS):
                    ahead = s + LM
                    if X and ahead < H:
                        mask_bias(X, ahead)
                    if F and ahead == H:
                        head(e, masked, F, -1)
                        e.wait_ge(ld_mask, times(F, 16))
                        hold(e)
                        e.tensor_scalar(mask_neg[:, :, :], mask_raw[:, :, :].bitcast(U8), MASKED, None, ALU.mult).then_inc(ev["mask_ready"], 1)
                        e.wait_ge(ev["mask_ready"], F.n)
                    if F and ahead >= H:
                        mask_bias(F, ahead - H)
                    for at, x, k, n in ((13, G, 0, "xa"), (5, T, 3, "x4"), (0, F, 1, "y"), (8, B, 2, "x2")):
                        if s == at and x:
                            power(x, k, ev[n + "_var"], ev[n + "_rstd"])
                    if s == 12 and F:
                        wait(e, ev["res_moved"], F.p)
                        e.wait_ge(ev["x1_ready"], F.n)
                        e.tensor_tensor(x1res[:, :, :], x1[:, :, :], rows(bo[:, :]), ALU.add).then_inc(ev["x1res_ready"], 1)
                    if s == 7 and T:
                        e.wait_ge(ev["f_ready"], T.n)
                        wait(e, stored, times(T, 16, prev=True))
                        e.tensor_tensor(t_r1[:, :, :], fN[:, :, :], grid_r1[:, :, :], ALU.mult).then_inc(ev["r1_ready"], 1)
                        e.tensor_tensor(t_r2[:, :, :], fN[:, :, :], grid_r2[:, :, :], ALU.mult).then_inc(ev["r2_ready"], 1)
                    if s == 9 and T:
                        e.tensor_tensor(t_a[:, :, :], fN[:, :, :], grid_a[:, :, :], ALU.mult).then_inc(ev["ga_ready"], 1)
                    if s == 10 and B:
                        e.wait_ge(ev["n3_ready"], B.n)
                        e.tensor_tensor(x2b[:, :, :], x2[:, :, :], rows(b2r[:, :]), ALU.add).then_inc(ev["x2b_ready"], 1)
                    if s == 10 and T:
                        e.tensor_tensor(t_b[:, :, :], fN[:, :, :], grid_b[:, :, :], ALU.mult).then_inc(ev["gb2_ready"], 1)
                    if s == 11 and T:
                        e.tensor_tensor(t_c[:, :, :], fN[:, :, :], grid_c[:, :, :], ALU.mult).then_inc(ev["gc_ready"], 1)
                    if s == 3 and T:
                        e.wait_ge(ev["bcf_ready"], T.n)
                        e.wait_ge(ev["x3_turned"], T.n)
                        e.tensor_tensor(x3c[:, :, :], x3[:, :, :], rows(bcf[:, :]), ALU.add).then_inc(ev["x3c_ready"], 1)

            turns(e, body)

        @block.scalar
        def _(e):
            e.wait_ge(dve_set, 1)
            e.activation(x1T[:, :, 0:NB], x1T[:, :, 0:NB], ACT.Sin).then_inc(act_set, 1)
            e.wait_ge(act_set, 1)
            e.activation(x1T[:, :, 0:NB], x1T[:, :, 0:NB], ACT.Silu).then_inc(act_set, 1)
            e.wait_ge(ready, 4)

            def copy_turned(x, h):
                head(e, turned, x, h)
                head(e, mixed, x, h - NP2)
                e.activation(pt[:, h % NP2, :, :], two(tbank[h % 2]), ACT.Copy).then_inc(copied[h % 4], 1)

            def body(t):
                G, F, X, B, T, U = phases(e, t)
                if T:
                    kind = e.value_load(ids_ok[0:1, 2, bass.ds(T.i, 1)], min_val=0, max_val=NC2 - 1)
                for s in range(SLOTS):
                    for x, h in lagging(X, B, s - 1):
                        head(e, biased, x, h)
                        for q in range(TT):
                            i = e.activation(sc[:, h % NS, q, :], sc[:, h % NS, q, :], ACT.Exp,
                                             bias=negmax[:, q, h:h + 1], scale=-1.0)
                        i.then_inc(expd[h % 4], 1)
                    for x, h in lagging(X, B, s - LT):
                        if s in ACT_COPIES:
                            copy_turned(x, h)
                    if s == 2 and B:
                        head(e, mixed, B, H - 1)
                        e.activation(cts[:, 2:4, :], two(cbank), ACT.Copy).then_inc(ev["ct_hi"], 1)
                    if s == 2 and X:
                        head(e, mixed, X, -1)
                        e.wait_ge(ev["v_ready"], X.n)
                        e.activation(vp[:, :, :, 0:DH], vnext[:, :, :].rearrange("p t (h c) -> p t h c", h=H), ACT.Copy).then_inc(ev["vp_ready"], 1)
                    if s == 9 and F:
                        e.wait_ge(ev["v_done"], F.n)
                        wait(e, ev["vp_ready"], F.p)
                        e.activation(vnext[:, :, :], two(fbank), ACT.Copy).then_inc(ev["v_ready"], 1)
                    if s == 2 and T:
                        e.wait_ge(ev["x3_turned"], T.n)
                        wait(e, ev["b_done"], T.p)
                        e.activation(x3T[:, :, :], two(bbank[0]), ACT.Copy).then_inc(ev["x3T_ready"], 1)
                    if s == 3 and T:
                        with e.If(kind == 2):
                            for j in range(2):
                                e.wait_ge(wa_done[j], T.n)
                                for m in range(2):
                                    i = e.activation(gaT[:, 2 * j + m, :], two(bbank[(j + 1) % 2])[:, m, :], ACT.Gelu,
                                                     bias=bac[:, 2 * j + m:2 * j + m + 1])
                                i.then_inc(ga2_ready[j], 1)
                        with e.Else():
                            for j in range(2):
                                e.sem_inc(ga2_ready[j], 1)
                    if s == 4 and T:
                        e.wait_ge(ev["b_done"], T.n)
                        wait(e, ev["c_done"], T.p)
                        for m in range(KT):
                            i = e.activation(gbT[:, m, :], two(bbank[1])[:, m, :], ACT.Gelu, bias=bsel[:, bass.ds(T.i, 1), m])
                        i.then_inc(ev["gb_ready"], 1)
                    if s == 7 and B:
                        e.wait_ge(ev["c2_turned"], B.n)
                        wait(e, ev["wo_done"], B.p)
                        e.activation(ctxT[:, :, :], two(bbank[0]), ACT.Copy).then_inc(ev["ctxT_ready"], 1)
                    if s == 10 and B:
                        e.wait_ge(ev["n3_turned"], B.n)
                        wait(e, ev["w1_done"], B.h[-1])
                        e.activation(n3T[:, :, :], two(bbank[0]), ACT.Copy).then_inc(ev["n3T_ready"], 1)
                    if s in (12, 13, 14, 15) and B:
                        j = s - 12
                        quarter(e, "w1_done", B, j)
                        wait(e, ev["w2_done"], B.p)
                        for m in range(2 * j, 2 * j + 2):
                            i = e.activation(ffT[:, m, :], two(bbank[(j + 1) % 2])[:, m % 2, :], ACT.Identity, bias=b1c[:, m:m + 1])
                        i.then_inc(ev["u1_ready"], 1)
                        quarter(e, "u1_ready", B, j)
                        if j >= 2:
                            quarter(e, "ff_ready", B, j - 2)
                        e.activation(th[:, j % 2, :, :], ffT[:, 2 * j:2 * j + 2, :], ACT.Tanh, scale=0.851).then_inc(ev["th_ready"], 1)
                    if s == 5 and F:
                        e.wait_ge(ev["x1_turned"], F.n)
                        wait(e, ev["v_done"], F.p)
                        e.activation(x1T[:, :, :], two(fbank), ACT.Copy).then_inc(ev["x1T_ready"], 1)
                    if s in (6, 7) and F:
                        done, hi, b, out = ((ev["q_done"], qh, bq, ev["qh_ready"]), (ev["k_done"], kh, bk, ev["kh_ready"]))[s - 6]
                        e.wait_ge(done, F.n)
                        for m in range(KT):
                            wait(e, ld_stack[m], times(F, 128, prev=True))
                        for m in range(KT):
                            i = e.activation(hi[:, m, :], two(fbank)[:, m, :], ACT.Identity, bias=b[:, m:m + 1])
                        i.then_inc(out, 1)
                    if s == 4 and U:
                        e.wait_ge(ev["w2s_ready"], U.n)
                        e.activation(outN[:, :, :], t_e[:, :, :], ACT.Relu).then_inc(ev["out_ready"], 1)
                    if s == 10 and X:
                        head(e, mixed, X, HM - 1)
                        wait(e, ev["c1_hi"], X.p)
                        e.activation(cts[:, 0:2, :], two(cbank), ACT.Copy).then_inc(ev["ct_lo"], 1)
                    if s == 10 and G:
                        e.wait_ge(ev["xT_turned"], G.n)
                        wait(e, ev["down_done"], G.p)
                        e.activation(xT[:, :, :], two(fbank), ACT.Copy).then_inc(ev["xT_ready"], 1)
                    if s == 11 and G:
                        e.wait_ge(ev["down_done"], G.n)
                        wait(e, ev["expert_done"], G.p)
                        e.activation(g0[:, :], fbank[0:A, 0:S], ACT.Gelu, bias=down_b[:, 0:1]).then_inc(ev["g0_ready"], 1)
                    if s == 12 and G:
                        e.wait_ge(ev["expert_done"], G.n)
                        e.wait_ge(ev["wexp_ready"], G.n)
                        wait(e, ev["up_done"], G.p)
                        e.activation(g1[0:A, :], fbank[0:A, 0:S], ACT.Identity, bias=wexp[:, A:A + 1]).then_inc(ev["g1_ready"], 1)
                    if s == 9 and X:
                        if B:
                            e.wait_ge(ev["x2_ready"], B.n)
                        e.wait_ge(ev["x1res_ready"], X.n)
                        e.activation(x1late[:, :, :], x1res[:, :, :], ACT.Copy).then_inc(ev["res_moved"], 1)

            turns(e, body)

        @block.vector
        def _(e):
            chain = [0]
            own = sem_dve

            def link(i):
                chain[0] += 1
                i.then_inc(own, 1)
                e.wait_ge(own, chain[0])

            e.memset(qs[64:128, :, :].bitcast(F32), 0.0)
            link(e.memset(ks[64:128, :, :].bitcast(F32), 0.0))
            e.wait_ge(ld_ids, 64)
            link(e.tensor_copy(idf[:, :, :], ids[:, :, :]))
            e.tensor_scalar(flags[:, 4, :], idf[:, 0, :], 0.0, None, ALU.is_ge)
            e.tensor_scalar(flags[:, 5, :], idf[:, 0, :], float(NE), None, ALU.is_lt)
            e.tensor_scalar(flags[:, 6, :], idf[:, 2, :], 0.0, None, ALU.is_ge)
            link(e.tensor_scalar(flags[:, 7, :], idf[:, 2, :], float(NC2), None, ALU.is_lt))
            e.tensor_tensor(dom_ok, flags[:, 4, :], flags[:, 5, :], ALU.mult)
            link(e.tensor_tensor(kind_ok, flags[:, 6, :], flags[:, 7, :], ALU.mult))
            e.tensor_scalar(dom_no, dom_ok, -1.0, 1.0, ALU.mult, ALU.add)
            e.tensor_scalar(ids_ok[:, 0, :], idf[:, 0, :], 0.0, float(NE - 1), ALU.max, ALU.min)
            e.tensor_copy(ids_ok[:, 1, :], idf[:, 1, :])
            link(e.tensor_scalar(ids_ok[:, 2, :], idf[:, 2, :], 0.0, float(NC2 - 1), ALU.max, ALU.min))
            e.sem_inc(idx_ready, 1)
            e.wait_ge(ld_set, 16 * LOADS)
            ang, turn, red = x1T[:, 0, 32:48], x1T[:, 0, 48:64], x1T[:, 0, 64:80]
            link(e.tensor_scalar(turn, idf[:, 1, :], 40.0, None, ALU.mult))
            link(e.tensor_scalar(ang, turn, freq, None, ALU.mult))
            for k in range(2):
                link(e.tensor_scalar(turn, ang, 1.0 / (2 * np.pi), 0.25 * k, ALU.mult, ALU.add))
                link(e.tensor_scalar(turn, turn, ROUND, None, ALU.add))
                link(e.tensor_scalar(turn, turn, -ROUND, None, ALU.add))
                link(e.scalar_tensor_tensor(out=red, in0=turn, scalar=-TWO_PI[0], in1=ang, op0=ALU.mult, op1=ALU.add))
                link(e.scalar_tensor_tensor(out=red, in0=turn, scalar=-TWO_PI[1], in1=red, op0=ALU.mult, op1=ALU.add))
                link(e.scalar_tensor_tensor(out=red, in0=turn, scalar=-TWO_PI[2], in1=red, op0=ALU.mult, op1=ALU.add))
                link(e.tensor_scalar(red, red, float(np.pi / 2) * k, None, ALU.add))
                i = e.tensor_scalar(x1T[:, k, 0:NB], red, -3.1415925, 3.1415925, ALU.max, ALU.min)
                link(i)
            e.sem_inc(dve_set, 1)
            e.wait_ge(pe_set, 1)
            i = e.tensor_scalar(x3T[0:NB, 0, :], fbank[0:NB, 0:D], 1.0, None, ALU.add)
            link(i)
            link(e.tensor_copy(x3T[0:NB, 1, :], fbank[0:NB, D:2 * D]))
            e.sem_inc(dve_set, 1)
            e.tensor_scalar(wq[:, :, :], wq[:, :, :], DH ** -0.5, None, ALU.mult)
            link(e.tensor_scalar(bq, bq, DH ** -0.5, None, ALU.mult))
            ones = n3[:, 0, 0:P]
            link(e.memset(n3[:, 0, 0:P], 1.0))
            for k in range(KT):
                i = e.tensor_scalar(gbT[:, k, 0:P], ones, bv[:, k:k + 1], None, ALU.mult)
            link(i)
            e.sem_inc(dve_set, 1)
            e.wait_ge(pe_set, 2)
            link(e.tensor_tensor(bo[:, :], bbank[0][:, 0:D], bo[:, :], ALU.add))
            link(e.tensor_tensor(b1c, bbank[1][:, 0:FM], b1c, ALU.add))
            for k in range(KT):
                i = e.tensor_scalar(w1[:, k, :], w1[:, k, :], g2c[:, k:k + 1], None, ALU.mult)
            e.tensor_scalar(w2[:, :, :], w2[:, :, :], 0.5, None, ALU.mult)
            link(i)
            link(e.memset(bsel[:, :, :], 0.0))
            for c in range(NC2):
                link(e.tensor_scalar(flags[:, 4, :], idf[:, 2, :], float(c), None, ALU.is_equal))
                for m in range(KT):
                    link(e.scalar_tensor_tensor(out=bsel[:, :, m], in0=flags[:, 4, :], scalar=bbc[:, c, m:m + 1],
                                                in1=bsel[:, :, m], op0=ALU.mult, op1=ALU.add))
            A0, A1, B0, B1, B2 = x2, x3, t_a, t_b, t_c
            e.tensor_scalar(grid_r1[:, :, :], A0[:, :, :], -1.0, None, ALU.mult)
            e.tensor_scalar(grid_r2[:, :, :], B0[:, :, :], 0.5, None, ALU.mult)
            e.tensor_scalar(grid_p[:, :, :], B2[:, :, :], 0.5, None, ALU.mult)
            link(e.tensor_scalar(grid_c[:, :, :], B1[:, :, :], -1.0, None, ALU.mult))
            e.tensor_tensor(grid_a[:, :, :], B1[:, :, :], A1[:, :, :], ALU.subtract)
            link(e.tensor_tensor(grid_b[:, :, :], B1[:, :, :], A1[:, :, :], ALU.add))
            e.tensor_scalar(grid_a[:, :, :], grid_a[:, :, :], 0.5, None, ALU.mult)
            link(e.tensor_scalar(grid_b[:, :, :], grid_b[:, :, :], -0.5, None, ALU.mult))
            link(e.memset(edge_u[:, :, :, :], 0.0))
            for side_, cs in ((0, (0, 1, 2, 3)), (1, (3, 2, 1, 0))):
                sign = 1.0 if side_ == 0 else -1.0
                for k, (ca, cb, cu) in enumerate(((1.5, 1.0, -1.5), (-2.0, -2.5, 2.0), (0.5, 2.0, -0.5), (0.0, -0.5, 0.0))):
                    j = cs[k] if side_ == 0 else D - 4 + cs[k]
                    e.tensor_scalar(edge_u[:, :, side_, cs[k]], B2[:, :, j], sign * cu, None, ALU.mult)
                    link(e.tensor_scalar(edge_e[:, :, side_, cs[k]], B1[:, :, j], cb, None, ALU.mult))
                    link(e.scalar_tensor_tensor(out=edge_e[:, :, side_, cs[k]], in0=A1[:, :, j], scalar=sign * ca,
                                                in1=edge_e[:, :, side_, cs[k]], op0=ALU.mult, op1=ALU.add))
            e.sem_inc(ready, 1)
            e.wait_ge(ready, 4)

            def norm_stats(x, k, src, s_ev, a_ev, v_ev):
                for q in range(TT):
                    i = e.bn_stats(stats[:, k, q, :], src[:, q, :])
                i.then_inc(s_ev, 1)
                e.wait_ge(s_ev, x.n)
                hold(e)
                for q in range(TT):
                    i = e.bn_aggr(mv[:, k, q, :], stats[:, k, q, :])
                i.then_inc(a_ev, 1)
                e.wait_ge(a_ev, x.n)
                e.tensor_scalar(var[:, k, :], mv[:, k, :, 1], EPS, None, ALU.add).then_inc(v_ev, 1)

            def norm_apply(x, k, dst, src, r_ev, o_ev):
                e.wait_ge(r_ev, x.n)
                for q in range(TT):
                    i = e.tensor_scalar(dst[:, q, :], src[:, q, :], mv[:, k, q, 0:1], rstd[:, k, q:q + 1], ALU.subtract, ALU.mult)
                i.then_inc(o_ev, 1)

            def norm_affine(x, k, dst, src, gain, offset, r_ev, s_ev, o_ev):
                e.wait_ge(r_ev, x.n)
                for q in range(TT):
                    i = e.scalar_tensor_tensor(out=src[:, q, :], in0=src[:, q, :], scalar=mv[:, k, q, 0:1], in1=gain,
                                               op0=ALU.subtract, op1=ALU.mult)
                i.then_inc(s_ev, 1)
                e.wait_ge(s_ev, x.n)
                for q in range(TT):
                    i = e.scalar_tensor_tensor(out=dst[:, q, :], in0=src[:, q, :], scalar=rstd[:, k, q:q + 1], in1=offset,
                                               op0=ALU.mult, op1=ALU.add)
                i.then_inc(o_ev, 1)

            def context(x, u, c1, s_ev, i_ev, o_ev):
                e.wait_ge(c1, x.n)
                v = bbank[1 - u][:, :].rearrange("p (q h c) -> p q h c", q=TT, h=HM)
                hs = slice(HM * u, HM * u + HM)
                if u == 0:
                    e.wait_ge(ev["nan_ready"], x.n)
                e.tensor_tensor(rsum[:, :, hs], v[:, :, :, DH], nanz[:, :, hs], ALU.add).then_inc(s_ev, 1)
                e.wait_ge(s_ev, x.n)
                e.reciprocal(rinv[:, :, hs], rsum[:, :, hs]).then_inc(i_ev, 1)
                e.wait_ge(i_ev, x.n)
                for q in range(TT):
                    i = e.tensor_tensor(ctxN[:, q, u * P:u * P + P].rearrange("p (h c) -> p h c", h=HM), v[:, q, :, 0:DH],
                                        rinv[:, q, hs].unsqueeze(2).broadcast_to([P, HM, DH]), ALU.mult)
                i.then_inc(o_ev, 1)

            def edges(x, grid, k, dst, t_ev, c_ev):
                near = bass.AP(fN, 0, [[TT * D, P], [D, TT], [D - 4, 2], [1, 4]])
                e.tensor_tensor(edge_t[:, k, :, :, :], near, grid[:, :, :, :], ALU.mult).then_inc(t_ev, 1)
                e.wait_ge(t_ev, x.n)
                e.tensor_reduce(bass.AP(dst, 0, [[TT * D, P], [D, TT], [D - 1, 2]]), edge_t[:, k, :, :, :], AX_X, ALU.add).then_inc(c_ev, 1)

            def body(t):
                G, F, X, B, T, U = phases(e, t)
                for s in range(SLOTS):
                    if X:
                        head(e, scored, X, s)
                        e.wait_ge(ld_side[s // 4], times(X, 16))
                        head(e, masked, X, s)
                        head(e, turned, X, s - NS)
                        if s == 0:
                            wait(e, ev["nan_ready"], X.p)
                        hold(e)
                        for q in range(TT):
                            i = e.tensor_tensor_reduce(sc[:, s % NS, q, :], two(sbank[s % 2])[:, q, :], side[:, s % NSIDE, q, :],
                                                       -1.0, 3.4e38, ALU.add, ALU.min, negmax[:, q, s:s + 1])
                        i.then_inc(biased[s % 4], 1)
                    for x, h in lagging(X, B, s - LT):
                        if s not in ACT_COPIES:
                            head(e, turned, x, h)
                            head(e, mixed, x, h - NP2)
                            e.tensor_copy(pt[:, h % NP2, :, :], two(tbank[h % 2])).then_inc(copied[h % 4], 1)
                    if s in (12, 13, 14, 15) and B:
                        j = s - 12
                        quarter(e, "th_ready", B, j)
                        f = ffT[:, 2 * j:2 * j + 2, :]
                        e.scalar_tensor_tensor(out=f, in0=th[:, j % 2, :, :], scalar=1.0, in1=f,
                                               op0=ALU.add, op1=ALU.mult).then_inc(ev["ff_ready"], 1)
                    if s == 4 and G:
                        e.wait_ge(ld_exp, times(G, 16))
                        wait(e, ev["expert_done"], G.p)
                        wait(e, ev["g1_ready"], G.p)
                        e.tensor_scalar(wexp[:, 0:A], ident[0:A, 0:A], dom_no[0:A, bass.ds(G.i, 1)], None, ALU.mult)
                        e.tensor_scalar(wexp[:, A:A + 1], wexp_raw[:, A + 1:A + 2], 1.0, None, ALU.mult).then_inc(wexp_half, 1)
                        e.wait_ge(wexp_half, G.n)
                        e.scalar_tensor_tensor(out=wexp[:, 0:A + 1], in0=wexp_raw[:, 0:A + 1], scalar=dom_ok[0:A, bass.ds(G.i, 1)],
                                               in1=wexp[:, 0:A + 1], op0=ALU.mult, op1=ALU.add).then_inc(ev["wexp_ready"], 1)
                    if s == 1 and T:
                        e.wait_ge(ev["w2_done"], T.n)
                        e.wait_ge(ev["x2b_ready"], T.n)
                        wait(e, ev["x4_ready"], T.p)
                        e.tensor_tensor(x3[:, :, :], two(bbank[1]), x2b[:, :, :], ALU.add).then_inc(ev["x3_ready"], 1)
                    if s == 13 and G:
                        e.wait_ge(ev["up_done"], G.n)
                        wait(e, ev["x1_scaled"], G.p)
                        e.tensor_tensor(xa[:, :, :], two(fbank), xN[:, :, :], ALU.add).then_inc(ev["xa_ready"], 1)
                        e.wait_ge(ev["xa_ready"], G.n)
                        norm_stats(G, 0, xa, ev["xa_stats"], ev["xa_aggr"], ev["xa_var"])
                    if s == 5 and T:
                        e.wait_ge(ev["c_done"], T.n)
                        e.wait_ge(ev["x3c_ready"], T.n)
                        wait(e, ev["f_scaled"], T.p)
                        e.scalar_tensor_tensor(out=x4[:, :, :], in0=two(bbank[0]), scalar=kind_ok[:, bass.ds(T.i, 1)], in1=x3c[:, :, :],
                                               op0=ALU.mult, op1=ALU.add).then_inc(ev["x4_ready"], 1)
                    if s == 5 and T:
                        e.wait_ge(ev["x4_ready"], T.n)
                        norm_stats(T, 3, x4, ev["x4_stats"], ev["x4_aggr"], ev["x4_var"])
                    if s == 15 and G:
                        norm_affine(G, 0, yN, xa, gamma0[:, :], beta0[:, :], ev["xa_rstd"], ev["y_scaled"], ev["y_ready"])
                    if s == 0 and F:
                        e.wait_ge(ev["y_ready"], F.n)
                        norm_stats(F, 1, yN, ev["y_stats"], ev["y_aggr"], ev["y_var"])
                    if s == 6 and B:
                        context(B, 0, ev["c1_lo"], ev["sum_lo"], ev["inv_lo"], ev["ctxn_lo"])
                    if s == 6 and B:
                        context(B, 1, ev["c1_hi"], ev["sum_hi"], ev["inv_hi"], ev["ctxn_hi"])
                    if s == 6 and T:
                        norm_affine(T, 3, fN, x4, gamma3[:, :], beta3[:, :], ev["x4_rstd"], ev["f_scaled"], ev["f_ready"])
                    if s == 8 and B:
                        e.wait_ge(ev["wo_done"], B.n)
                        e.wait_ge(ev["res_moved"], B.n)
                        e.tensor_tensor(x2[:, :, :], two(bbank[1]), x1late[:, :, :], ALU.add).then_inc(ev["x2_ready"], 1)
                        e.wait_ge(ev["x2_ready"], B.n)
                        norm_stats(B, 2, x2, ev["x2_stats"], ev["x2_aggr"], ev["x2_var"])
                    if s == 10 and T:
                        e.wait_ge(ev["f_ready"], T.n)
                        wait(e, ev["out_ready"], T.p)
                        e.tensor_tensor(t_p[:, :, :], fN[:, :, :], grid_p[:, :, :], ALU.mult).then_inc(ev["p_ready"], 1)
                        edges(T, edge_u, 0, t_u, ev["u_edge"], ev["u_cols"])
                        e.wait_ge(ev["p_ready"], T.n)
                        e.tensor_tensor(t_u[:, :, 1:D - 1], t_p[:, :, 2:D], t_p[:, :, 0:D - 2], ALU.subtract).then_inc(ev["u_inner"], 1)
                    if s == 9 and B:
                        norm_apply(B, 2, n3, x2, ev["x2_rstd"], ev["n3_ready"])
                    if s == 2 and F:
                        e.wait_ge(ld_ada, times(F, 16))
                        wait(e, ev["x1_turned"], F.p)
                        wait(e, ev["x1res_ready"], F.p)
                        norm_affine(F, 1, x1, yN, ada[:, 0, :], ada[:, 1, :], ev["y_rstd"], ev["x1_scaled"], ev["x1_ready"])
                    if s == 11 and T:
                        e.wait_ge(ev["u_inner"], T.n)
                        e.wait_ge(ev["u_cols"], T.n)
                        e.wait_ge(ev["r1_ready"], T.n)
                        e.tensor_tensor(t_u[:, :, :], t_u[:, :, :], t_r1[:, :, :], ALU.add).then_inc(ev["u_ready"], 1)
                    if s == 10 and B:
                        e.wait_ge(ld_kind, times(B, 48))
                        wait(e, ev["x3c_ready"], B.p)
                        e.tensor_scalar(bcf[:, :], bcr[:, :], kind_ok[:, bass.ds(B.i, 1)], None, ALU.mult).then_inc(ev["bcf_ready"], 1)
                    if s == 14 and T:
                        e.wait_ge(ev["ga_ready"], T.n)
                        e.wait_ge(ev["gb2_ready"], T.n)
                        wait(e, ev["out_ready"], T.p)
                        edges(T, edge_e, 1, t_e, ev["e_edge"], ev["e_cols"])
                        e.tensor_tensor(t_e[:, :, 1:D - 1], t_a[:, :, 2:D], t_b[:, :, 0:D - 2], ALU.subtract).then_inc(ev["e_inner"], 1)
                        e.wait_ge(ev["gc_ready"], T.n)
                        e.wait_ge(ev["e_inner"], T.n)
                        e.tensor_tensor(t_e[:, :, 1:D - 1], t_e[:, :, 1:D - 1], t_c[:, :, 1:D - 1], ALU.add).then_inc(ev["e_ready"], 1)
                    if s == H - 1 and X:
                        head(e, biased, X, H - 1)
                        e.tensor_scalar(nan2[:, :, :], negmax[:, :, :], 2.0, None, ALU.mult).then_inc(ev["nan_twice"], 1)
                        e.wait_ge(ev["nan_twice"], X.n)
                        e.tensor_tensor(nanz[:, :, :], nan2[:, :, :], nan2[:, :, :], ALU.subtract).then_inc(ev["nan_ready"], 1)
                    if s == 4 and U:
                        e.wait_ge(ev["d_done"], U.n)
                        e.wait_ge(ev["e_ready"], U.n)
                        e.wait_ge(ev["e_cols"], U.n)
                        e.tensor_tensor(t_e[:, :, :], two(fbank), t_e[:, :, :], ALU.add).then_inc(ev["w_ready"], 1)
                        e.wait_ge(ev["w_ready"], U.n)
                        e.scalar_tensor_tensor(out=t_e[:, :, :], in0=t_e[:, :, :], scalar=dt[:, bass.ds(U.i, 1)], in1=fN[:, :, :],
                                               op0=ALU.mult, op1=ALU.add).then_inc(ev["w2s_ready"], 1)
                    if s in (6, 7) and F:
                        ready_, hi, lo, b, out = ((ev["qh_ready"], qh, ql, bq, ev["ql_ready"]), (ev["kh_ready"], kh, kl, bk, ev["kl_ready"]))[s - 6]
                        e.wait_ge(ready_, F.n)
                        for m in range(KT):
                            i = e.scalar_tensor_tensor(out=lo[:, m, :], in0=two(fbank)[:, m, :], scalar=b[:, m:m + 1],
                                                       in1=hi[:, m, :].bitcast(F32), op0=ALU.add, op1=ALU.subtract)
                        i.then_inc(out, 1)

            turns(e, body)

        @block.tensor
        def _(e):
            e.wait_ge(act_set, 2)
            e.wait_ge(ld_set, 16 * LOADS)
            e.wait_ge(pool_set, 3)
            for k in range(KT):
                e.matmul(fbank[0:NB, :], x1T[:, k, 0:NB], ffT[:, 2 * k:2 * k + 2, :], start=(k == 0), stop=False)
            e.matmul(fbank[0:NB, :], ones_row[0:1, 0:NB], xa[0:1, :, :], start=False, stop=True).then_inc(pe_set, 1)
            e.wait_ge(dve_set, 3)
            for k in range(KT):
                e.matmul(bbank[0][:, 0:D], gbT[:, k, 0:P], wo[:, k, :], start=(k == 0), stop=(k == KT - 1))
            for m in range(FM):
                for k in range(KT):
                    i = e.matmul(bbank[1][:, m:m + 1], w1[:, k, m * P:m * P + P], beta2c[:, k:k + 1], start=(k == 0), stop=(k == KT - 1))
            i.then_inc(pe_set, 1)
            e.sem_inc(ready, 2)
            e.wait_ge(ready, 4)

            def turn(dst, src, done):
                for k in range(KT):
                    for q in range(TT):
                        i = e.transpose(dst[:, k * S + q * P:k * S + q * P + P], src[:, q, k * P:k * P + P], ident[:, :])
                i.then_inc(done, 1)

            def project_T(dst, w, c0, xt, n_m, n_k, done):
                for m in range(n_m):
                    for k in range(n_k):
                        i = e.matmul(two(dst)[:, m, :], w[:, k, c0 + m * P:c0 + m * P + P], xt[:, k, :], start=(k == 0), stop=(k == n_k - 1))
                if done is not None:
                    i.then_inc(done, 1)

            def project(dst, xt, w, n_k, done, q0=0, q1=TT):
                for q in range(q0, q1):
                    for k in range(n_k):
                        i = e.matmul(two(dst)[:, q, :], xt[:, k, q * P:q * P + P], w[:, k, :], start=(k == 0), stop=(k == n_k - 1))
                if done is not None:
                    i.then_inc(done, 1)

            def body(t):
                G, F, X, B, T, U = phases(e, t)
                if T:
                    kind = e.value_load(ids_ok[0:1, 2, bass.ds(T.i, 1)], min_val=0, max_val=NC2 - 1)
                for s in range(SLOTS):
                    if X:
                        if s % HM == 0:
                            e.wait_ge(ld_stack[s // HM], times(X, 128))
                        head(e, biased, X, s - 2)
                        for q in range(TT):
                            i = e.matmul(two(sbank[s % 2])[:, q, :], qs[:, s, q * P:q * P + P], ks[:, s, :], start=True, stop=True)
                        i.then_inc(scored[s % 4], 1)
                    for x, h in lagging(X, B, s - LT):
                        head(e, expd, x, h)
                        head(e, copied, x, h - 2)
                        for k in range(TT):
                            for q in range(TT):
                                i = e.transpose(tbank[h % 2][:, k * S + q * P:k * S + q * P + P], sc[:, h % NS, q, k * P:k * P + P], ident[:, :])
                        i.then_inc(turned[h % 4], 1)
                    for x, h in lagging(X, B, s - LP):
                        head(e, copied, x, h)
                        if h == 0:
                            e.wait_ge(ev["vp_ready"], x.n)
                            wait(e, ev["ct_hi"], x.p)
                        if h == HM:
                            e.wait_ge(ev["ct_lo"], x.n)
                        o = VW * (h % 4)
                        for k in range(TT):
                            i = e.matmul(two(cbank)[o:o + VW, h // 4 % 2, :], vp[:, k, h, :], pt[:, h % NP2, k, :],
                                         start=(k == 0), stop=(k == TT - 1))
                        i.then_inc(mixed[h % 4], 1)
                    if s == 2 and T:
                        e.wait_ge(ev["x3_ready"], T.n)
                        turn(bbank[0], x3, ev["x3_turned"])
                    if s == 9 and F:
                        e.wait_ge(ev["kl_ready"], F.n)
                        project(fbank, x1T, wv, KT, ev["v_done"])
                    if s == 3 and T:
                        e.wait_ge(ev["x3T_ready"], T.n)
                        with e.If(kind == 2):
                            for j in range(2):
                                project_T(bbank[(j + 1) % 2], wa, 2 * j * P, x3T, 2, KT, wa_done[j])
                        with e.Else():
                            for j in range(2):
                                e.sem_inc(wa_done[j], 1)
                    if s == 4 and T:
                        e.wait_ge(ld_kind, times(T, 48))
                        for j in range(2):
                            e.wait_ge(ga2_ready[j], T.n)
                        with e.If(kind == 2):
                            project_T(bbank[1], wb, 0, gaT, KT, A2 // P, ev["b_done"])
                        with e.Else():
                            project_T(bbank[1], wb, 0, x3T, KT, KT, ev["b_done"])
                    if s == 5 and T:
                        e.wait_ge(ev["gb_ready"], T.n)
                        project(bbank[0], gbT, wc, KT, ev["c_done"])
                    if s == 6 and B:
                        e.wait_ge(ev["ct_hi"], B.n)
                        for u in range(2):
                            wait(e, (ev["gb_ready"], ev["x4_ready"])[u], B.p)
                            for q in range(TT):
                                for g in range(2):
                                    i = e.transpose(bbank[1 - u][:, q * S + g * P:q * S + g * P + P], cts[:, 2 * u + g, q * P:q * P + P], ident[:, :])
                            i.then_inc((ev["c1_lo"], ev["c1_hi"])[u], 1)
                    if s == 7 and B:
                        e.wait_ge(ev["ctxn_lo"], B.n)
                        e.wait_ge(ev["ctxn_hi"], B.n)
                        turn(bbank[0], ctxN, ev["c2_turned"])
                    if s == 8 and B:
                        e.wait_ge(ev["ctxT_ready"], B.n)
                        project(bbank[1], ctxT, wo, KT, ev["wo_done"])
                    if s == 10 and B:
                        e.wait_ge(ev["n3_ready"], B.n)
                        turn(bbank[0], n3, ev["n3_turned"])
                    if s in (11, 12, 13, 14) and B:
                        j = s - 11
                        if j >= 2:
                            quarter(e, "u1_ready", B, j - 2)
                        else:
                            e.wait_ge(ev[("x2_ready", "n3T_ready")[j]], B.n)
                        if j == 0:
                            e.wait_ge(ev["n3T_ready"], B.n)
                        project_T(bbank[(j + 1) % 2], w1, 2 * j * P, n3T, 2, KT, ev["w1_done"])
                    if s == 5 and F:
                        e.wait_ge(ev["x1_ready"], F.n)
                        if U:
                            e.wait_ge(ev["w_ready"], U.n)
                        turn(fbank, x1, ev["x1_turned"])
                    if s == 6 and F:
                        e.wait_ge(ev["x1T_ready"], F.n)
                        project_T(fbank, wq, 0, x1T, KT, KT, ev["q_done"])
                    if s in (3, 4) and U:
                        q = s - 3
                        if q == 0:
                            e.wait_ge(ev["u_ready"], U.n)
                            e.wait_ge(ev["r2_ready"], U.n)
                            if F:
                                e.wait_ge(ev["xa_ready"], F.n)
                            elif X:
                                e.wait_ge(ev["v_ready"], X.n)
                            wait(e, ev["w_ready"], U.p)
                        for n, (m, u) in enumerate(((d1T, t_u), (d2T, t_r2))):
                            for k in range(KT):
                                i = e.matmul(two(fbank)[:, q, :], m[:, k, q * P:q * P + P], u[:, k, :],
                                             start=(n == 0 and k == 0), stop=(n == 1 and k == KT - 1))
                        if q == TT - 1:
                            i.then_inc(ev["d_done"], 1)
                    if s == 10 and G:
                        e.wait_ge(ld_x, times(G, 16))
                        if F:
                            e.wait_ge(ev["v_ready"], F.n)
                        turn(fbank, xN, ev["xT_turned"])
                    if s == 11 and G:
                        e.wait_ge(ev["xT_ready"], G.n)
                        for k in range(KT):
                            i = e.matmul(fbank[0:A, 0:S], downT[:, k, :], xT[:, k, :], start=(k == 0), stop=(k == KT - 1))
                        i.then_inc(ev["down_done"], 1)
                    if s == 12 and G:
                        e.wait_ge(ev["g0_ready"], G.n)
                        e.wait_ge(ev["wexp_ready"], G.n)
                        hold(e)
                        e.matmul(fbank[0:A, 0:S], wexp[:, 0:A], g0[:, :], start=True, stop=True).then_inc(ev["expert_done"], 1)
                    if s == 13 and G:
                        e.wait_ge(ev["g1_ready"], G.n)
                        for q in range(TT):
                            i = e.matmul(two(fbank)[:, q, :], g1[:, q * P:q * P + P], upT[:, :], start=True, stop=True)
                        i.then_inc(ev["up_done"], 1)
                    if s == 7 and F:
                        e.wait_ge(ev["ql_ready"], F.n)
                        project_T(fbank, wk, 0, x1T, KT, KT, ev["k_done"])
                    x, part = {15: (B, 0), 0: (T, 1), 1: (T, 2)}.get(s, (None, 0))
                    if x:
                        if part < 2:
                            quarter(e, "ff_ready", x, 2 * part + 1)
                        if part == 0:
                            quarter(e, "u1_ready", x, 2)
                        for n in range(*((0, 4), (4, 10), (10, TT * FM))[part]):
                            q, k = n // FM, n % FM
                            i = e.matmul(two(bbank[1])[:, q, :], ffT[:, k, q * P:q * P + P], w2[:, k, :], start=(k == 0), stop=(k == FM - 1))
                        if part == 2:
                            i.then_inc(ev["w2_done"], 1)

            turns(e, body)


def kernel(x, itok_B_0_15, itok_B_34_63, fside_Bx16xSxS_0, itok_B_0_2, condB_dt, mask_Bx1xSxS_bk0, **w):
    import concourse.bacc as bacc
    from concourse.bass_utils import run_bass_kernel_spmd

    def arr(a):
        return np.ascontiguousarray(np.asarray(a))

    c = {k.replace("_cond_", "_"): arr(v) for k, v in w.items()}

    def by_head(a):
        return arr(a.reshape(-1, KT, HM, DH).transpose(0, 1, 3, 2).reshape(a.shape))

    def column(v):
        return v.reshape(-1, P).T

    ins = {
        "x": arr(x), "dom": arr(itok_B_0_15), "step": arr(itok_B_34_63), "kind": arr(itok_B_0_2), "dt": arr(condB_dt),
        "side": arr(fside_Bx16xSxS_0), "mask": arr(mask_Bx1xSxS_bk0).reshape(NB, S, S).view(np.int32),
        "freq": np.exp(np.arange(D // 2, dtype=np.float32) * np.float32(-np.log(10000.0) / (D // 2 - 1))),
        "down_b": c["L0_down_b"], "downT": arr(c["L0_down_W"].T), "upT": arr(c["L0_up_W"].T), "up_b": c["L0_up_b"],
        "expert": np.concatenate([c["L0_expert_W"].transpose(0, 2, 1), c["L0_expert_b"][:, :, None],
                                  c["L0_domain_emb"][:, :, None]], axis=2),
        "gamma0": c["L0_ln_gamma"], "beta0": c["L0_ln_beta"],
        "wq": by_head(c["L1_Wq"]), "wk": by_head(c["L1_Wk"]), "wv": c["L1_Wv"], "wo": c["L1_Wo"],
        "w1": c["L1_W1"], "w2": c["L1_W2"], "w_ada": c["L1_W_ada"], "b_ada": c["L1_b_ada"],
        "b2": c["L1_b2"], "bo": c["L1_bo"],
        "colpack": arr(np.concatenate([column(v) for v in (
            by_head(c["L1_bq"]), by_head(c["L1_bk"]), c["L1_bv"], c["L1_g2"], c["L1_beta2"], c["L1_b1"], c["L2_b1_sr"],
            c["L2_b1_nr"], c["L2_b1_tsr"], c["L2_b2_sr"])], axis=1)),
        "wa": c["L2_w1_sr"],
        "wb": np.concatenate([c["L2_w1_nr"], c["L2_w1_tsr"], c["L2_w2_sr"]]).reshape(4, D, D),
        "wc": np.stack([c["L2_w2_nr"], c["L2_w2_tsr"], c["L2_w3_sr"]]),
        "bc": np.stack([c["L2_b2_nr"], c["L2_b2_tsr"], c["L2_b3_sr"]]),
        "gamma3": c["L2_gamma"], "beta3": c["L2_beta"],
        "d1T": arr(rest_grad(S).T), "d2T": arr(rest_grad2(S).T),
        "grid_A": c["L3_A_grid"], "grid_B": c["L3_B_grid"],
    }
    nc = bacc.Bacc("TRN2", target_bir_lowering=False, num_devices=1)
    d = {n: nc.dram_tensor("in_" + n, a.shape, mybir.dt.from_np(a.dtype), kind="ExternalInput").ap() for n, a in ins.items()}
    d["ada_rows"] = nc.dram_tensor("ada_rows", (NB, 2 * D), F32, kind="Internal").ap()
    d["out"] = nc.dram_tensor("out", (NB, S, D), F32, kind="ExternalOutput").ap()
    build(nc, d)
    return run_bass_kernel_spmd(nc, [{"in_" + n: a for n, a in ins.items()}], core_ids=[0]).results[0]["out"]
```

```python
from contextlib import ExitStack

import numpy as np

import concourse.bass as bass
from concourse import mybir

ALU = mybir.AluOpType
ACT = mybir.ActivationFunctionType
AX_X = mybir.AxisListType.X
F32 = mybir.dt.float32
F32R = mybir.dt.float32r
I32 = mybir.dt.int32
U8 = mybir.dt.uint8

P = 128
NB = 16
S = 256
D = 256
TT = S // P
KT = D // P
H = 16
DH = D // H
HM = H // KT
A = 64
NE = 16
FF = 1024
FM = FF // P
NC2 = 3
NSIDE = 8
A2 = 512
VW = 32
NBLK = 4
LM = 3
LT, LP = 2, 3
ACT_COPIES = (0, 1, 2, 3, 5, 6, 7, 8, 9, 10, 14)
SLOTS = H
EPS = 1e-5
MASKED = -float(2.0 ** 127)
ROUND = float(1.5 * 2 ** 23)
TWO_PI = (6.28125, 0.0019350051879882812, 3.0198672e-07)

EVENTS = """
xT_turned xT_ready down_done g0_ready wexp_ready expert_done g1_ready up_done xa_ready
xa_stats xa_aggr xa_var xa_rstd y_scaled y_ready
y_stats y_aggr y_var y_rstd x1_scaled x1_ready x1_turned x1T_ready
q_done qh_ready ql_ready k_done kh_ready kl_ready mask_ready
v_done v_ready vp_ready res_moved x1res_ready ct_lo ct_hi nan_ready
c1_lo c1_hi sum_lo sum_hi inv_lo inv_hi ctxn_lo ctxn_hi c2_turned ctxT_ready wo_done x2_ready
x2_stats x2_aggr x2_var x2_rstd n3_ready x2b_ready n3_turned n3T_ready n3l_ready
w1_done u1_ready th_ready ff_ready w2_done x3_ready bcf_ready x3c_ready x3_turned x3T_ready b_done gb_ready c_done x4_ready
x4_stats x4_aggr x4_var x4_rstd f_scaled f_ready
ga_ready gb2_ready gc_ready r1_ready r2_ready p_ready u_edge u_cols u_inner u_ready
e_edge e_cols e_inner e_ready d_done w_ready w2s_ready out_ready
""".split()


class Sample:

    def __init__(self, e, t, off):
        self.e, self.t, self.off = e, t, off
        self.i = self.keep(t + off)
        self.p = self.i
        self.n = self.keep(t + (off + 1))
        self.h = {k: self.keep(t * 4 + (4 * off + k + 1)) for k in range(-1, 4)}

    def keep(self, v):
        return v if isinstance(v, int) else self.e.snap(v)


def rest_grad(n):
    m = np.zeros((n, n), np.float32)
    for i in range(1, n - 1):
        m[i, i + 1], m[i, i - 1] = 0.5, -0.5
    m[0, :3] = (-1.5, 2.0, -0.5)
    m[n - 1, n - 3:] = (0.5, -2.0, 1.5)
    return m


def rest_grad2(n):
    m = np.zeros((n, n), np.float32)
    for i in range(1, n - 1):
        m[i, i - 1], m[i, i], m[i, i + 1] = 1.0, -2.0, 1.0
    m[0, :4] = (2.0, -5.0, 4.0, -1.0)
    m[n - 1, n - 4:] = (-1.0, 4.0, -5.0, 2.0)
    return m


def build(nc, d):
    with ExitStack() as ctx:
        def sb(name, shape, dt=F32):
            return ctx.enter_context(nc.sbuf_tensor(name, shape, dt))

        def sem(name):
            return ctx.enter_context(nc.semaphore(name))

        ident = sb("ident", [P, P])
        ones_row = sb("ones_row", [1, P])
        downT = sb("downT", [P, KT, A])
        down_b = sb("down_b", [A, 1])
        upT = sb("upT", [A + 1, D])
        wq, wql = sb("wq", [P, KT, D], F32R), sb("wql", [P, KT, D], F32R)
        wk, wkl = sb("wk", [P, KT, D], F32R), sb("wkl", [P, KT, D], F32R)
        wv, wvl = sb("wv", [P, KT, D], F32R), sb("wvl", [P, KT, D], F32R)
        wo = sb("wo", [P, KT, D])
        w1 = sb("w1", [P, KT, FF], F32R)
        w1l = sb("w1l", [P, KT, FF], F32R)
        w2 = sb("w2", [P, FM, D])
        wa = sb("wa", [P, KT, A2])
        cols = sb("cols", [P, 64])
        bq, bk, bv = cols[:, 0:2], cols[:, 2:4], cols[:, 4:6]
        g2c, beta2c, b1c, bac, freq = cols[:, 6:8], cols[:, 8:10], cols[:, 10:18], cols[:, 18:22], cols[:, 22:23]
        bbc = cols[:, 24:30].rearrange("p (c m) -> p c m", c=NC2)
        gamma0 = sb("gamma0", [P, D])
        beta0 = sb("beta0", [P, D])
        b2r = sb("b2r", [P, D])
        bo = sb("bo", [P, D])
        gamma3 = sb("gamma3", [P, D])
        beta3 = sb("beta3", [P, D])
        d1T = sb("d1T", [P, KT, S])
        d2T = sb("d2T", [P, KT, S])
        grid_a = sb("grid_a", [P, TT, D])
        grid_b = sb("grid_b", [P, TT, D])
        grid_c = sb("grid_c", [P, TT, D])
        grid_r1 = sb("grid_r1", [P, TT, D])
        grid_r2 = sb("grid_r2", [P, TT, D])
        grid_p = sb("grid_p", [P, TT, D])
        edge_e = sb("edge_e", [P, TT, 2, 4])
        edge_u = sb("edge_u", [P, TT, 2, 4])
        ids = sb("ids", [P, 3, NB], I32)
        idf = sb("idf", [P, 3, NB])
        flags = sb("flags", [P, 8, NB])
        dom_ok, dom_no, kind_ok, dt = flags[:, 0, :], flags[:, 1, :], flags[:, 2, :], flags[:, 3, :]
        ids_ok = sb("ids_ok", [P, 3, NB], I32)
        half_neg = sb("half_neg", [P, TT])
        bsel = sb("bsel", [P, NB, KT])

        xN = sb("xN", [P, TT, D])
        g0 = sb("g0", [A, S])
        g1 = sb("g1", [A + 1, S])
        wexp_raw = sb("wexp_raw", [A, A + 2])
        wexp = sb("wexp", [A, A + 2])
        xa = sb("xa", [P, TT, D])
        yN = xa
        x1 = sb("x1", [P, TT, D])
        ada = sb("ada", [P, 2, D])
        qh = sb("qh", [P, KT, S], F32R)
        ql = sb("ql", [P, KT, S], F32R)
        kh = sb("kh", [P, KT, S], F32R)
        kl = sb("kl", [P, KT, S], F32R)
        qs = sb("qs", [P, H, S], F32R)
        ks = sb("ks", [P, H, S], F32R)
        mask_raw = sb("mask_raw", [P, TT, S // 4], I32)
        mask_neg = sb("mask_neg", [P, TT, S])
        side = sb("side", [P, NSIDE, TT, S])
        NS, NP2 = 4, 2
        sc = sb("sc", [P, NS, TT, S])
        w1_raw = sc[:, :, :, :].rearrange("p (k a) t x -> p k (a t x)", k=KT)
        pt = sb("pt", [P, NP2, TT, S])
        negmax = sb("negmax", [P, TT, H])
        nanz = sb("nanz", [P, TT, H])
        vp = sb("vp", [P, TT, H, VW])
        cts = sb("cts", [P, H // 4, S])
        rsum = sb("rsum", [P, TT, H])
        rinv = sb("rinv", [P, TT, H])
        x1res = sb("x1res", [P, TT, D])
        x1late = sb("x1late", [P, TT, D])
        n3 = sb("n3", [P, TT, D])
        n3h = sb("n3h", [P, KT, S], F32R)
        ctxT = sb("ctxT", [P, KT, S])
        n3l = sb("n3l", [P, KT, S], F32R)
        xT = n3
        ctxN, x3T = n3, ctxT
        x1h, x1l = n3h, n3l
        x2 = sb("x2", [P, TT, D])
        x2b = x2
        ffT = sb("ffT", [P, FM, S])
        th = sb("th", [P, 2, 2, S])
        x3 = sb("x3", [P, TT, D])
        x3c = x3
        gaT = ffT[:, 0:A2 // P, :]
        gbT = sb("gbT", [P, KT, S])
        vnext = gbT
        wb = sb("wb", [P, A2 // P, D])
        wc = sb("wc", [P, KT, D])
        bcr = sb("bcr", [P, D])
        bcf = bcr
        x4 = sb("x4", [P, TT, D])
        fN = sb("fN", [P, TT, D])
        t_a, t_b = wb[:, 0:TT, :], wb[:, TT:2 * TT, :]
        t_c = x4
        t_r1 = sb("t_r1", [P, TT, D])
        t_r2 = sb("t_r2", [P, TT, D])
        t_u = sb("t_u", [P, TT, D])
        t_e = sb("t_e", [P, TT, D])
        t_p = t_e
        edge_t = sb("edge_t", [P, 2, TT, 2, 4])
        outN = t_r1
        switch = sb("switch", [P, 1])
        stats = sb("stats", [P, 4, TT, 6])
        mv = sb("mv", [P, 4, TT, 2])
        var = sb("var", [P, 4, TT])
        rstd = sb("rstd", [P, 4, TT])

        def bank(name):
            return ctx.enter_context(nc.psum_tensor(name, [P, 512], F32))

        sbank = [bank("score_bank0"), bank("score_bank1")]
        tbank = [bank("turn_bank0"), bank("turn_bank1")]
        cbank = bank("context_bank")
        fbank = bank("front_bank")
        bbank = [bank("back_bank0"), bank("back_bank1")]

        def two(b):
            return b[:, :].rearrange("p (a x) -> p a x", a=2)

        ev = {n: sem(n) for n in EVENTS}
        masked = [sem(f"masked{h}") for h in range(4)]
        scored = [sem(f"scored{h}") for h in range(4)]
        biased = [sem(f"biased{h}") for h in range(4)]
        expd = [sem(f"expd{h}") for h in range(4)]
        turned = [sem(f"turned{h}") for h in range(4)]
        copied = [sem(f"copied{h}") for h in range(4)]
        mixed = [sem(f"mixed{h}") for h in range(4)]
        wa_done = [sem(f"wa_done{j}") for j in range(2)]
        ga2_ready = [sem(f"ga2_ready{j}") for j in range(2)]
        ld_x, ld_mask, ld_exp, ld_ada, ld_kind, ld_row = sem("ld_x"), sem("ld_mask"), sem("ld_exp"), sem("ld_ada"), sem("ld_kind"), sem("ld_row")
        ld_side = [sem(f"ld_side{c}") for c in range(4)]
        ld_stack = [sem(f"ld_stack{m}") for m in range(KT)]
        stored = sem("stored")
        wexp_half = sem("wexp_half")
        passed = {k: sem(f"passed_{n}") for k, n in ((nc.vector.engine, "dve"), (nc.tensor.engine, "pe"), (nc.gpsimd.engine, "pool"))}
        ld_first, ld_second, ld_set = sem("ld_first"), sem("ld_second"), sem("ld_set")
        ld_ids, st_ada = sem("ld_ids"), sem("st_ada")
        pool_set, dve_set, act_set, pe_set, ready = (
            sem("pool_set"), sem("dve_set"), sem("act_set"), sem("pe_set"), sem("ready"))
        sem_dve = sem("sem_dve")

        block = ctx.enter_context(nc.Block())

        def wait(e, s, n):
            if not (isinstance(n, int) and n <= 0):
                e.wait_ge(s, n)

        def phase(e, t, off):
            if isinstance(t, int) and not 0 <= t + off < NB:
                return None
            return Sample(e, t, off)

        def hold(e):
            e.sem_inc(passed[e.engine], 1)

        def quarter(e, s, x, j):
            e.wait_ge(ev[s], x.h[j])

        def times(x, k, prev=False):
            return x.keep((x.t + x.off + (0 if prev else 1)) * k)

        def head(e, s, x, h):
            wait(e, s[h % 4], x.h[h // 4])

        def turns(e, body):
            for t in range(-2, 4):
                body(t)
            with e.Fori(4, NB - 2) as t:
                body(t)
            for t in range(NB - 2, NB + 3):
                body(t)

        def lagging(x, before, h):
            x, h = (x, h) if h >= 0 else (before, h + H)
            return [(x, h)] if x else []

        def is_step(t, s, t0, s0):
            return isinstance(t, int) and (t, s) == (t0, s0)

        def phases(e, t):
            return phase(e, t, 2), phase(e, t, 1), phase(e, t, 0), phase(e, t, -1), phase(e, t, -2), phase(e, t, -3)

        LOADS_FIRST, LOADS_SECOND, LOADS = 9, 5, 15

        @block.sync
        def _(e):
            for k in range(3):
                e.dma_start(ids[:, k, :], d[("dom", "step", "kind")[k]].partition_broadcast(P)).then_inc(ld_ids, 16)
            e.dma_start(dt, d["dt"].partition_broadcast(P)).then_inc(ld_ids, 16)
            def load_all(pairs, count, done):
                assert len(pairs) == count
                for dst, src in pairs:
                    e.dma_start(dst, src).then_inc(done, 16)

            load_all((
                (freq, d["freq"].rearrange("(p a) -> p a", a=1)),
                (cols[:, 0:22], d["colpack"][:, 0:22]),
                (cols[:, 24:30], d["colpack"][:, 22:28]),
                (down_b[:, :], d["down_b"].rearrange("(p a) -> p a", a=1)),
                (downT[:, :, :], d["downT"].rearrange("(k p) a -> p k a", p=P)),
                (upT[0:A, :], d["upT"]),
                (upT[A:A + 1, :], d["up_b"].rearrange("(a n) -> a n", a=1)),
                (gamma0[:, :], d["gamma0"].partition_broadcast(P)),
                (beta0[:, :], d["beta0"].partition_broadcast(P)),
            ), LOADS_FIRST, ld_first)
            e.dma_start(xN[:, :, :], d["x"][0:1].rearrange("b (t p) n -> p (b t) n", p=P)).then_inc(ld_x, 16)
            load_all((
                (ffT[:, 0:4, :], d["w_ada"].rearrange("(k p) n -> p k n", p=P)),
                (x1[0:1, :, :], d["b_ada"].rearrange("(a k n) -> a k n", a=1, k=2)),
                (pt[:, 0, :, :], d["wq"].rearrange("(k p) n -> p k n", p=P)),
                (pt[:, 1, :, :], d["wk"].rearrange("(k p) n -> p k n", p=P)),
                (th[:, 0, :, :], d["wv"].rearrange("(k p) n -> p k n", p=P)),
            ), LOADS_SECOND, ld_second)
            e.wait_ge(dve_set, 1)
            dom0 = e.value_load(ids_ok[0:1, 0, 0:1], min_val=0, max_val=NE - 1)
            e.dma_start(wexp_raw[:, :], d["expert"][bass.ds(dom0, 1)].rearrange("e a n -> (e a) n")).then_inc(ld_exp, 16)
            load_all((
                (bo[:, :], d["bo"].partition_broadcast(P)),
                (wo[:, :, :], d["wo"].rearrange("(k p) n -> p k n", p=P)),
                (w1_raw, d["w1"].rearrange("(k p) n -> p k n", p=P)),
                (w2[:, :, :], d["w2"].rearrange("(k p) n -> p k n", p=P)),
                (t_a[:, :, :], d["grid_B"][0].rearrange("(t p) n -> p t n", p=P)),
                (t_b[:, :, :], d["grid_B"][1].rearrange("(t p) n -> p t n", p=P)),
                (t_c[:, :, :], d["grid_B"][2].rearrange("(t p) n -> p t n", p=P)),
                (x2[:, :, :], d["grid_A"][0].rearrange("(t p) n -> p t n", p=P)),
                (x3[:, :, :], d["grid_A"][1].rearrange("(t p) n -> p t n", p=P)),
                (wa[:, :, :], d["wa"].rearrange("(k p) n -> p k n", p=P)),
                (b2r[:, :], d["b2"].partition_broadcast(P)),
                (gamma3[:, :], d["gamma3"].partition_broadcast(P)),
                (beta3[:, :], d["beta3"].partition_broadcast(P)),
                (d1T[:, :, :], d["d1T"].rearrange("(k p) n -> p k n", p=P)),
                (d2T[:, :, :], d["d2T"].rearrange("(k p) n -> p k n", p=P)),
            ), LOADS, ld_set)
            e.wait_ge(dve_set, 3)
            e.dma_start(d["ada_rows"], x3T[0:NB, :, :]).then_inc(st_ada, 16)
            e.wait_ge(st_ada, 16)

            def load_side(x, c):
                e.dma_start(side[:, 4 * c % NSIDE:4 * c % NSIDE + 4, :, :],
                            d["side"][bass.ds(x.i, 1), 4 * c:4 * c + 4].rearrange("b h (t p) k -> p (b h) t k", p=P)
                            ).then_inc(ld_side[c], 16)

            def stack(x, prev, m):
                if prev is not None:
                    head(e, scored, prev, HM * m + HM - 1)
                for b in range(NBLK):
                    for dst, hi, lo, low in ((qs, qh, ql, b >= 2), (ks, kh, kl, b % 2 == 1)):
                        src = lo if low else hi
                        e.dma_start(dst[DH * b:DH * b + DH, HM * m:HM * m + HM, :].bitcast(F32), src[:, m, :].bitcast(F32)).then_inc(ld_stack[m], 16)

            def body(t):
                G, F, X, B, T, U = phases(e, t)
                for s in range(SLOTS):
                    if is_step(t, s, -1, 5):
                        e.wait_ge(ready, 2)
                    if s == 0 and G and not is_step(t, s, -2, 0):
                        wait(e, ev["xa_ready"], G.p)
                        e.dma_start(xN[:, :, :], d["x"][bass.ds(G.i, 1)].rearrange("b (t p) n -> p (b t) n", p=P)).then_inc(ld_x, 16)
                        wait(e, ev["wexp_ready"], G.p)
                        dom = e.value_load(ids_ok[0:1, 0, bass.ds(G.i, 1)], min_val=0, max_val=NE - 1)
                        e.dma_start(wexp_raw[:, :], d["expert"][bass.ds(dom, 1)].rearrange("e a n -> (e a) n")).then_inc(ld_exp, 16)
                    if s == 2 and G:
                        wait(e, ev["x1_ready"], G.p)
                        e.dma_start(ada[:, :, :].rearrange("p a n -> p (a n)"), d["ada_rows"][bass.ds(G.i, 1)].rearrange("b n -> (b n)").partition_broadcast(P)).then_inc(ld_ada, 16)
                    if s == 0 and F:
                        wait(e, ev["mask_ready"], F.p)
                        e.dma_start(mask_raw[:, :, :], d["mask"][bass.ds(F.i, 1)].rearrange("b (t p) n -> p (b t) n", p=P)).then_inc(ld_mask, 16)
                        if isinstance(t, int) and t == -1:
                            for c in range(2):
                                load_side(F, c)
                    if s == 5 and B:
                        kind = e.value_load(ids_ok[0:1, 2, bass.ds(B.i, 1)], min_val=0, max_val=NC2 - 1)
                    if s == 6 and B:
                        wait(e, ev["c_done"], B.p)
                        e.dma_start(wc[:, :, :], d["wc"][bass.ds(kind, 1)].rearrange("c (k p) n -> p (c k) n", p=P)).then_inc(ld_kind, 16)
                        wait(e, ev["x3c_ready"], B.p)
                        e.dma_start(bcr[:, :], d["bc"][bass.ds(kind, 1)].rearrange("c n -> (c n)").partition_broadcast(P)).then_inc(ld_row, 16)
                    if s == 14 and B:
                        wait(e, ev["e_ready"], B.p)
                        e.dma_start(wb[:, :, :], d["wb"][bass.ds(kind, 2)].rearrange("c (k p) n -> p (c k) n", p=P)).then_inc(ld_kind, 16)
                    if s % 4 == 0 and X and (s < 12 or F):
                        c = s // 4
                        head(e, biased, X, 4 * c - 1)
                        if not (isinstance(t, int) and t == 0 and s == 0):
                            load_side(X if c < 3 else F, (c + 1) % 4)
                    if s == 7 and U:
                        e.wait_ge(ev["out_ready"], U.n)
                        e.dma_start(d["out"][bass.ds(U.i, 1)].rearrange("b (t p) n -> p (b t) n", p=P), outN[:, :, :]).then_inc(stored, 16)
                    if s == 8 and F:
                        e.wait_ge(ev["ql_ready"], F.n)
                        e.wait_ge(ev["kl_ready"], F.n)
                        stack(F, X, 0)
                    if s == 0 and X:
                        stack(X, B, 1)

            turns(e, body)
            e.wait_ge(stored, 16 * NB)

        @block.gpsimd
        def _(e):
            e.memset(ident[:, :], 0.0).then_inc(pool_set, 1)
            e.memset(half_neg[:, :], -0.5)
            e.memset(ones_row[:, :], 1.0)
            e.memset(g1[:, :], 1.0)
            e.memset(vp[:, :, :, :], 0.0).then_inc(pool_set, 1)
            e.wait_ge(pool_set, 2)
            e.memset(vp[:, :, :, DH:DH + 1], 1.0)
            e.affine_select(out=ident[:, :], in_=ident[:, :], compare_op=ALU.not_equal, fill=1.0,
                            base=0, pattern=[[-1, P]], channel_multiplier=1).then_inc(pool_set, 1)
            e.wait_ge(pool_set, 3)
            e.memset(qs[:, :, :].bitcast(F32), 0.0)
            e.memset(ks[:, :, :].bitcast(F32), 0.0).then_inc(ready, 1)

            def power(x, k, var_ev, rstd_ev):
                e.wait_ge(var_ev, x.n)
                e.tensor_tensor(rstd[:, k, :], var[:, k, :], half_neg[:, :], ALU.pow).then_inc(rstd_ev, 1)

            def rows(r):
                return r.unsqueeze(1).broadcast_to([P, TT, D])

            def mask_bias(x, h):
                if h % 4 == 0:
                    e.wait_ge(ld_side[h // 4], times(x, 16))
                v = side[:, h % NSIDE, :, :]
                e.tensor_tensor(v, v, mask_neg[:, :, :], ALU.add).then_inc(masked[h % 4], 1)

            def body(t):
                G, F, X, B, T, U = phases(e, t)
                for s in range(SLOTS):
                    if is_step(t, s, -1, 5):
                        e.wait_ge(ready, 2)
                    if is_step(t, s, 1, 0):
                        e.wait_ge(ready, 4)
                    ahead = s + LM
                    if X and ahead < H:
                        mask_bias(X, ahead)
                    if F and ahead == H:
                        head(e, masked, F, -1)
                        e.wait_ge(ld_mask, times(F, 16))
                        hold(e)
                        e.tensor_scalar(mask_neg[:, :, :], mask_raw[:, :, :].bitcast(U8), MASKED, None, ALU.mult).then_inc(ev["mask_ready"], 1)
                        e.wait_ge(ev["mask_ready"], F.n)
                    if F and ahead >= H:
                        mask_bias(F, ahead - H)
                    for at, x, k, n in ((13, G, 0, "xa"), (5, T, 3, "x4"), (1, F, 1, "y"), (8, B, 2, "x2")):
                        if s == at and x:
                            power(x, k, ev[n + "_var"], ev[n + "_rstd"])
                    if is_step(t, s, -1, 12):
                        e.wait_ge(ready, 3)
                    if s == 12 and F:
                        wait(e, ev["res_moved"], F.p)
                        e.wait_ge(ev["x1_ready"], F.n)
                        e.tensor_tensor(x1res[:, :, :], x1[:, :, :], rows(bo[:, :]), ALU.add).then_inc(ev["x1res_ready"], 1)
                    if s == 7 and T:
                        e.wait_ge(ev["f_ready"], T.n)
                        e.tensor_tensor(t_r2[:, :, :], fN[:, :, :], grid_r2[:, :, :], ALU.mult).then_inc(ev["r2_ready"], 1)
                    if s == 8 and T:
                        wait(e, stored, times(T, 16, prev=True))
                        e.tensor_tensor(t_r1[:, :, :], fN[:, :, :], grid_r1[:, :, :], ALU.mult).then_inc(ev["r1_ready"], 1)
                    if s == 9 and T:
                        e.tensor_tensor(t_a[:, :, :], fN[:, :, :], grid_a[:, :, :], ALU.mult).then_inc(ev["ga_ready"], 1)
                    if s == 10 and B:
                        e.wait_ge(ev["n3_ready"], B.n)
                        e.tensor_tensor(x2b[:, :, :], x2[:, :, :], rows(b2r[:, :]), ALU.add).then_inc(ev["x2b_ready"], 1)
                    if s == 10 and T:
                        e.tensor_tensor(t_b[:, :, :], fN[:, :, :], grid_b[:, :, :], ALU.mult).then_inc(ev["gb2_ready"], 1)
                    if s == 11 and T:
                        e.tensor_tensor(t_c[:, :, :], fN[:, :, :], grid_c[:, :, :], ALU.mult).then_inc(ev["gc_ready"], 1)
                    if s == 3 and T:
                        e.wait_ge(ev["bcf_ready"], T.n)
                        e.wait_ge(ev["x3_turned"], T.n)
                        e.tensor_tensor(x3c[:, :, :], x3[:, :, :], rows(bcf[:, :]), ALU.add).then_inc(ev["x3c_ready"], 1)

            turns(e, body)

        @block.scalar
        def _(e):
            e.wait_ge(dve_set, 2)
            e.activation(x1late[:, :, 0:NB], x1late[:, :, 0:NB], ACT.Sin).then_inc(act_set, 1)
            e.wait_ge(act_set, 1)
            e.activation(x1late[:, :, 0:NB], x1late[:, :, 0:NB], ACT.Silu).then_inc(act_set, 1)
            e.wait_ge(ld_first, 16 * LOADS_FIRST)
            e.wait_ge(pool_set, 3)

            def bring_gelu():
                e.activation(switch[:, :], ident[:, 0:1], ACT.Gelu)

            def copy_turned(x, h):
                head(e, turned, x, h)
                head(e, mixed, x, h - NP2)
                e.activation(pt[:, h % NP2, :, :], two(tbank[h % 2]), ACT.Copy).then_inc(copied[h % 4], 1)

            def body(t):
                G, F, X, B, T, U = phases(e, t)
                if T:
                    kind = e.value_load(ids_ok[0:1, 2, bass.ds(T.i, 1)], min_val=0, max_val=NC2 - 1)
                for s in range(SLOTS):
                    if is_step(t, s, -1, 5):
                        e.wait_ge(ready, 2)
                    if is_step(t, s, 1, 0):
                        e.wait_ge(ready, 4)
                    for x, h in lagging(X, B, s - 1):
                        head(e, biased, x, h)
                        for q in range(TT):
                            i = e.activation(sc[:, h % NS, q, :], sc[:, h % NS, q, :], ACT.Exp,
                                             bias=negmax[:, q, h:h + 1], scale=-1.0)
                        i.then_inc(expd[h % 4], 1)
                    for x, h in lagging(X, B, s - LT):
                        if s in ACT_COPIES:
                            copy_turned(x, h)
                    if s == 2 and B:
                        head(e, mixed, B, H - 1)
                        e.activation(cts[:, 2:4, :], two(cbank), ACT.Copy).then_inc(ev["ct_hi"], 1)
                    if s == 2 and X:
                        head(e, mixed, X, -1)
                        e.wait_ge(ev["v_ready"], X.n)
                        e.activation(vp[:, :, :, 0:DH], vnext[:, :, :].rearrange("p t (h c) -> p t h c", h=H), ACT.Copy).then_inc(ev["vp_ready"], 1)
                    if s == 9 and F:
                        e.wait_ge(ev["v_done"], F.n)
                        wait(e, ev["vp_ready"], F.p)
                        e.activation(vnext[:, :, :], two(fbank), ACT.Copy).then_inc(ev["v_ready"], 1)
                    if s == 2 and T:
                        e.wait_ge(ev["x3_turned"], T.n)
                        wait(e, ev["b_done"], T.p)
                        e.activation(x3T[:, :, :], two(bbank[0]), ACT.Copy).then_inc(ev["x3T_ready"], 1)
                    if s == 3 and T:
                        with e.If(kind == 2):
                            for j in range(2):
                                e.wait_ge(wa_done[j], T.n)
                                for m in range(2):
                                    i = e.activation(gaT[:, 2 * j + m, :], two(bbank[(j + 1) % 2])[:, m, :], ACT.Gelu,
                                                     bias=bac[:, 2 * j + m:2 * j + m + 1])
                                i.then_inc(ga2_ready[j], 1)
                        with e.Else():
                            for j in range(2):
                                e.sem_inc(ga2_ready[j], 1)
                    if s == 4 and T:
                        bring_gelu()
                        e.wait_ge(ev["b_done"], T.n)
                        wait(e, ev["c_done"], T.p)
                        for m in range(KT):
                            i = e.activation(gbT[:, m, :], two(bbank[1])[:, m, :], ACT.Gelu, bias=bsel[:, bass.ds(T.i, 1), m])
                        i.then_inc(ev["gb_ready"], 1)
                    if s == 4 and F:
                        e.wait_ge(ev["x1_turned"], F.n)
                        wait(e, ev["v_done"], F.p)
                        e.activation(x1h[:, :, :], two(fbank), ACT.Copy).then_inc(ev["x1T_ready"], 1)
                    if s == 7 and B:
                        e.wait_ge(ev["c2_turned"], B.n)
                        wait(e, ev["wo_done"], B.p)
                        e.activation(ctxT[:, :, :], two(bbank[0]), ACT.Copy).then_inc(ev["ctxT_ready"], 1)
                    if s == 10 and B:
                        e.wait_ge(ev["n3_turned"], B.n)
                        wait(e, ev["w1_done"], B.h[-1])
                        e.activation(n3h[:, :, :], two(bbank[0]), ACT.Copy).then_inc(ev["n3T_ready"], 1)
                    if s in (12, 13, 14, 15) and B:
                        j = s - 12
                        quarter(e, "w1_done", B, j)
                        wait(e, ev["w2_done"], B.p)
                        for m in range(2 * j, 2 * j + 2):
                            i = e.activation(ffT[:, m, :], two(bbank[(j + 1) % 2])[:, m % 2, :], ACT.Identity, bias=b1c[:, m:m + 1])
                        i.then_inc(ev["u1_ready"], 1)
                        quarter(e, "u1_ready", B, j)
                        if j >= 2:
                            quarter(e, "ff_ready", B, j - 2)
                        e.activation(th[:, j % 2, :, :], ffT[:, 2 * j:2 * j + 2, :], ACT.Tanh, scale=0.851).then_inc(ev["th_ready"], 1)
                    if s in (6, 7) and F:
                        done, hi, b, out = ((ev["q_done"], qh, bq, ev["qh_ready"]), (ev["k_done"], kh, bk, ev["kh_ready"]))[s - 6]
                        e.wait_ge(done, F.n)
                        for m in range(KT):
                            wait(e, ld_stack[m], times(F, 128, prev=True))
                        for m in range(KT):
                            i = e.activation(hi[:, m, :], two(fbank)[:, m, :], ACT.Identity, bias=b[:, m:m + 1])
                        i.then_inc(out, 1)
                    if s == 5 and U:
                        e.wait_ge(ev["w2s_ready"], U.n)
                        e.activation(outN[:, :, :], t_e[:, :, :], ACT.Relu).then_inc(ev["out_ready"], 1)
                    if s == 10 and X:
                        head(e, mixed, X, HM - 1)
                        wait(e, ev["c1_hi"], X.p)
                        e.activation(cts[:, 0:2, :], two(cbank), ACT.Copy).then_inc(ev["ct_lo"], 1)
                    if s == 10 and G:
                        e.wait_ge(ev["xT_turned"], G.n)
                        wait(e, ev["down_done"], G.p)
                        e.activation(xT[:, :, :], two(fbank), ACT.Copy).then_inc(ev["xT_ready"], 1)
                    if s == 11 and G:
                        bring_gelu()
                        e.wait_ge(ev["down_done"], G.n)
                        wait(e, ev["expert_done"], G.p)
                        e.activation(g0[:, :], fbank[0:A, 0:S], ACT.Gelu, bias=down_b[:, 0:1]).then_inc(ev["g0_ready"], 1)
                    if s == 12 and G:
                        e.wait_ge(ev["expert_done"], G.n)
                        e.wait_ge(ev["wexp_ready"], G.n)
                        wait(e, ev["up_done"], G.p)
                        e.activation(g1[0:A, :], fbank[0:A, 0:S], ACT.Identity, bias=wexp[:, A:A + 1]).then_inc(ev["g1_ready"], 1)
                    if s == 9 and X:
                        if B:
                            e.wait_ge(ev["x2_ready"], B.n)
                        e.wait_ge(ev["x1res_ready"], X.n)
                        e.activation(x1late[:, :, :], x1res[:, :, :], ACT.Copy).then_inc(ev["res_moved"], 1)

            turns(e, body)

        @block.vector
        def _(e):
            chain = [0]
            own = sem_dve

            def link(i):
                chain[0] += 1
                i.then_inc(own, 1)
                e.wait_ge(own, chain[0])

            e.wait_ge(ld_ids, 64)
            link(e.tensor_copy(idf[:, :, :], ids[:, :, :]))
            e.tensor_scalar(flags[:, 4, :], idf[:, 0, :], 0.0, None, ALU.is_ge)
            e.tensor_scalar(flags[:, 5, :], idf[:, 0, :], float(NE), None, ALU.is_lt)
            e.tensor_scalar(flags[:, 6, :], idf[:, 2, :], 0.0, None, ALU.is_ge)
            link(e.tensor_scalar(flags[:, 7, :], idf[:, 2, :], float(NC2), None, ALU.is_lt))
            e.tensor_tensor(dom_ok, flags[:, 4, :], flags[:, 5, :], ALU.mult)
            link(e.tensor_tensor(kind_ok, flags[:, 6, :], flags[:, 7, :], ALU.mult))
            e.tensor_scalar(dom_no, dom_ok, -1.0, 1.0, ALU.mult, ALU.add)
            e.tensor_scalar(ids_ok[:, 0, :], idf[:, 0, :], 0.0, float(NE - 1), ALU.max, ALU.min)
            e.tensor_copy(ids_ok[:, 1, :], idf[:, 1, :])
            link(e.tensor_scalar(ids_ok[:, 2, :], idf[:, 2, :], 0.0, float(NC2 - 1), ALU.max, ALU.min))
            e.sem_inc(dve_set, 1)
            e.wait_ge(ld_first, 16 * LOADS_FIRST)
            ang, turn, red = x1late[:, 0, 32:48], x1late[:, 0, 48:64], x1late[:, 0, 64:80]
            link(e.tensor_scalar(turn, idf[:, 1, :], 40.0, None, ALU.mult))
            link(e.tensor_scalar(ang, turn, freq, None, ALU.mult))
            for k in range(2):
                link(e.tensor_scalar(turn, ang, 1.0 / (2 * np.pi), 0.25 * k, ALU.mult, ALU.add))
                link(e.tensor_scalar(turn, turn, ROUND, None, ALU.add))
                link(e.tensor_scalar(turn, turn, -ROUND, None, ALU.add))
                link(e.scalar_tensor_tensor(out=red, in0=turn, scalar=-TWO_PI[0], in1=ang, op0=ALU.mult, op1=ALU.add))
                link(e.scalar_tensor_tensor(out=red, in0=turn, scalar=-TWO_PI[1], in1=red, op0=ALU.mult, op1=ALU.add))
                link(e.scalar_tensor_tensor(out=red, in0=turn, scalar=-TWO_PI[2], in1=red, op0=ALU.mult, op1=ALU.add))
                link(e.tensor_scalar(red, red, float(np.pi / 2) * k, None, ALU.add))
                i = e.tensor_scalar(x1late[:, k, 0:NB], red, -3.1415925, 3.1415925, ALU.max, ALU.min)
                link(i)
            e.sem_inc(dve_set, 1)
            e.wait_ge(pe_set, 1)
            i = e.tensor_scalar(x3T[0:NB, 0, :], sbank[0][0:NB, 0:D], 1.0, None, ALU.add)
            link(i)
            link(e.tensor_copy(x3T[0:NB, 1, :], sbank[0][0:NB, D:2 * D]))
            e.sem_inc(dve_set, 1)
            e.wait_ge(pool_set, 3)
            A0, A1, B0, B1, B2 = x2, x3, t_a, t_b, t_c

            def set_projections():
                e.wait_ge(ld_second, 16 * LOADS_SECOND)
                raws = ((pt[:, 0, :, :], wq, wql, DH ** -0.5), (pt[:, 1, :, :], wk, wkl, 1.0), (th[:, 0, :, :], wv, wvl, 1.0))
                for raw, high, low, scale in raws:
                    i = e.tensor_scalar(high[:, :, :], raw, scale, None, ALU.mult)
                link(i)
                for raw, high, low, scale in raws:
                    i = e.scalar_tensor_tensor(out=low[:, :, :], in0=raw, scalar=scale, in1=high[:, :, :].bitcast(F32),
                                               op0=ALU.mult, op1=ALU.subtract)
                link(i)
                link(e.tensor_scalar(bq, bq, DH ** -0.5, None, ALU.mult))
                ones = cts[:, 0, 0:P]
                link(e.memset(ones, 1.0))
                for k in range(KT):
                    i = e.tensor_scalar(gbT[:, k, 0:P], ones, bv[:, k:k + 1], None, ALU.mult)
                link(i)
                e.sem_inc(dve_set, 1)
                e.sem_inc(ready, 1)

            def set_feed_forward():
                e.wait_ge(ld_set, 16 * LOADS)
                e.wait_ge(pe_set, 2)
                link(e.tensor_tensor(bo[:, :], bbank[0][:, 0:D], bo[:, :], ALU.add))
                e.sem_inc(ready, 1)
                link(e.tensor_tensor(b1c, bbank[1][:, 0:FM], b1c, ALU.add))
                for k in range(KT):
                    i = e.tensor_scalar(w1[:, k, :], w1_raw[:, k, :], g2c[:, k:k + 1], None, ALU.mult)
                link(i)
                for k in range(KT):
                    i = e.scalar_tensor_tensor(out=w1l[:, k, :], in0=w1_raw[:, k, :], scalar=g2c[:, k:k + 1],
                                               in1=w1[:, k, :].bitcast(F32), op0=ALU.mult, op1=ALU.subtract)
                link(i)

            def set_conditional():
                link(e.tensor_scalar(w2[:, :, :], w2[:, :, :], 0.5, None, ALU.mult))
                link(e.memset(bsel[:, :, :], 0.0))
                for c in range(NC2):
                    link(e.tensor_scalar(flags[:, 4, :], idf[:, 2, :], float(c), None, ALU.is_equal))
                    for m in range(KT):
                        link(e.scalar_tensor_tensor(out=bsel[:, :, m], in0=flags[:, 4, :], scalar=bbc[:, c, m:m + 1],
                                                    in1=bsel[:, :, m], op0=ALU.mult, op1=ALU.add))

            def set_grids():
                e.tensor_scalar(grid_r1[:, :, :], A0[:, :, :], -1.0, None, ALU.mult)
                e.tensor_scalar(grid_r2[:, :, :], B0[:, :, :], 0.5, None, ALU.mult)
                e.tensor_scalar(grid_p[:, :, :], B2[:, :, :], 0.5, None, ALU.mult)
                link(e.tensor_scalar(grid_c[:, :, :], B1[:, :, :], -1.0, None, ALU.mult))
                e.tensor_tensor(grid_a[:, :, :], B1[:, :, :], A1[:, :, :], ALU.subtract)
                link(e.tensor_tensor(grid_b[:, :, :], B1[:, :, :], A1[:, :, :], ALU.add))
                e.tensor_scalar(grid_a[:, :, :], grid_a[:, :, :], 0.5, None, ALU.mult)
                link(e.tensor_scalar(grid_b[:, :, :], grid_b[:, :, :], -0.5, None, ALU.mult))

            def set_edges():
                link(e.memset(edge_u[:, :, :, :], 0.0))
                for side_, cs in ((0, (0, 1, 2, 3)), (1, (3, 2, 1, 0))):
                    sign = 1.0 if side_ == 0 else -1.0
                    for k, (ca, cb, cu) in enumerate(((1.5, 1.0, -1.5), (-2.0, -2.5, 2.0), (0.5, 2.0, -0.5), (0.0, -0.5, 0.0))):
                        j = cs[k] if side_ == 0 else D - 4 + cs[k]
                        e.tensor_scalar(edge_u[:, :, side_, cs[k]], B2[:, :, j], sign * cu, None, ALU.mult)
                        link(e.tensor_scalar(edge_e[:, :, side_, cs[k]], B1[:, :, j], cb, None, ALU.mult))
                        link(e.scalar_tensor_tensor(out=edge_e[:, :, side_, cs[k]], in0=A1[:, :, j], scalar=sign * ca,
                                                    in1=edge_e[:, :, side_, cs[k]], op0=ALU.mult, op1=ALU.add))
                e.sem_inc(ready, 1)


            def norm_stats(x, k, src, s_ev, a_ev, v_ev):
                for q in range(TT):
                    i = e.bn_stats(stats[:, k, q, :], src[:, q, :])
                i.then_inc(s_ev, 1)
                e.wait_ge(s_ev, x.n)
                hold(e)
                for q in range(TT):
                    i = e.bn_aggr(mv[:, k, q, :], stats[:, k, q, :])
                i.then_inc(a_ev, 1)
                e.wait_ge(a_ev, x.n)
                e.tensor_scalar(var[:, k, :], mv[:, k, :, 1], EPS, None, ALU.add).then_inc(v_ev, 1)

            def norm_apply(x, k, dst, src, r_ev, o_ev):
                e.wait_ge(r_ev, x.n)
                for q in range(TT):
                    i = e.tensor_scalar(dst[:, q, :], src[:, q, :], mv[:, k, q, 0:1], rstd[:, k, q:q + 1], ALU.subtract, ALU.mult)
                i.then_inc(o_ev, 1)

            def norm_affine(x, k, dst, src, gain, offset, r_ev, s_ev, o_ev):
                e.wait_ge(r_ev, x.n)
                for q in range(TT):
                    i = e.scalar_tensor_tensor(out=src[:, q, :], in0=src[:, q, :], scalar=mv[:, k, q, 0:1], in1=gain,
                                               op0=ALU.subtract, op1=ALU.mult)
                i.then_inc(s_ev, 1)
                e.wait_ge(s_ev, x.n)
                for q in range(TT):
                    i = e.scalar_tensor_tensor(out=dst[:, q, :], in0=src[:, q, :], scalar=rstd[:, k, q:q + 1], in1=offset,
                                               op0=ALU.mult, op1=ALU.add)
                i.then_inc(o_ev, 1)

            def context(x, u, c1, s_ev, i_ev, o_ev):
                e.wait_ge(c1, x.n)
                v = bbank[1 - u][:, :].rearrange("p (q h c) -> p q h c", q=TT, h=HM)
                hs = slice(HM * u, HM * u + HM)
                if u == 0:
                    e.wait_ge(ev["nan_ready"], x.n)
                e.tensor_tensor(rsum[:, :, hs], v[:, :, :, DH], nanz[:, :, hs], ALU.add).then_inc(s_ev, 1)
                e.wait_ge(s_ev, x.n)
                e.reciprocal(rinv[:, :, hs], rsum[:, :, hs]).then_inc(i_ev, 1)
                e.wait_ge(i_ev, x.n)
                for q in range(TT):
                    i = e.tensor_tensor(ctxN[:, q, u * P:u * P + P].rearrange("p (h c) -> p h c", h=HM), v[:, q, :, 0:DH],
                                        rinv[:, q, hs].unsqueeze(2).broadcast_to([P, HM, DH]), ALU.mult)
                i.then_inc(o_ev, 1)

            def edges(x, grid, k, dst, t_ev, c_ev):
                near = bass.AP(fN, 0, [[TT * D, P], [D, TT], [D - 4, 2], [1, 4]])
                e.tensor_tensor(edge_t[:, k, :, :, :], near, grid[:, :, :, :], ALU.mult).then_inc(t_ev, 1)
                e.wait_ge(t_ev, x.n)
                e.tensor_reduce(bass.AP(dst, 0, [[TT * D, P], [D, TT], [D - 1, 2]]), edge_t[:, k, :, :, :], AX_X, ALU.add).then_inc(c_ev, 1)

            def body(t):
                G, F, X, B, T, U = phases(e, t)
                for s in range(SLOTS):
                    for t0, s0, setup in ((-2, 5, set_projections), (-1, 9, set_feed_forward), (0, 3, set_conditional),
                                          (0, 5, set_grids), (0, 8, set_edges)):
                        if is_step(t, s, t0, s0):
                            setup()
                    if X:
                        head(e, scored, X, s)
                        e.wait_ge(ld_side[s // 4], times(X, 16))
                        head(e, masked, X, s)
                        head(e, turned, X, s - NS)
                        if s == 0:
                            wait(e, ev["nan_ready"], X.p)
                        hold(e)
                        for q in range(TT):
                            i = e.tensor_tensor_reduce(sc[:, s % NS, q, :], two(sbank[s % 2])[:, q, :], side[:, s % NSIDE, q, :],
                                                       -1.0, 3.4e38, ALU.add, ALU.min, negmax[:, q, s:s + 1])
                        i.then_inc(biased[s % 4], 1)
                    for x, h in lagging(X, B, s - LT):
                        if s not in ACT_COPIES:
                            head(e, turned, x, h)
                            head(e, mixed, x, h - NP2)
                            e.tensor_copy(pt[:, h % NP2, :, :], two(tbank[h % 2])).then_inc(copied[h % 4], 1)
                    x, j = {13: (B, 0), 14: (B, 1), 15: (B, 2), 0: (T, 3)}.get(s, (None, 0))
                    if x:
                        quarter(e, "th_ready", x, j)
                        f = ffT[:, 2 * j:2 * j + 2, :]
                        e.scalar_tensor_tensor(out=f, in0=th[:, j % 2, :, :], scalar=1.0, in1=f,
                                               op0=ALU.add, op1=ALU.mult).then_inc(ev["ff_ready"], 1)
                    if s == 4 and G:
                        e.wait_ge(ld_exp, times(G, 16))
                        wait(e, ev["expert_done"], G.p)
                        wait(e, ev["g1_ready"], G.p)
                        e.tensor_scalar(wexp[:, 0:A], ident[0:A, 0:A], dom_no[0:A, bass.ds(G.i, 1)], None, ALU.mult)
                        e.tensor_scalar(wexp[:, A:A + 1], wexp_raw[:, A + 1:A + 2], 1.0, None, ALU.mult).then_inc(wexp_half, 1)
                        e.wait_ge(wexp_half, G.n)
                        e.scalar_tensor_tensor(out=wexp[:, 0:A + 1], in0=wexp_raw[:, 0:A + 1], scalar=dom_ok[0:A, bass.ds(G.i, 1)],
                                               in1=wexp[:, 0:A + 1], op0=ALU.mult, op1=ALU.add).then_inc(ev["wexp_ready"], 1)
                    if s == 1 and T:
                        e.wait_ge(ev["w2_done"], T.n)
                        e.wait_ge(ev["x2b_ready"], T.n)
                        wait(e, ev["x4_ready"], T.p)
                        e.tensor_tensor(x3[:, :, :], two(bbank[1]), x2b[:, :, :], ALU.add).then_inc(ev["x3_ready"], 1)
                    if s == 13 and G:
                        e.wait_ge(ev["up_done"], G.n)
                        wait(e, ev["x1_scaled"], G.p)
                        e.tensor_tensor(xa[:, :, :], two(fbank), xN[:, :, :], ALU.add).then_inc(ev["xa_ready"], 1)
                        e.wait_ge(ev["xa_ready"], G.n)
                        norm_stats(G, 0, xa, ev["xa_stats"], ev["xa_aggr"], ev["xa_var"])
                    if s == 5 and T:
                        e.wait_ge(ev["c_done"], T.n)
                        e.wait_ge(ev["x3c_ready"], T.n)
                        wait(e, ev["f_scaled"], T.p)
                        e.scalar_tensor_tensor(out=x4[:, :, :], in0=two(bbank[0]), scalar=kind_ok[:, bass.ds(T.i, 1)], in1=x3c[:, :, :],
                                               op0=ALU.mult, op1=ALU.add).then_inc(ev["x4_ready"], 1)
                    if s == 5 and T:
                        e.wait_ge(ev["x4_ready"], T.n)
                        norm_stats(T, 3, x4, ev["x4_stats"], ev["x4_aggr"], ev["x4_var"])
                    if s == 0 and F:
                        norm_affine(F, 0, yN, xa, gamma0[:, :], beta0[:, :], ev["xa_rstd"], ev["y_scaled"], ev["y_ready"])
                    if s == 1 and F:
                        e.wait_ge(ev["y_ready"], F.n)
                        norm_stats(F, 1, yN, ev["y_stats"], ev["y_aggr"], ev["y_var"])
                    if s == 6 and B:
                        context(B, 0, ev["c1_lo"], ev["sum_lo"], ev["inv_lo"], ev["ctxn_lo"])
                    if s == 6 and B:
                        context(B, 1, ev["c1_hi"], ev["sum_hi"], ev["inv_hi"], ev["ctxn_hi"])
                    if s in (6, 7) and F:
                        ready_, hi, lo, b, out = ((ev["qh_ready"], qh, ql, bq, ev["ql_ready"]), (ev["kh_ready"], kh, kl, bk, ev["kl_ready"]))[s - 6]
                        e.wait_ge(ready_, F.n)
                        for m in range(KT):
                            i = e.scalar_tensor_tensor(out=lo[:, m, :], in0=two(fbank)[:, m, :], scalar=b[:, m:m + 1],
                                                       in1=hi[:, m, :].bitcast(F32), op0=ALU.add, op1=ALU.subtract)
                        i.then_inc(out, 1)
                    if s == 6 and T:
                        norm_affine(T, 3, fN, x4, gamma3[:, :], beta3[:, :], ev["x4_rstd"], ev["f_scaled"], ev["f_ready"])
                    if s == 8 and B:
                        e.wait_ge(ev["wo_done"], B.n)
                        e.wait_ge(ev["res_moved"], B.n)
                        e.tensor_tensor(x2[:, :, :], two(bbank[1]), x1late[:, :, :], ALU.add).then_inc(ev["x2_ready"], 1)
                        e.wait_ge(ev["x2_ready"], B.n)
                        norm_stats(B, 2, x2, ev["x2_stats"], ev["x2_aggr"], ev["x2_var"])
                    if s == 10 and T:
                        e.wait_ge(ev["f_ready"], T.n)
                        wait(e, ev["out_ready"], T.p)
                        e.tensor_tensor(t_p[:, :, :], fN[:, :, :], grid_p[:, :, :], ALU.mult).then_inc(ev["p_ready"], 1)
                        edges(T, edge_u, 0, t_u, ev["u_edge"], ev["u_cols"])
                        e.wait_ge(ev["p_ready"], T.n)
                        e.tensor_tensor(t_u[:, :, 1:D - 1], t_p[:, :, 2:D], t_p[:, :, 0:D - 2], ALU.subtract).then_inc(ev["u_inner"], 1)
                    if s == 9 and B:
                        norm_apply(B, 2, n3, x2, ev["x2_rstd"], ev["n3_ready"])
                    if s == 2 and F:
                        e.wait_ge(ld_ada, times(F, 16))
                        wait(e, ev["x1_turned"], F.p)
                        wait(e, ev["x1res_ready"], F.p)
                        norm_affine(F, 1, x1, yN, ada[:, 0, :], ada[:, 1, :], ev["y_rstd"], ev["x1_scaled"], ev["x1_ready"])
                    if s == 11 and T:
                        e.wait_ge(ev["u_inner"], T.n)
                        e.wait_ge(ev["u_cols"], T.n)
                        e.wait_ge(ev["r1_ready"], T.n)
                        e.tensor_tensor(t_u[:, :, :], t_u[:, :, :], t_r1[:, :, :], ALU.add).then_inc(ev["u_ready"], 1)
                    if s == 10 and B:
                        e.wait_ge(ld_row, times(B, 16))
                        wait(e, ev["x3c_ready"], B.p)
                        e.tensor_scalar(bcf[:, :], bcr[:, :], kind_ok[:, bass.ds(B.i, 1)], None, ALU.mult).then_inc(ev["bcf_ready"], 1)
                    if s == 10 and B:
                        e.wait_ge(ev["n3T_ready"], B.n)
                        e.tensor_tensor(n3l[:, :, :], two(bbank[0]), n3h[:, :, :].bitcast(F32), ALU.subtract).then_inc(ev["n3l_ready"], 1)
                    if s == 12 and T:
                        e.wait_ge(ev["ga_ready"], T.n)
                        e.wait_ge(ev["gb2_ready"], T.n)
                        wait(e, ev["out_ready"], T.p)
                        edges(T, edge_e, 1, t_e, ev["e_edge"], ev["e_cols"])
                        e.tensor_tensor(t_e[:, :, 1:D - 1], t_a[:, :, 2:D], t_b[:, :, 0:D - 2], ALU.subtract).then_inc(ev["e_inner"], 1)
                        e.wait_ge(ev["gc_ready"], T.n)
                        e.wait_ge(ev["e_inner"], T.n)
                        e.tensor_tensor(t_e[:, :, 1:D - 1], t_e[:, :, 1:D - 1], t_c[:, :, 1:D - 1], ALU.add).then_inc(ev["e_ready"], 1)
                    if s == H - 1 and X:
                        head(e, biased, X, H - 1)
                        e.tensor_scalar(nanz[:, :, :], negmax[:, :, :], 2.0, 0.0, ALU.mult, ALU.mult).then_inc(ev["nan_ready"], 1)
                    if s == 3 and U:
                        e.wait_ge(ev["d_done"], U.n)
                        e.wait_ge(ev["e_ready"], U.n)
                        e.wait_ge(ev["e_cols"], U.n)
                        e.tensor_tensor(t_e[:, :, :], two(fbank), t_e[:, :, :], ALU.add).then_inc(ev["w_ready"], 1)
                        e.wait_ge(ev["w_ready"], U.n)
                        e.scalar_tensor_tensor(out=t_e[:, :, :], in0=t_e[:, :, :], scalar=dt[:, bass.ds(U.i, 1)], in1=fN[:, :, :],
                                               op0=ALU.mult, op1=ALU.add).then_inc(ev["w2s_ready"], 1)
                    if s == 4 and F:
                        e.wait_ge(ev["x1T_ready"], F.keep((F.t + F.off) * 2 + 1))
                        e.tensor_tensor(x1l[:, :, :], two(fbank), x1h[:, :, :].bitcast(F32), ALU.subtract).then_inc(ev["x1T_ready"], 1)

            turns(e, body)

        @block.tensor
        def _(e):
            e.wait_ge(act_set, 2)
            e.wait_ge(ld_second, 16 * LOADS_SECOND)
            e.wait_ge(pool_set, 3)
            for k in range(KT):
                e.matmul(sbank[0][0:NB, :], x1late[:, k, 0:NB], ffT[:, 2 * k:2 * k + 2, :], start=(k == 0), stop=False)
            e.matmul(sbank[0][0:NB, :], ones_row[0:1, 0:NB], x1[0:1, :, :], start=False, stop=True).then_inc(pe_set, 1)
            e.wait_ge(ld_first, 16 * LOADS_FIRST)

            def turn(dst, src, done):
                for k in range(KT):
                    for q in range(TT):
                        i = e.transpose(dst[:, k * S + q * P:k * S + q * P + P], src[:, q, k * P:k * P + P], ident[:, :])
                i.then_inc(done, 1)

            def project_T(dst, w, c0, xt, n_m, n_k, done):
                for m in range(n_m):
                    for k in range(n_k):
                        i = e.matmul(two(dst)[:, m, :], w[:, k, c0 + m * P:c0 + m * P + P], xt[:, k, :], start=(k == 0), stop=(k == n_k - 1))
                if done is not None:
                    i.then_inc(done, 1)

            def project(dst, xt, w, n_k, done, q0=0, q1=TT):
                for q in range(q0, q1):
                    for k in range(n_k):
                        i = e.matmul(two(dst)[:, q, :], xt[:, k, q * P:q * P + P], w[:, k, :], start=(k == 0), stop=(k == n_k - 1))
                if done is not None:
                    i.then_inc(done, 1)

            def in_parts(w, wl, x, xl):
                return (w, x), (w, xl), (wl, x)

            def project_T_parts(dst, w, wl, c0, x, xl, n_m, done):
                for m in range(n_m):
                    c = slice(c0 + m * P, c0 + m * P + P)
                    for n, (k, (a, b)) in enumerate((k, ab) for k in range(KT) for ab in in_parts(w, wl, x, xl)):
                        i = e.matmul(two(dst)[:, m, :], a[:, k, c], b[:, k, :], start=(n == 0), stop=(n == 3 * KT - 1))
                i.then_inc(done, 1)

            def body(t):
                G, F, X, B, T, U = phases(e, t)
                if T:
                    kind = e.value_load(ids_ok[0:1, 2, bass.ds(T.i, 1)], min_val=0, max_val=NC2 - 1)
                for s in range(SLOTS):
                    if is_step(t, s, -1, 8):
                        e.wait_ge(ld_set, 16 * LOADS)
                        e.wait_ge(dve_set, 4)
                        for k in range(KT):
                            e.matmul(bbank[0][:, 0:D], gbT[:, k, 0:P], wo[:, k, :], start=(k == 0), stop=(k == KT - 1))
                        for m in range(FM):
                            for k in range(KT):
                                i = e.matmul(bbank[1][:, m:m + 1], w1_raw[:, k, m * P:m * P + P], beta2c[:, k:k + 1], start=(k == 0), stop=(k == KT - 1))
                        i.then_inc(pe_set, 1)
                    if is_step(t, s, -1, 5):
                        e.wait_ge(ready, 2)
                    if is_step(t, s, 1, 0):
                        e.wait_ge(ready, 4)
                    if X:
                        if s % HM == 0:
                            e.wait_ge(ld_stack[s // HM], times(X, 128))
                        head(e, biased, X, s - 2)
                        for q in range(TT):
                            i = e.matmul(two(sbank[s % 2])[:, q, :], qs[:, s, q * P:q * P + P], ks[:, s, :], start=True, stop=True)
                        i.then_inc(scored[s % 4], 1)
                    for x, h in lagging(X, B, s - LT):
                        head(e, expd, x, h)
                        head(e, copied, x, h - 2)
                        for k in range(TT):
                            for q in range(TT):
                                i = e.transpose(tbank[h % 2][:, k * S + q * P:k * S + q * P + P], sc[:, h % NS, q, k * P:k * P + P], ident[:, :])
                        i.then_inc(turned[h % 4], 1)
                    for x, h in lagging(X, B, s - LP):
                        head(e, copied, x, h)
                        if h == 0:
                            e.wait_ge(ev["vp_ready"], x.n)
                            wait(e, ev["ct_hi"], x.p)
                        if h == HM:
                            e.wait_ge(ev["ct_lo"], x.n)
                        o = VW * (h % 4)
                        for k in range(TT):
                            i = e.matmul(two(cbank)[o:o + VW, h // 4 % 2, :], vp[:, k, h, :], pt[:, h % NP2, k, :],
                                         start=(k == 0), stop=(k == TT - 1))
                        i.then_inc(mixed[h % 4], 1)
                    if s == 2 and T:
                        e.wait_ge(ev["x3_ready"], T.n)
                        turn(bbank[0], x3, ev["x3_turned"])
                    if s == 9 and F:
                        e.wait_ge(ev["kl_ready"], F.n)
                        for q in range(TT):
                            for n, (k, (w, x)) in enumerate((k, wx) for k in range(KT) for wx in in_parts(wv, wvl, x1h, x1l)):
                                i = e.matmul(two(fbank)[:, q, :], x[:, k, q * P:q * P + P], w[:, k, :], start=(n == 0), stop=(n == 3 * KT - 1))
                        i.then_inc(ev["v_done"], 1)
                    if s == 3 and T:
                        e.wait_ge(ev["x3T_ready"], T.n)
                        with e.If(kind == 2):
                            for j in range(2):
                                project_T(bbank[(j + 1) % 2], wa, 2 * j * P, x3T, 2, KT, wa_done[j])
                        with e.Else():
                            for j in range(2):
                                e.sem_inc(wa_done[j], 1)
                    if s == 4 and T:
                        e.wait_ge(ld_kind, times(T, 32))
                        for j in range(2):
                            e.wait_ge(ga2_ready[j], T.n)
                        with e.If(kind == 2):
                            project_T(bbank[1], wb, 0, gaT, KT, A2 // P, ev["b_done"])
                        with e.Else():
                            project_T(bbank[1], wb, 0, x3T, KT, KT, ev["b_done"])
                    if s == 4 and F:
                        e.wait_ge(ev["x1_ready"], F.n)
                        if U:
                            e.wait_ge(ev["w_ready"], U.n)
                        turn(fbank, x1, ev["x1_turned"])
                    if s == 5 and T:
                        e.wait_ge(ev["gb_ready"], T.n)
                        project(bbank[0], gbT, wc, KT, ev["c_done"])
                    if s == 6 and B:
                        e.wait_ge(ev["ct_hi"], B.n)
                        for u in range(2):
                            wait(e, (ev["gb_ready"], ev["x4_ready"])[u], B.p)
                            for q in range(TT):
                                for g in range(2):
                                    i = e.transpose(bbank[1 - u][:, q * S + g * P:q * S + g * P + P], cts[:, 2 * u + g, q * P:q * P + P], ident[:, :])
                            i.then_inc((ev["c1_lo"], ev["c1_hi"])[u], 1)
                    if s == 7 and B:
                        e.wait_ge(ev["ctxn_lo"], B.n)
                        e.wait_ge(ev["ctxn_hi"], B.n)
                        turn(bbank[0], ctxN, ev["c2_turned"])
                    if s == 8 and B:
                        e.wait_ge(ev["ctxT_ready"], B.n)
                        project(bbank[1], ctxT, wo, KT, ev["wo_done"])
                    if s == 10 and B:
                        e.wait_ge(ev["n3_ready"], B.n)
                        turn(bbank[0], n3, ev["n3_turned"])
                    if s in (11, 12, 13, 14) and B:
                        j = s - 11
                        if j >= 2:
                            quarter(e, "u1_ready", B, j - 2)
                        else:
                            e.wait_ge(ev[("x2_ready", "n3l_ready")[j]], B.n)
                        if j == 0:
                            e.wait_ge(ev["n3l_ready"], B.n)
                        project_T_parts(bbank[(j + 1) % 2], w1, w1l, 2 * j * P, n3h, n3l, 2, ev["w1_done"])
                    if s == 6 and F:
                        e.wait_ge(ev["x1T_ready"], times(F, 2))
                        project_T_parts(fbank, wq, wql, 0, x1h, x1l, KT, ev["q_done"])
                    if s in (2, 3) and U:
                        q = s - 2
                        if q == 0:
                            e.wait_ge(ev["u_ready"], U.n)
                            e.wait_ge(ev["r2_ready"], U.n)
                            if F:
                                e.wait_ge(ev["xa_ready"], F.n)
                            elif X:
                                e.wait_ge(ev["v_ready"], X.n)
                            wait(e, ev["w_ready"], U.p)
                        for n, (m, u) in enumerate(((d1T, t_u), (d2T, t_r2))):
                            for k in range(KT):
                                i = e.matmul(two(fbank)[:, q, :], m[:, k, q * P:q * P + P], u[:, k, :],
                                             start=(n == 0 and k == 0), stop=(n == 1 and k == KT - 1))
                        if q == TT - 1:
                            i.then_inc(ev["d_done"], 1)
                    if s == 10 and G:
                        e.wait_ge(ld_x, times(G, 16))
                        if F:
                            e.wait_ge(ev["v_ready"], F.n)
                        turn(fbank, xN, ev["xT_turned"])
                    if s == 11 and G:
                        e.wait_ge(ev["xT_ready"], G.n)
                        for k in range(KT):
                            i = e.matmul(fbank[0:A, 0:S], downT[:, k, :], xT[:, k, :], start=(k == 0), stop=(k == KT - 1))
                        i.then_inc(ev["down_done"], 1)
                    if s == 12 and G:
                        e.wait_ge(ev["g0_ready"], G.n)
                        e.wait_ge(ev["wexp_ready"], G.n)
                        hold(e)
                        e.matmul(fbank[0:A, 0:S], wexp[:, 0:A], g0[:, :], start=True, stop=True).then_inc(ev["expert_done"], 1)
                    if s == 13 and G:
                        e.wait_ge(ev["g1_ready"], G.n)
                        for q in range(TT):
                            i = e.matmul(two(fbank)[:, q, :], g1[:, q * P:q * P + P], upT[:, :], start=True, stop=True)
                        i.then_inc(ev["up_done"], 1)
                    if s == 7 and F:
                        e.wait_ge(ev["ql_ready"], F.n)
                        project_T_parts(fbank, wk, wkl, 0, x1h, x1l, KT, ev["k_done"])
                    x, part = {15: (B, 0), 0: (T, 1), 1: (T, 2)}.get(s, (None, 0))
                    if x:
                        if part == 0:
                            quarter(e, "u1_ready", x, 2)
                        for n in range(*((0, 4), (4, 10), (10, TT * FM))[part]):
                            q, k = n // FM, n % FM
                            if q == 0 and k in (0, 4, 6):
                                quarter(e, "ff_ready", x, max(k // 2, 1))
                            i = e.matmul(two(bbank[1])[:, q, :], ffT[:, k, q * P:q * P + P], w2[:, k, :], start=(k == 0), stop=(k == FM - 1))
                        if part == 2:
                            i.then_inc(ev["w2_done"], 1)

            turns(e, body)


def kernel(x, itok_B_0_15, itok_B_34_63, fside_Bx16xSxS_0, itok_B_0_2, condB_dt, mask_Bx1xSxS_bk0, **w):
    import concourse.bacc as bacc
    from concourse.bass_utils import run_bass_kernel_spmd

    def arr(a):
        return np.ascontiguousarray(np.asarray(a))

    c = {k.replace("_cond_", "_"): arr(v) for k, v in w.items()}

    def by_head(a):
        return arr(a.reshape(-1, KT, HM, DH).transpose(0, 1, 3, 2).reshape(a.shape))

    def column(v):
        return v.reshape(-1, P).T

    ins = {
        "x": arr(x), "dom": arr(itok_B_0_15), "step": arr(itok_B_34_63), "kind": arr(itok_B_0_2), "dt": arr(condB_dt),
        "side": arr(fside_Bx16xSxS_0), "mask": arr(mask_Bx1xSxS_bk0).reshape(NB, S, S).view(np.int32),
        "freq": np.exp(np.arange(D // 2, dtype=np.float32) * np.float32(-np.log(10000.0) / (D // 2 - 1))),
        "down_b": c["L0_down_b"], "downT": arr(c["L0_down_W"].T), "upT": arr(c["L0_up_W"].T), "up_b": c["L0_up_b"],
        "expert": np.concatenate([c["L0_expert_W"].transpose(0, 2, 1), c["L0_expert_b"][:, :, None],
                                  c["L0_domain_emb"][:, :, None]], axis=2),
        "gamma0": c["L0_ln_gamma"], "beta0": c["L0_ln_beta"],
        "wq": by_head(c["L1_Wq"]), "wk": by_head(c["L1_Wk"]), "wv": c["L1_Wv"], "wo": c["L1_Wo"],
        "w1": c["L1_W1"], "w2": c["L1_W2"], "w_ada": c["L1_W_ada"], "b_ada": c["L1_b_ada"],
        "b2": c["L1_b2"], "bo": c["L1_bo"],
        "colpack": arr(np.concatenate([column(v) for v in (
            by_head(c["L1_bq"]), by_head(c["L1_bk"]), c["L1_bv"], c["L1_g2"], c["L1_beta2"], c["L1_b1"], c["L2_b1_sr"],
            c["L2_b1_nr"], c["L2_b1_tsr"], c["L2_b2_sr"])], axis=1)),
        "wa": c["L2_w1_sr"],
        "wb": np.concatenate([c["L2_w1_nr"], c["L2_w1_tsr"], c["L2_w2_sr"]]).reshape(4, D, D),
        "wc": np.stack([c["L2_w2_nr"], c["L2_w2_tsr"], c["L2_w3_sr"]]),
        "bc": np.stack([c["L2_b2_nr"], c["L2_b2_tsr"], c["L2_b3_sr"]]),
        "gamma3": c["L2_gamma"], "beta3": c["L2_beta"],
        "d1T": arr(rest_grad(S).T), "d2T": arr(rest_grad2(S).T),
        "grid_A": c["L3_A_grid"], "grid_B": c["L3_B_grid"],
    }
    nc = bacc.Bacc("TRN2", target_bir_lowering=False, num_devices=1)
    d = {n: nc.dram_tensor("in_" + n, a.shape, mybir.dt.from_np(a.dtype), kind="ExternalInput").ap() for n, a in ins.items()}
    d["ada_rows"] = nc.dram_tensor("ada_rows", (NB, 2 * D), F32, kind="Internal").ap()
    d["out"] = nc.dram_tensor("out", (NB, S, D), F32, kind="ExternalOutput").ap()
    build(nc, d)
    return run_bass_kernel_spmd(nc, [{"in_" + n: a for n, a in ins.items()}], core_ids=[0]).results[0]["out"]
```
